# Optimizing a Trainium2 kernel written in Bass

```python
import numpy as np
import jax
import jax.numpy as jnp

def _softmax(x, axis=-1):
    return jax.nn.softmax(x, axis=axis)

def _gelu(x):
    return jax.nn.gelu(x, approximate=True)

def _silu(x):
    return jax.nn.silu(x)

def _sigmoid(x):
    return jax.nn.sigmoid(x)

def _layernorm(x, axis=-1, eps=1e-05):
    m = jnp.mean(x, axis=axis, keepdims=True)
    v = jnp.var(x, axis=axis, keepdims=True)
    return (x - m) / jnp.sqrt(v + eps)

def _scatter_add(tgt, idx, src, axis=0):
    return tgt.at[idx].add(src)

def _segment_sum(src, seg, n):
    return jax.ops.segment_sum(src, seg, n)
kernel_name = 'mk_macaron_d2_jaxref_r8_062689'

def setup_inputs(seed: int=0):
    np.random.seed(seed)
    _w = jnp.asarray

    def _L0_attn_setup():
        import jax, jax.numpy as jnp
        import numpy as np
        B, S, D, H = (2, 256, 256, 16)
        HD = D // H

        def _alibi_slopes(num_heads):
            ratio = 2.0 ** (-8.0 / num_heads)
            return ratio ** jnp.arange(1, num_heads + 1, dtype=jnp.float32)
        key = jax.random.key(seed)
        ks = jax.random.split(key, 9)
        sd = 1.0 / np.sqrt(D)
        inp = {'x': jax.random.normal(ks[0], (B, S, D), dtype=jnp.float32)}
        for i, name in enumerate(['Wq', 'Wk', 'Wv', 'Wo']):
            inp[name] = jax.random.normal(ks[1 + i], (D, D), dtype=jnp.float32) * sd
        for i, name in enumerate(['bq', 'bk', 'bv', 'bo']):
            inp[name] = jax.random.normal(ks[5 + i], (D,), dtype=jnp.float32) * 0.02
        return inp
    _L0_attn_in = _L0_attn_setup()

    def _L0_ffn_setup():
        import jax, jax.numpy as jnp
        import numpy as np
        HIDDEN = 256
        N_EXPERTS = 8
        N_SHARED = 2
        TOP_K = 2
        MOE_FF = 176
        SHARED_FF = N_SHARED * MOE_FF
        SCALE = 2.5
        BATCH, SEQ = (2, 128)
        key = jax.random.key(seed)
        ks = jax.random.split(key, 8)
        s = 0.02
        return {'hidden_states': jax.random.normal(ks[0], (BATCH, SEQ, HIDDEN), jnp.float32), 'gate_w': jax.random.normal(ks[1], (N_EXPERTS, HIDDEN), jnp.float32) * s, 'shared_wg': jax.random.normal(ks[2], (SHARED_FF, HIDDEN), jnp.float32) * s, 'shared_wu': jax.random.normal(ks[3], (SHARED_FF, HIDDEN), jnp.float32) * s, 'shared_wd': jax.random.normal(ks[4], (HIDDEN, SHARED_FF), jnp.float32) * s, 'exp_wg': jax.random.normal(ks[5], (N_EXPERTS, MOE_FF, HIDDEN), jnp.float32) * s, 'exp_wu': jax.random.normal(ks[6], (N_EXPERTS, MOE_FF, HIDDEN), jnp.float32) * s, 'exp_wd': jax.random.normal(ks[7], (N_EXPERTS, HIDDEN, MOE_FF), jnp.float32) * s}
    _L0_ffn_in = _L0_ffn_setup()

    def _L1_attn_setup():
        import jax, jax.numpy as jnp
        import numpy as np
        DIM = 256
        HEADS = 16
        HEAD_DIM = DIM // HEADS
        RANK = 16
        ALPHA = 8.0
        SCALING = ALPHA / RANK
        SCALE = HEAD_DIM ** (-0.5)

        def lora_linear(x, W, b, Bm, Am):
            out = jnp.einsum('bld,od->blo', x, W) + b
            upd = jnp.einsum('blr,or->blo', jnp.einsum('bld,rd->blr', x, Bm), Am)
            return out + SCALING * upd

        def _split(t):
            B, L, D = t.shape
            return t.reshape(B, L, HEADS, HEAD_DIM).transpose(0, 2, 1, 3)
        key = jax.random.key(seed)
        ks = jax.random.split(key, 20)
        B, L = (4, 256)
        x = jax.random.normal(ks[0], (B, L, DIM), dtype=jnp.float32)
        s = 0.02
        inp = {'x': x}
        for i, name in enumerate(['q', 'k', 'v', 'o']):
            inp[f'W{name}'] = jax.random.normal(ks[1 + 4 * i], (DIM, DIM), jnp.float32) * s
            inp[f'b{name}'] = jax.random.normal(ks[2 + 4 * i], (DIM,), jnp.float32) * s
            inp[f'B{name}'] = jax.random.normal(ks[3 + 4 * i], (RANK, DIM), jnp.float32) * s
            inp[f'A{name}'] = jax.random.uniform(ks[4 + 4 * i], (DIM, RANK), jnp.float32, -0.1, 0.1)
        return inp
    _L1_attn_in = _L1_attn_setup()

    def _L1_ffn_setup():
        import jax, jax.numpy as jnp
        import numpy as np
        E = 8
        TOP_K = 2
        H = 256
        I_MOE = 176
        I_SH = 704
        B, S = (2, 256)

        def _moe_forward(hidden_states, router_weight, gate_up_proj, down_proj, sh_gate_w, sh_up_w, sh_down_w, shared_gate_w):
            b, s, h = hidden_states.shape
            x = hidden_states.reshape(-1, h)
            shared = jnp.einsum('ti,hi->th', jax.nn.silu(x @ sh_gate_w.T) * (x @ sh_up_w.T), sh_down_w)
            logits = x @ router_weight.T
            probs = jax.nn.softmax(logits.astype(jnp.float32), axis=-1)
            top_v, top_i = jax.lax.top_k(probs, TOP_K)
            top_v = top_v / top_v.sum(axis=-1, keepdims=True)
            combine = (jax.nn.one_hot(top_i, E, dtype=top_v.dtype) * top_v[..., None]).sum(axis=1)
            out = jnp.zeros_like(x)
            for e in range(E):
                gu = x @ gate_up_proj[e].T
                gate, up = (gu[:, :I_MOE], gu[:, I_MOE:])
                cur = jax.nn.silu(gate) * up @ down_proj[e].T
                out = out + cur * combine[:, e:e + 1]
            out = out + jax.nn.sigmoid(x @ shared_gate_w.T) * shared
            return out.reshape(b, s, h)
        key = jax.random.key(seed)
        ks = jax.random.split(key, 8)
        scale = 0.02
        return {'hidden_states': jax.random.normal(ks[0], (B, S, H), dtype=jnp.float32), 'router_weight': jax.random.normal(ks[1], (E, H), dtype=jnp.float32) * scale, 'gate_up_proj': jax.random.normal(ks[2], (E, 2 * I_MOE, H), dtype=jnp.float32) * scale, 'down_proj': jax.random.normal(ks[3], (E, H, I_MOE), dtype=jnp.float32) * scale, 'sh_gate_w': jax.random.normal(ks[4], (I_SH, H), dtype=jnp.float32) * scale, 'sh_up_w': jax.random.normal(ks[5], (I_SH, H), dtype=jnp.float32) * scale, 'sh_down_w': jax.random.normal(ks[6], (H, I_SH), dtype=jnp.float32) * scale, 'shared_gate_w': jax.random.normal(ks[7], (1, H), dtype=jnp.float32) * scale}
    _L1_ffn_in = _L1_ffn_setup()
    _d = {'L0_attn_x': _L0_attn_in['x'], 'L0_attn_Wq': _L0_attn_in['Wq'], 'L0_attn_bq': _L0_attn_in['bq'], 'L0_attn_Wk': _L0_attn_in['Wk'], 'L0_attn_bk': _L0_attn_in['bk'], 'L0_attn_Wv': _L0_attn_in['Wv'], 'L0_attn_bv': _L0_attn_in['bv'], 'L0_attn_Wo': _L0_attn_in['Wo'], 'L0_attn_bo': _L0_attn_in['bo'], 'L0_ffn_gate_w': _L0_ffn_in['gate_w'], 'L0_ffn_shared_wg': _L0_ffn_in['shared_wg'], 'L0_ffn_shared_wu': _L0_ffn_in['shared_wu'], 'L0_ffn_shared_wd': _L0_ffn_in['shared_wd'], 'L0_ffn_exp_wg': _L0_ffn_in['exp_wg'], 'L0_ffn_exp_wu': _L0_ffn_in['exp_wu'], 'L0_ffn_exp_wd': _L0_ffn_in['exp_wd'], 'L1_attn_Wq': _L1_attn_in['Wq'], 'L1_attn_bq': _L1_attn_in['bq'], 'L1_attn_Bq': _L1_attn_in['Bq'], 'L1_attn_Aq': _L1_attn_in['Aq'], 'L1_attn_Wk': _L1_attn_in['Wk'], 'L1_attn_bk': _L1_attn_in['bk'], 'L1_attn_Bk': _L1_attn_in['Bk'], 'L1_attn_Ak': _L1_attn_in['Ak'], 'L1_attn_Wv': _L1_attn_in['Wv'], 'L1_attn_bv': _L1_attn_in['bv'], 'L1_attn_Bv': _L1_attn_in['Bv'], 'L1_attn_Av': _L1_attn_in['Av'], 'L1_attn_Wo': _L1_attn_in['Wo'], 'L1_attn_bo': _L1_attn_in['bo'], 'L1_attn_Bo': _L1_attn_in['Bo'], 'L1_attn_Ao': _L1_attn_in['Ao'], 'L1_ffn_router_weight': _L1_ffn_in['router_weight'], 'L1_ffn_gate_up_proj': _L1_ffn_in['gate_up_proj'], 'L1_ffn_down_proj': _L1_ffn_in['down_proj'], 'L1_ffn_sh_gate_w': _L1_ffn_in['sh_gate_w'], 'L1_ffn_sh_up_w': _L1_ffn_in['sh_up_w'], 'L1_ffn_sh_down_w': _L1_ffn_in['sh_down_w'], 'L1_ffn_shared_gate_w': _L1_ffn_in['shared_gate_w']}
    _x0 = _d['L0_attn_x']
    _d['L0_attn_x'] = jax.random.normal(jax.random.fold_in(jax.random.key(seed), 1), (4, 512, 256), dtype=_x0.dtype)
    del _x0
    return _d

def reference(L0_attn_x, L0_attn_Wq, L0_attn_bq, L0_attn_Wk, L0_attn_bk, L0_attn_Wv, L0_attn_bv, L0_attn_Wo, L0_attn_bo, L0_ffn_gate_w, L0_ffn_shared_wg, L0_ffn_shared_wu, L0_ffn_shared_wd, L0_ffn_exp_wg, L0_ffn_exp_wu, L0_ffn_exp_wd, L1_attn_Wq, L1_attn_bq, L1_attn_Bq, L1_attn_Aq, L1_attn_Wk, L1_attn_bk, L1_attn_Bk, L1_attn_Ak, L1_attn_Wv, L1_attn_bv, L1_attn_Bv, L1_attn_Av, L1_attn_Wo, L1_attn_bo, L1_attn_Bo, L1_attn_Ao, L1_ffn_router_weight, L1_ffn_gate_up_proj, L1_ffn_down_proj, L1_ffn_sh_gate_w, L1_ffn_sh_up_w, L1_ffn_sh_down_w, L1_ffn_shared_gate_w):

    def _L0_attn_ref(x, Wq, bq, Wk, bk, Wv, bv, Wo, bo):
        import jax, jax.numpy as jnp
        import numpy as np
        B, S, D, H = (2, 256, 256, 16)
        HD = D // H

        def _alibi_slopes(num_heads):
            ratio = 2.0 ** (-8.0 / num_heads)
            return ratio ** jnp.arange(1, num_heads + 1, dtype=jnp.float32)
        b, s, d = x.shape

        def proj(W, bias):
            return (x @ W + bias).reshape(b, s, H, HD).transpose(0, 2, 1, 3)
        q, k, v = (proj(Wq, bq), proj(Wk, bk), proj(Wv, bv))
        scores = jnp.einsum('bhqd,bhkd->bhqk', q, k) / jnp.sqrt(jnp.float32(HD))
        distances = jnp.arange(1 - s, 1, dtype=jnp.float32)
        bias = _alibi_slopes(H)[None, :, None, None] * distances[None, None, None, :]
        scores = scores + bias
        causal = jnp.tril(jnp.ones((s, s), dtype=bool))[None, None]
        scores = jnp.where(causal, scores, jnp.finfo(scores.dtype).min)
        attn = jax.nn.softmax(scores, axis=-1)
        ctx = jnp.einsum('bhqk,bhkd->bhqd', attn, v)
        ctx = ctx.transpose(0, 2, 1, 3).reshape(b, s, d)
        return ctx @ Wo + bo

    def _L0_ffn_ref(hidden_states, gate_w, shared_wg, shared_wu, shared_wd, exp_wg, exp_wu, exp_wd):
        import jax, jax.numpy as jnp
        import numpy as np
        HIDDEN = 256
        N_EXPERTS = 8
        N_SHARED = 2
        TOP_K = 2
        MOE_FF = 176
        SHARED_FF = N_SHARED * MOE_FF
        SCALE = 2.5
        BATCH, SEQ = (2, 128)
        B, S, D = hidden_states.shape
        T = B * S
        xf = hidden_states.reshape(T, D)
        scores = jax.nn.sigmoid(xf @ gate_w.T)
        topk_w, topk_idx = jax.lax.top_k(scores, TOP_K)
        topk_w = topk_w / (topk_w.sum(axis=-1, keepdims=True) + 1e-20)
        topk_w = topk_w * SCALE
        shared_out = jax.nn.silu(xf @ shared_wg.T) * (xf @ shared_wu.T) @ shared_wd.T
        h = jax.nn.silu(jnp.einsum('td,efd->etf', xf, exp_wg)) * jnp.einsum('td,efd->etf', xf, exp_wu)
        all_out = jnp.einsum('etf,edf->etd', h, exp_wd)
        picked = all_out[topk_idx, jnp.arange(T)[:, None]]
        routed_out = (topk_w[..., None] * picked).sum(axis=1)
        return (shared_out + routed_out).reshape(B, S, D)

    def _L1_attn_ref(x, Wq, bq, Bq, Aq, Wk, bk, Bk, Ak, Wv, bv, Bv, Av, Wo, bo, Bo, Ao):
        import jax, jax.numpy as jnp
        import numpy as np
        DIM = 256
        HEADS = 16
        HEAD_DIM = DIM // HEADS
        RANK = 16
        ALPHA = 8.0
        SCALING = ALPHA / RANK
        SCALE = HEAD_DIM ** (-0.5)

        def lora_linear(x, W, b, Bm, Am):
            out = jnp.einsum('bld,od->blo', x, W) + b
            upd = jnp.einsum('blr,or->blo', jnp.einsum('bld,rd->blr', x, Bm), Am)
            return out + SCALING * upd

        def _split(t):
            B, L, D = t.shape
            return t.reshape(B, L, HEADS, HEAD_DIM).transpose(0, 2, 1, 3)
        q = _split(lora_linear(x, Wq, bq, Bq, Aq))
        k = _split(lora_linear(x, Wk, bk, Bk, Ak))
        v = _split(lora_linear(x, Wv, bv, Bv, Av))
        scores = jnp.einsum('bhqd,bhkd->bhqk', q, k) * SCALE
        attn = jax.nn.softmax(scores, axis=-1)
        out = jnp.einsum('bhqk,bhkd->bhqd', attn, v)
        B, H, L, hd = out.shape
        out = out.transpose(0, 2, 1, 3).reshape(B, L, H * hd)
        return lora_linear(out, Wo, bo, Bo, Ao)

    def _L1_ffn_ref(hidden_states, router_weight, gate_up_proj, down_proj, sh_gate_w, sh_up_w, sh_down_w, shared_gate_w):
        import jax, jax.numpy as jnp
        import numpy as np
        E = 8
        TOP_K = 2
        H = 256
        I_MOE = 176
        I_SH = 704
        B, S = (2, 256)

        def _moe_forward(hidden_states, router_weight, gate_up_proj, down_proj, sh_gate_w, sh_up_w, sh_down_w, shared_gate_w):
            b, s, h = hidden_states.shape
            x = hidden_states.reshape(-1, h)
            shared = jnp.einsum('ti,hi->th', jax.nn.silu(x @ sh_gate_w.T) * (x @ sh_up_w.T), sh_down_w)
            logits = x @ router_weight.T
            probs = jax.nn.softmax(logits.astype(jnp.float32), axis=-1)
            top_v, top_i = jax.lax.top_k(probs, TOP_K)
            top_v = top_v / top_v.sum(axis=-1, keepdims=True)
            combine = (jax.nn.one_hot(top_i, E, dtype=top_v.dtype) * top_v[..., None]).sum(axis=1)
            out = jnp.zeros_like(x)
            for e in range(E):
                gu = x @ gate_up_proj[e].T
                gate, up = (gu[:, :I_MOE], gu[:, I_MOE:])
                cur = jax.nn.silu(gate) * up @ down_proj[e].T
                out = out + cur * combine[:, e:e + 1]
            out = out + jax.nn.sigmoid(x @ shared_gate_w.T) * shared
            return out.reshape(b, s, h)
        return _moe_forward(hidden_states, router_weight, gate_up_proj, down_proj, sh_gate_w, sh_up_w, sh_down_w, shared_gate_w)
    x = L0_attn_x
    x = x + 0.5 * _L0_ffn_ref(_layernorm(x, axis=-1), L0_ffn_gate_w, L0_ffn_shared_wg, L0_ffn_shared_wu, L0_ffn_shared_wd, L0_ffn_exp_wg, L0_ffn_exp_wu, L0_ffn_exp_wd)
    x = x + _L0_attn_ref(_layernorm(x, axis=-1), L0_attn_Wq, L0_attn_bq, L0_attn_Wk, L0_attn_bk, L0_attn_Wv, L0_attn_bv, L0_attn_Wo, L0_attn_bo)
    x = x + 0.5 * _L0_ffn_ref(_layernorm(x, axis=-1), L0_ffn_gate_w, L0_ffn_shared_wg, L0_ffn_shared_wu, L0_ffn_shared_wd, L0_ffn_exp_wg, L0_ffn_exp_wu, L0_ffn_exp_wd)
    x = x + 0.5 * _L1_ffn_ref(_layernorm(x, axis=-1), L1_ffn_router_weight, L1_ffn_gate_up_proj, L1_ffn_down_proj, L1_ffn_sh_gate_w, L1_ffn_sh_up_w, L1_ffn_sh_down_w, L1_ffn_shared_gate_w)
    x = x + _L1_attn_ref(_layernorm(x, axis=-1), L1_attn_Wq, L1_attn_bq, L1_attn_Bq, L1_attn_Aq, L1_attn_Wk, L1_attn_bk, L1_attn_Bk, L1_attn_Ak, L1_attn_Wv, L1_attn_bv, L1_attn_Bv, L1_attn_Av, L1_attn_Wo, L1_attn_bo, L1_attn_Bo, L1_attn_Ao)
    x = x + 0.5 * _L1_ffn_ref(_layernorm(x, axis=-1), L1_ffn_router_weight, L1_ffn_gate_up_proj, L1_ffn_down_proj, L1_ffn_sh_gate_w, L1_ffn_sh_up_w, L1_ffn_sh_down_w, L1_ffn_shared_gate_w)
    return x

_drawn_inputs = setup_inputs


def setup_inputs(seed=0):
    import zlib

    import numpy as np

    out = dict(_drawn_inputs(seed))
    spreads = {}
    factors = {'L0_attn_bq': 8.0,
     'L0_attn_bk': 64.0,
     'L0_attn_bv': 2.762,
     'L0_attn_bo': 3.109,
     'L0_ffn_gate_w': 2.939,
     'L0_ffn_shared_wg': 3.024,
     'L0_ffn_shared_wu': 2.983,
     'L0_ffn_shared_wd': 2.982,
     'L1_attn_Wq': 8.0,
     'L1_attn_bq': 8.0,
     'L1_attn_Bq': 8.0,
     'L1_attn_Aq': 8.0,
     'L1_attn_Wk': 8.0,
     'L1_attn_bk': 64.0,
     'L1_attn_Bk': 8.0,
     'L1_attn_Ak': 8.0,
     'L1_attn_Wv': 8.0,
     'L1_attn_bv': 8.0,
     'L1_attn_Bv': 8.0,
     'L1_attn_Av': 8.0,
     'L1_attn_Wo': 6.067,
     'L1_attn_bo': 19.579,
     'L1_attn_Bo': 8.0,
     'L1_attn_Ao': 8.0,
     'L1_ffn_router_weight': 6.997,
     'L1_ffn_gate_up_proj': 6.03,
     'L1_ffn_down_proj': 6.039,
     'L1_ffn_sh_gate_w': 4.204,
     'L1_ffn_sh_up_w': 4.103,
     'L1_ffn_sh_down_w': 4.122,
     'L1_ffn_shared_gate_w': 8.0}
    for name, (base, spread) in spreads.items():
        noise = np.random.default_rng([zlib.crc32(name.encode()), seed]).standard_normal(out[name].shape)
        drawn = base * np.exp(spread * noise) if base else spread * noise
        out[name] = jnp.asarray(drawn.astype(out[name].dtype))
    for name, factor in factors.items():
        out[name] = (out[name] * factor).astype(out[name].dtype)
    return out
```

```python
from contextlib import ExitStack

import numpy as np

import concourse.bass as bass
from concourse import mybir

F32 = mybir.dt.float32
F32R = mybir.dt.float32r
BF16 = mybir.dt.bfloat16
ALU = mybir.AluOpType
ACT = mybir.ActivationFunctionType
AX = mybir.AxisListType

P = 128
D = 256
KT = D // P
B, S = 4, 512
TT = S // P
E = 8
MOE = 176
SHARED = (352, 704)
TILES = tuple(-(-(E * MOE + s) // P) for s in SHARED)
WC = 3 * D
RC = 16
LO_ROW = 32
EPS = 1e-5
RING = 3

H = 16
HD = D // H
G = 4
HG = H // G
ROW_M, ROW_A, ROW_D = 0, 1, 2
ROWS = ROW_D + HD
STACK = 96
RANK = 16
NEG = -1e30
HALF = G // 2
SLOTS, LAG, TURN = 11, 3, 10
PROBS = 4
B_UNITS = 2 * TT
LORA_UNITS = 3 * KT + G
A_PROLOGUE = 2 * G + TT * HG + TT
A_UNITS = 2 * G + G * TT * HG + TT + KT
A_QK = (TT * HG, 2 * HALF + 3 * TT * HG)
STACKED = 16 * 6 * HG
MAX_STACKED = 16 * 3

ROUTER_STEPS = (11, 15)


def split3(pe, out, w_hi, w_lo, x_hi, x_lo, start, stop):
    pe.matmul(out, w_hi, x_hi, start=start, stop=False)
    pe.matmul(out, w_hi, x_lo, start=False, stop=False)
    return pe.matmul(out, w_lo, x_hi, start=False, stop=stop)


class Norm:

    def __init__(self, sh, sem):
        self.sh = sh
        self.done = 0
        self.summed = sem("ln_summed")
        self.mean = sem("ln_mean")
        self.centred = sem("ln_centred")
        self.squared = sem("ln_squared")
        self.sq_summed = sem("ln_sq_summed")
        self.var = sem("ln_var")
        self.log = sem("ln_log")
        self.root = sem("ln_root")
        self.root_squared = sem("ln_root_squared")
        self.refined = sem("ln_refined")
        self.rstd = sem("ln_rstd")
        self.normed = sem("ln_normed")
        self.hi = sem("ln_hi")
        self.lo = sem("ln_lo")

    def sum_tiles(self, dve, x):
        dve.tensor_tensor(self.sh.ln_sum[:], x[:, 0, :], x[:, 1, :], ALU.add).then_inc(self.summed, 1)

    def take_mean(self, pe, n):
        pe.wait_ge(self.summed, self.done + n + 1)
        pe.matmul(self.sh.misc[:], self.sh.mean_w[:], self.sh.ln_sum[:], start=True, stop=True).then_inc(self.mean, 1)

    def centre(self, dve, x, n):
        dve.wait_ge(self.mean, self.done + n + 1)
        dve.tensor_tensor(self.sh.ln_x[:, 0, :], x[:, 0, :], self.sh.misc[:], ALU.subtract)
        dve.tensor_tensor(self.sh.ln_x[:, 1, :], x[:, 1, :], self.sh.misc[:],
                          ALU.subtract).then_inc(self.centred, 1)

    def square(self, act, n):
        act.wait_ge(self.centred, self.done + n + 1)
        act.activation(self.sh.ln_sq[:], self.sh.ln_x[:], ACT.Square).then_inc(self.squared, 1)

    def sum_squares(self, dve, n):
        dve.wait_ge(self.squared, self.done + n + 1)
        dve.tensor_tensor(self.sh.ln_sum[:], self.sh.ln_sq[:, 0, :], self.sh.ln_sq[:, 1, :],
                          ALU.add).then_inc(self.sq_summed, 1)

    def take_var(self, pe, n):
        pe.wait_ge(self.sq_summed, self.done + n + 1)
        pe.matmul(self.sh.misc[:], self.sh.mean_w[:], self.sh.ln_sum[:], start=True, stop=True).then_inc(self.var, 1)

    def take_root(self, act, n):
        act.wait_ge(self.var, self.done + n + 1)
        act.activation(self.sh.ln_r[:], self.sh.misc[:], ACT.Ln, bias=self.sh.eps[:, 0:1]).then_inc(self.log, 1)
        act.wait_ge(self.log, self.done + n + 1)
        act.activation(self.sh.ln_r[:], self.sh.ln_r[:], ACT.Exp, scale=-0.5).then_inc(self.root, 1)
        act.wait_ge(self.root, self.done + n + 1)
        act.activation(self.sh.ln_sq[:, 0], self.sh.ln_r[:], ACT.Square).then_inc(self.root_squared, 1)

    def scale(self, dve, n):
        r, r2 = self.sh.ln_r, self.sh.ln_sq[:, 0]
        dve.wait_ge(self.root_squared, self.done + n + 1)
        dve.scalar_tensor_tensor(out=r2, in0=self.sh.misc[:], scalar=EPS, in1=r2, op0=ALU.add,
                                 op1=ALU.mult).then_inc(self.refined, 1)
        dve.wait_ge(self.refined, self.done + n + 1)
        dve.scalar_tensor_tensor(out=r[:], in0=r2, scalar=-3.0, in1=r[:], op0=ALU.add,
                                 op1=ALU.mult).then_inc(self.rstd, 1)
        dve.wait_ge(self.centred, self.done + n + 1)
        dve.wait_ge(self.rstd, self.done + n + 1)
        for kt in range(KT):
            x = self.sh.ln_x[:, kt, :]
            last = dve.scalar_tensor_tensor(out=x, in0=x, scalar=-0.5, in1=r[:], op0=ALU.mult, op1=ALU.mult)
        last.then_inc(self.normed, 1)

    def split_hi(self, act, hi, n):
        act.wait_ge(self.normed, self.done + n + 1)
        act.activation(hi[:], self.sh.ln_x[:], ACT.Copy).then_inc(self.hi, 1)

    def split_lo(self, pool, hi, lo, n):
        pool.wait_ge(self.hi, self.done + n + 1)
        pool.tensor_tensor(lo[:], self.sh.ln_x[:], hi[:].bitcast(F32), ALU.subtract).then_inc(self.lo, 1)


def load_constants(nc, sh, dram, loaded, made):
    with nc.Block() as block:
        @block.sync
        def _(sp):
            for b in range(B):
                sp.dma_start(sh.x[:, b], dram["x"][:, b]).then_inc(loaded, 16)
            sp.dma_start(sh.mean_w[:], dram["mean_w"]).then_inc(loaded, 16)
            sp.dma_start(sh.ident[:], dram["ident"]).then_inc(loaded, 16)
            sp.wait_ge(loaded, 16 * (B + 2))

        @block.vector
        def _(dve):
            dve.memset(sh.eps[:], EPS).then_inc(made, 1)
            dve.wait_ge(made, 1)


def store_output(nc, sh, out, stored):
    with nc.Block() as block:
        @block.sync
        def _(sp):
            for b in range(B):
                sp.dma_start(out[:, b], sh.x[:, b]).then_inc(stored, 16)
            sp.wait_ge(stored, 16 * B)




def ffn_phase(nc, sh, name, layer, dram):
    T = TILES[layer]
    with ExitStack() as ctx:
        def sb(n, shape, dt):
            return ctx.enter_context(nc.sbuf_tensor(f"{name}_{n}", shape, dt))

        def sem(n):
            handle = nc.alloc_semaphore(name=f"{name}_{n}")
            sh.semaphores.append(handle)
            return handle

        raw = sb("raw", [P, RING, WC], F32)
        w_hi = sb("w_hi", [P, T, WC], F32R)
        w_lo = sb("w_lo", [P, T, WC], F32R)
        rw = sb("rw", [P, KT, RC], F32)
        rw_hi = sb("rw_hi", [P, KT, RC], F32R)
        rw_lo = sb("rw_lo", [P, KT, RC], F32R)
        sel = sb("sel", [LO_ROW + RC, T, P], F32R)
        comb_t = [sb(f"comb_t{p}", [LO_ROW + RC, S], F32R) for p in range(2)]
        act_g = [sb(f"act_g{p}", [P, S], F32) for p in range(2)]
        hid = [sb(f"hid{p}", [P, S], F32) for p in range(2)]
        hid_hi = [sb(f"hid_hi{p}", [P, S], F32R) for p in range(2)]
        hid_lo = [sb(f"hid_lo{p}", [P, S], F32R) for p in range(2)]
        x_hi = [sb(f"x_hi{p}", [P, KT, S], F32R) for p in range(2)]
        x_lo = [sb(f"x_lo{p}", [P, KT, S], F32R) for p in range(2)]
        tri = sb("tri", [P, E * E], F32)
        sig = sb("sig", [P, TT, E + 1], F32)
        score = sb("score", [P, TT, E], F32)
        ahead = sb("ahead", [P, TT, E, E], F32)
        tied = sb("tied", [P, TT, E, E], F32)
        col = sb("col", [P, 4, TT], F32)
        comb = sb("comb", [P, TT, RC], F32)

        psg = [sh.pair_b[0][:, 0], sh.pair_b[0][:, 1]]
        psu = [sh.pair_b[1][:, 0], sh.pair_b[1][:, 1]]
        psc = sh.bank
        psy = sh.pair_a

        const_loaded = sem("const_loaded")
        const_split = sem("const_split")
        const_set = sem("const_set")
        raw_loaded = [sem(f"raw_loaded{r}") for r in range(RING)]
        w_hi_made = sem("w_hi_made")
        w_split = sem("w_split")
        ln = sh.norm
        logits_made = sem("logits_made")
        neg_exp_made = sem("neg_exp_made")
        shifted = sem("shifted")
        soft_exp_made = sem("soft_exp_made")
        comb_made = sem("comb_made")
        comb_turned = sem("comb_turned")
        comb_hi_made = sem("comb_hi_made")
        comb_split = sem("comb_split")
        router_step = sem("router_step")
        gate_made = sem("gate_made")
        up_made = sem("up_made")
        scale_made = sem("scale_made")
        act_made = sem("act_made")
        up_used = sem("up_used")
        hid_made = sem("hid_made")
        hid_hi_made = sem("hid_hi_made")
        hid_lo_made = sem("hid_lo_made")
        down_made = sem("down_made")
        added = sem("added")

        def chunk_ahead(i, j):
            return 2 * i + 1 if j == 0 else 2 - 2 * i

        with nc.Block() as block:
            @block.sync
            def _(sp):
                sp.dma_start(rw[:], dram["router"][layer]).then_inc(const_loaded, 16)
                sp.dma_start(tri[:], dram["tri"]).then_inc(const_loaded, 16)
                sel_raw = raw[:].rearrange("p r c -> p (r c)")[0:LO_ROW + RC, 0:T * P]
                sp.dma_start(sel_raw, dram["sel"][layer]).then_inc(const_loaded, 16)
                sp.wait_ge(const_split, 1)
                for t in range(T):
                    if t >= RING:
                        sp.wait_ge(w_split, t - RING + 1)
                    sp.dma_start(raw[:, t % RING], dram["ffn"][layer][t]).then_inc(raw_loaded[t % RING], 16)

            @block.gpsimd
            def _(pool):
                pool.wait_ge(const_loaded, 48)
                sel_raw = raw[:].rearrange("p r c -> p (r c)")[0:LO_ROW + RC, 0:T * P]
                pool.tensor_copy(sel[:].rearrange("p t c -> p (t c)"), sel_raw).then_inc(const_split, 1)
                pool.tensor_copy(rw_hi[:], rw[:]).then_inc(const_split, 1)
                pool.wait_ge(const_split, 2)
                pool.tensor_tensor(rw_lo[:], rw[:], rw_hi[:].bitcast(F32), ALU.subtract).then_inc(const_split, 1)
                ln.split_lo(pool, x_hi[0], x_lo[0], 0)
                for t in range(T):
                    r = t % RING
                    pool.wait_ge(raw_loaded[r], 16 * (t // RING + 1))
                    pool.tensor_copy(w_hi[:, t], raw[:, r]).then_inc(w_hi_made, 1)
                    pool.wait_ge(w_hi_made, t + 1)
                    pool.tensor_tensor(w_lo[:, t], raw[:, r], w_hi[:, t].bitcast(F32),
                                       ALU.subtract).then_inc(w_split, 1)
                with pool.Fori(0, B // 2) as i:
                    for j in range(2):
                        ln.split_lo(pool, x_hi[1 - j], x_lo[1 - j], 2 * i + j + 1)

            @block.tensor
            def _(pe):
                pe.sem_inc(down_made, 2)

                def router_logits(p, n):
                    pe.wait_ge(ln.lo, ln.done + n + 1)
                    for q in range(TT):
                        lhs = slice(q * P, (q + 1) * P)
                        for k in range(KT):
                            out = sh.misc[:, q * RC:(q + 1) * RC]
                            pe.matmul(out, x_hi[p][:, k, lhs], rw_hi[:, k], start=(k == 0), stop=False)
                            pe.matmul(out, x_hi[p][:, k, lhs], rw_lo[:, k], start=False, stop=False)
                            ins = pe.matmul(out, x_lo[p][:, k, lhs], rw_hi[:, k], start=False, stop=(k == KT - 1))
                    ins.then_inc(logits_made, 1)

                def turn_comb(n):
                    pe.wait_ge(comb_made, n + 1)
                    for q in range(TT):
                        ins = pe.transpose(sh.misc[0:RC, q * P:(q + 1) * P], comb[:, q, :], sh.ident[:])
                    ins.then_inc(comb_turned, 1)

                def down(i, k):
                    t = k % T
                    pe.wait_ge(hid_hi_made, 2 * T * i + k + 3)
                    pe.wait_ge(hid_lo_made, 2 * T * i + k + 3)
                    if t == 0:
                        pe.wait_ge(added, 2 * i + k // T + 1)
                    for mt in range(KT):
                        cols = slice(2 * D + mt * P, 2 * D + (mt + 1) * P)
                        ins = split3(pe, psy[:, mt], w_hi[:, t, cols], w_lo[:, t, cols], hid_hi[k % 2][:],
                                     hid_lo[k % 2][:], start=(t == 0), stop=(t == T - 1))
                    ins.then_inc(down_made, 1)

                ln.take_mean(pe, 0)
                ln.take_var(pe, 0)
                pe.wait_ge(const_split, 3)
                router_logits(0, 0)
                turn_comb(0)
                with pe.Fori(0, B // 2) as i:
                    for k in range(2 * T):
                        j, t = k // T, k % T
                        if t == 0:
                            pe.wait_ge(ln.lo, ln.done + 2 * i + j + 1)
                        if j == 0:
                            pe.wait_ge(w_split, t + 1)
                        pe.wait_ge(act_made, 2 * T * i + k + 1)
                        for kt in range(KT):
                            c = slice(kt * P, (kt + 1) * P)
                            ins = split3(pe, psg[k % 2], w_hi[:, t, c], w_lo[:, t, c], x_hi[j][:, kt],
                                         x_lo[j][:, kt], start=(kt == 0), stop=(kt == KT - 1))
                        ins.then_inc(gate_made, 1)
                        pe.wait_ge(up_used, 2 * T * i + k + 1)
                        for kt in range(KT):
                            c = slice(D + kt * P, D + (kt + 1) * P)
                            ins = split3(pe, psu[k % 2], w_hi[:, t, c], w_lo[:, t, c], x_hi[j][:, kt],
                                         x_lo[j][:, kt], start=(kt == 0), stop=(kt == KT - 1))
                        ins.then_inc(up_made, 1)
                        if t == 0:
                            pe.wait_ge(comb_split, 2 * i + j + 1)
                        pe.wait_ge(hid_made, 2 * T * i + k + 2)
                        pe.matmul(psc[:], sel[:, t], comb_t[j][:], start=True, stop=True).then_inc(scale_made, 1)
                        if k >= 2:
                            down(i, k - 2)
                        n = 2 * i + j + 1
                        if t == 2:
                            ln.take_mean(pe, n)
                        if t == 4:
                            ln.take_var(pe, n)
                        if t == 7:
                            router_logits(1 - j, n)
                        if t == 10:
                            turn_comb(n)
                    down(i, 2 * T - 2)
                    down(i, 2 * T - 1)

            @block.scalar
            def _(act):
                act.sem_inc(act_made, 2)
                act.sem_inc(hid_hi_made, 2)

                def router_exps(n):
                    act.wait_ge(logits_made, n + 1)
                    act.activation(sig[:], sh.misc[:, 0:TT * RC].rearrange("p (q c) -> p q c", c=RC)[:, :, 0:E + 1],
                                   ACT.Exp, scale=-1.0).then_inc(neg_exp_made, 1)
                    if layer == 1:
                        act.wait_ge(shifted, n + 1)
                        act.activation(score[:], score[:], ACT.Exp).then_inc(soft_exp_made, 1)

                def split_hid(i, k):
                    act.wait_ge(hid_made, 2 * T * i + k + 3)
                    act.wait_ge(down_made, 2 * T * i + k + 1)
                    act.activation(hid_hi[k % 2][:], hid[k % 2][:], ACT.Copy).then_inc(hid_hi_made, 1)

                ln.square(act, 0)
                ln.take_root(act, 0)
                ln.split_hi(act, x_hi[0], 0)
                router_exps(0)
                with act.Fori(0, B // 2) as i:
                    for k in range(2 * T):
                        j, t = k // T, k % T
                        act.wait_ge(gate_made, 2 * T * i + k + 1)
                        act.wait_ge(hid_made, 2 * T * i + k + 1)
                        act.activation(act_g[k % 2][:], psg[k % 2], ACT.Silu).then_inc(act_made, 1)
                        if k >= 1:
                            split_hid(i, k - 1)
                        n = 2 * i + j + 1
                        if t == 3:
                            ln.square(act, n)
                        if t == 5:
                            ln.take_root(act, n)
                        if t == 6:
                            ln.split_hi(act, x_hi[1 - j], n)
                        if t == 8:
                            router_exps(n)
                    split_hid(i, 2 * T - 1)

            @block.vector
            def _(dve):
                dve.sem_inc(up_used, 2)
                dve.sem_inc(hid_made, 2)
                dve.sem_inc(hid_lo_made, 2)
                dve.sem_inc(added, 1)

                def router(n):
                    steps = [0]

                    def link(ins):
                        ins.then_inc(router_step, 1)
                        steps[0] += 1
                        dve.wait_ge(router_step, n * ROUTER_STEPS[layer] + steps[0])

                    lg = sh.misc[:, 0:TT * RC].rearrange("p (q c) -> p q c", c=RC)[:, :, 0:E]
                    dve.wait_ge(neg_exp_made, n + 1)
                    link(dve.tensor_scalar(sig[:], sig[:], 1.0, None, ALU.add))
                    link(dve.reciprocal(sig[:], sig[:]))
                    if layer == 1:
                        link(dve.tensor_reduce(col[:, 0], lg, AX.X, ALU.max))
                        dve.tensor_tensor(score[:], lg, col[:, 0].unsqueeze(2).to_broadcast([P, TT, E]),
                                          ALU.subtract).then_inc(shifted, 1)
                        dve.wait_ge(soft_exp_made, n + 1)
                        link(dve.tensor_reduce(col[:, 1], score[:], AX.X, ALU.add))
                        link(dve.reciprocal(col[:, 1], col[:, 1]))
                        link(dve.tensor_tensor(score[:], score[:], col[:, 1].unsqueeze(2).to_broadcast([P, TT, E]),
                                               ALU.mult))
                        sc = score[:]
                    else:
                        sc = sig[:, :, 0:E]
                    mine = sc.unsqueeze(3).to_broadcast([P, TT, E, E])
                    other = sc.unsqueeze(2).to_broadcast([P, TT, E, E])
                    tri4 = tri[:].rearrange("p (a b) -> p a b", a=E)
                    link(dve.tensor_tensor(ahead[:], other, mine, ALU.is_gt))
                    link(dve.tensor_tensor(tied[:], other, mine, ALU.is_equal))
                    for q in range(TT):
                        last = dve.tensor_tensor(tied[:, q], tied[:, q], tri4, ALU.mult)
                    link(last)
                    link(dve.tensor_tensor(ahead[:], ahead[:], tied[:], ALU.add))
                    link(dve.tensor_reduce(tied[:, :, :, 0], ahead[:], AX.X, ALU.add))
                    link(dve.scalar_tensor_tensor(out=comb[:, :, 0:E], in0=tied[:, :, :, 0], scalar=2.0, in1=sc,
                                                  op0=ALU.is_lt, op1=ALU.mult))
                    if layer == 1:
                        link(dve.tensor_reduce(col[:, 2], comb[:, :, 0:E], AX.X, ALU.add))
                        link(dve.reciprocal(col[:, 3], col[:, 2]))
                        link(dve.tensor_copy(comb[:, :, E:E + 1], sig[:, :, E:E + 1]))
                        gain = 1.0
                    else:
                        link(dve.tensor_reduce(col[:, 2], comb[:, :, 0:E], AX.X, ALU.add))
                        link(dve.tensor_scalar(col[:, 2], col[:, 2], 1e-20, None, ALU.add))
                        link(dve.reciprocal(col[:, 3], col[:, 2]))
                        gain = 2.5
                    dve.scalar_tensor_tensor(out=comb[:, :, 0:E], in0=comb[:, :, 0:E], scalar=gain,
                                             in1=col[:, 3].unsqueeze(2).to_broadcast([P, TT, E]), op0=ALU.mult,
                                             op1=ALU.mult).then_inc(comb_made, 1)
                    assert steps[0] == ROUTER_STEPS[layer], steps[0]

                def split_comb(p, n):
                    dve.wait_ge(comb_turned, n + 1)
                    dve.tensor_copy(comb_t[p][0:RC], sh.misc[0:RC]).then_inc(comb_hi_made, 1)
                    dve.wait_ge(comb_hi_made, n + 1)
                    dve.tensor_tensor(comb_t[p][LO_ROW:LO_ROW + RC], sh.misc[0:RC], comb_t[p][0:RC].bitcast(F32),
                                      ALU.subtract).then_inc(comb_split, 1)

                def split_hid(i, k):
                    dve.wait_ge(hid_hi_made, 2 * T * i + k + 3)
                    dve.wait_ge(down_made, 2 * T * i + k + 1)
                    dve.tensor_tensor(hid_lo[k % 2][:], hid[k % 2][:], hid_hi[k % 2][:].bitcast(F32),
                                      ALU.subtract).then_inc(hid_lo_made, 1)

                def add_output(i, j):
                    dve.wait_ge(down_made, 2 * T * i + (j + 1) * T + 2)
                    xc = sh.x[:, 2 * i + j]
                    dve.scalar_tensor_tensor(out=xc, in0=psy[:], scalar=0.5, in1=xc, op0=ALU.mult,
                                             op1=ALU.add).then_inc(added, 1)

                ln.sum_tiles(dve, sh.x[:, 0])
                ln.centre(dve, sh.x[:, 0], 0)
                ln.sum_squares(dve, 0)
                ln.scale(dve, 0)
                dve.memset(comb_t[0][:].bitcast(F32), 0.0).then_inc(const_set, 1)
                dve.memset(comb_t[1][:].bitcast(F32), 0.0).then_inc(const_set, 1)
                dve.memset(comb[:], 0.0).then_inc(const_set, 1)
                dve.wait_ge(const_set, 3)
                dve.memset(comb[:, :, E:E + 1], 1.0).then_inc(const_set, 1)
                dve.wait_ge(const_set, 4)
                dve.wait_ge(const_loaded, 48)
                router(0)
                split_comb(0, 0)
                with dve.Fori(0, B // 2) as i:
                    for k in range(2 * T):
                        j, t = k // T, k % T
                        if k == T + 2:
                            add_output(i, 0)
                        if k == T + 1:
                            dve.wait_ge(added, i + 1)
                        dve.wait_ge(act_made, 2 * T * i + k + 3)
                        dve.wait_ge(up_made, 2 * T * i + k + 1)
                        dve.tensor_tensor(act_g[k % 2][:], act_g[k % 2][:], psu[k % 2],
                                          ALU.mult).then_inc(up_used, 1)
                        dve.wait_ge(up_used, 2 * T * i + k + 3)
                        dve.wait_ge(scale_made, 2 * T * i + k + 1)
                        dve.wait_ge(hid_hi_made, 2 * T * i + k + 1)
                        dve.wait_ge(hid_lo_made, 2 * T * i + k + 1)
                        dve.tensor_tensor(hid[k % 2][:], act_g[k % 2][:], psc[:], ALU.mult).then_inc(hid_made, 1)
                        if k >= 1:
                            split_hid(i, k - 1)
                        n = 2 * i + j + 1
                        xn = sh.x[:, chunk_ahead(i, j)]
                        if t == 1:
                            ln.sum_tiles(dve, xn)
                        if t == 3:
                            ln.centre(dve, xn, n)
                        if t == 4:
                            ln.sum_squares(dve, n)
                        if t == 5:
                            ln.scale(dve, n)
                        if t == 8:
                            router(n)
                        if t == 11:
                            split_comb(1 - j, n)
                    split_hid(i, 2 * T - 1)
                    add_output(i, 1)




def attention_phase(nc, sh, name, layer, dram):
    causal = layer == 0
    lora = layer == 1
    with ExitStack() as ctx:
        def sb(n, shape, dt):
            return ctx.enter_context(nc.sbuf_tensor(f"{name}_{n}", shape, dt))

        def sem(n):
            handle = nc.alloc_semaphore(name=f"{name}_{n}")
            sh.semaphores.append(handle)
            return handle

        wqk_hi = sb("wqk_hi", [P, 2, KT, G * P], F32R)
        wqk_lo = sb("wqk_lo", [P, 2, KT, G * P], F32R)
        wv_hi = sb("wv_hi", [P, KT, D], F32R)
        wv_lo = sb("wv_lo", [P, KT, D], F32R)
        wo = sb("wo", [P, G, D], F32)
        b_col = sb("b_col", [P, 2 * G], F32)
        bv = sb("bv", [P, D], F32)
        bo = sb("bo", [P, KT], F32)
        den_sel = sb("den_sel", [P, P], F32)
        if causal:
            bias_rows = sb("bias_rows", [P, G, S], F32)
            mask_in = sb("mask_in", [P, 3, P], F32)
            mask = sb("mask", [P, 3, P], BF16)
        x_hi = sb("x_hi", [P, KT, S], F32R)
        x_lo = sb("x_lo", [P, KT, S], F32R)
        qk = [sb(f"{n}_all", [P, S], F32) for n in "qk"]
        qk_hi = sb("qk_hi", [P, 2, HALF, S], F32R)
        qk_lo = sb("qk_lo", [P, 2, HALF, S], F32R)
        stack = [sb(f"{n}_stack", [STACK, G, HG, S], F32R) for n in "qk"]
        neg_max = sb("neg_max", [P, TT, HG], F32)
        max_hi = sb("max_hi", [HG, S], F32R)
        max_lo = sb("max_lo", [HG, S], F32R)
        probs = sb("probs", [P, PROBS, 2, S], F32)
        v_one = sb("v_one", [P, TT, H, 32], F32)
        heads = sb("heads", [P, S], F32)
        rden = sb("rden", [P, S], F32)
        context = sb("context", [P, G, S], F32)

        flat = probs[:].rearrange("p a b c -> p (a b c)")
        wqk = flat[:, 0:4 * G * P].rearrange("p (w k c) -> p w k c", w=2, k=KT)
        wv = flat[:, 4 * G * P:4 * G * P + KT * D].rearrange("p (k c) -> p k c", k=KT)
        l_in = context[0:RANK].rearrange("p a b -> p (a b)")[:, 0:3 * D + G * P]
        l_out = flat[0:RANK, 4 * G * P + KT * D:4 * G * P + KT * D + 2 * G * P + D]
        l_out_o = rden[0:RANK, 0:D]

        ps_a = [sh.pair_a[:, 0], sh.pair_a[:, 1]]
        ps_b = sh.pair_b
        ps_o = sh.bank
        misc = sh.misc

        loaded = sem("loaded")
        w_hi_made = sem("w_hi_made")
        w_split = sem("w_split")
        set_up = sem("set_up")
        ln = sh.norm
        a_full = sem("a_full")
        a_taken = sem("a_taken")
        qk_hi_made = sem("qk_hi_made")
        qk_lo_made = sem("qk_lo_made")
        stacked = sem("stacked")
        max_stacked = sem("max_stacked")
        max_turned = sem("max_turned")
        max_hi_made = sem("max_hi_made")
        max_lo_made = sem("max_lo_made")
        b_full = sem("b_full")
        b_taken = sem("b_taken")
        pv_made = sem("pv_made")
        heads_kept = sem("heads_kept")
        den_made = sem("den_made")
        den_log = sem("den_log")
        rden_made = sem("rden_made")
        context_made = sem("context_made")

        def k_end(q):
            return (q + 1) * P if causal else S

        def q_start(k):
            return k * P if causal else 0

        n_loads = 9 if causal else 10
        before = LORA_UNITS if lora else 0
        base = before + A_PROLOGUE

        with nc.Block() as block:
            @block.sync
            def _(sp):
                for dst, src in ((wqk, "wqk"), (wv, "wv"), (wo[:], "wo"), (b_col[:], "b_col"), (bv[:], "bv"),
                                 (bo[:], "bo")):
                    sp.dma_start(dst, dram[src][layer]).then_inc(loaded, 16)
                sp.dma_start(den_sel[:], dram["den_sel"]).then_inc(loaded, 16)
                if causal:
                    sp.dma_start(bias_rows[:], dram["bias_rows"]).then_inc(loaded, 16)
                    sp.dma_start(mask_in[:], dram["masks"]).then_inc(loaded, 16)
                if lora:
                    for dst, src in ((l_in, "l_in"), (l_out, "l_out"), (l_out_o, "l_out_o")):
                        sp.dma_start(dst, dram[src]).then_inc(loaded, 16)
                sp.wait_ge(set_up, 2)

                def stack_rows(which, row, src, half):
                    for j in range(HG):
                        dst = stack[which][row:row + ROWS, HALF * half:HALF * (half + 1), j]
                        sp.dma_start(dst.bitcast(F32), src[32 * j:32 * j + ROWS, which].bitcast(F32)
                                     ).then_inc(stacked, 16)

                def stack_half(half, made):
                    sp.wait_ge(qk_hi_made, made)
                    for which, row in ((0, 0), (0, 32), (1, 0), (1, 64)):
                        stack_rows(which, row, qk_hi, half)
                    sp.wait_ge(qk_lo_made, made)
                    for which, row in ((0, 64), (1, 32)):
                        stack_rows(which, row, qk_lo, half)

                def stack_max(m, g):
                    sp.wait_ge(max_lo_made, m + 1)
                    for row, src in ((0, max_hi), (32, max_hi), (64, max_lo)):
                        sp.dma_start(stack[0][row:row + 1, g].bitcast(F32), src[:].bitcast(F32)
                                     ).then_inc(max_stacked, 16)

                def chunk(b, last):
                    stack_max(G * b + 1, 1)
                    stack_max(G * b + 2, 2)
                    if not last:
                        stack_half(0, 2 * G * b + 2 * G + 2 * HALF + 2)
                    stack_max(G * b + 3, 3)
                    if not last:
                        stack_max(G * b + 4, 0)
                        stack_half(1, 2 * G * b + 4 * G + 2)

                stack_half(0, 2 * HALF + 2)
                stack_max(0, 0)
                stack_half(1, 2 * G + 2)
                with sp.Fori(0, B - 1) as b:
                    chunk(b, False)
                chunk(B - 1, True)

            @block.gpsimd
            def _(pool):
                pool.sem_inc(qk_lo_made, 2)
                for which in range(2):
                    pool.memset(stack[which][:].bitcast(F32), 0.0).then_inc(set_up, 1)
                pool.wait_ge(w_hi_made, 3)
                pool.tensor_tensor(wqk_lo[:, 0], wqk[:, 0], wqk_hi[:, 0].bitcast(F32),
                                   ALU.subtract).then_inc(w_split, 1)
                pool.tensor_tensor(wqk_lo[:, 1], wqk[:, 1], wqk_hi[:, 1].bitcast(F32),
                                   ALU.subtract).then_inc(w_split, 1)
                pool.tensor_tensor(wv_lo[:], wv, wv_hi[:].bitcast(F32), ALU.subtract).then_inc(w_split, 1)

                def split_lo(b, n):
                    which = n % 2
                    pool.wait_ge(qk_hi_made, 2 * G * b + n + 3)
                    pool.tensor_tensor(qk_lo[:, which, n // 2 % HALF], qk[which][:],
                                       qk_hi[:, which, n // 2 % HALF].bitcast(F32),
                                       ALU.subtract).then_inc(qk_lo_made, 1)

                def chunk(b):
                    ln.split_lo(pool, x_hi, x_lo, b)
                    for n in range(2 * G):
                        split_lo(b, n)

                chunk(0)
                with pool.Fori(1, B) as b:
                    chunk(b)

            @block.tensor
            def _(pe):
                pe.sem_inc(pv_made, 2)

                def use_a(unit):
                    pe.wait_ge(a_taken, unit + 1)

                def project(unit, n, parity):
                    g, which = n // 2, n % 2
                    use_a(unit)
                    c = slice(g * P, (g + 1) * P)
                    for kt in range(KT):
                        ins = split3(pe, ps_a[parity], wqk_hi[:, which, kt, c], wqk_lo[:, which, kt, c],
                                     x_hi[:, kt], x_lo[:, kt], start=(kt == 0), stop=(kt == KT - 1))
                    ins.then_inc(a_full, 1)

                def project_v(unit, q, parity):
                    use_a(unit)
                    t = slice(q * P, (q + 1) * P)
                    for kt in range(KT):
                        ins = split3(pe, ps_a[parity][:, 0:D], x_hi[:, kt, t], x_lo[:, kt, t], wv_hi[:, kt],
                                     wv_lo[:, kt], start=(kt == 0), stop=(kt == KT - 1))
                    ins.then_inc(a_full, 1)

                def max_scores(unit, g, n, parity):
                    q, j = n // HG, n % HG
                    use_a(unit)
                    out = ps_a[parity]
                    end = k_end(q)
                    ins = pe.matmul(out[:, 0:end], stack[0][:, g, j, q * P:(q + 1) * P], stack[1][:, g, j, 0:end],
                                    start=True, stop=not causal)
                    if causal:
                        ins = pe.matmul(out[:, q * P:end], mask[:, 0], mask[:, 1], start=False, stop=True)
                    ins.then_inc(a_full, 1)

                def scores(m, g, u):
                    k, pair = u // 2, u % 2
                    pe.wait_ge(b_taken, B_UNITS * m + u + 1)
                    lo = q_start(k)
                    for half in range(2):
                        j = 2 * pair + half
                        out = ps_b[u % 2][:, half]
                        ins = pe.matmul(out[:, lo:S], stack[1][:, g, j, k * P:(k + 1) * P],
                                        stack[0][:, g, j, lo:S], start=True, stop=not causal)
                        if causal:
                            ins = pe.matmul(out[:, lo:lo + P], mask[:, 0], mask[:, 2], start=False, stop=True)
                    ins.then_inc(b_full, 1)

                def attend(m, g, k):
                    pe.wait_ge(b_taken, B_UNITS * m + 2 * k + 4)
                    if k == 0:
                        pe.wait_ge(heads_kept, m + 1)
                    lo = q_start(k)
                    for j in range(HG):
                        ins = pe.matmul(ps_o[32 * j:32 * (j + 1), lo:S], v_one[:, k, HG * g + j],
                                        probs[:, (2 * k + j // 2) % PROBS, j % 2, lo:S], start=(k == 0),
                                        stop=(k == TT - 1), tile_position=(0, 32 * j), skip_group_check=True)
                    ins.then_inc(pv_made, 1)

                def turn_max(m, last_unit):
                    pe.wait_ge(a_taken, last_unit + 3)
                    for q in range(TT):
                        ins = pe.transpose(misc[0:HG, q * P:(q + 1) * P], neg_max[:, q], sh.ident[:])
                    ins.then_inc(max_turned, 1)

                def spread_den(m, alone):
                    pe.wait_ge(heads_kept, m + 2)
                    if alone:
                        pe.wait_ge(den_log, m + 1)
                    else:
                        pe.wait_ge(max_hi_made, m + 2)
                        pe.wait_ge(max_lo_made, m + 2)
                    pe.matmul(misc[:], den_sel[:], heads[:], start=True, stop=True).then_inc(den_made, 1)

                def output(unit, mt, parity, b):
                    use_a(unit)
                    for g in range(G):
                        pe.wait_ge(context_made, G * b + g + 2)
                        ins = pe.matmul(ps_a[parity], wo[:, g, mt * P:(mt + 1) * P], context[:, g], start=(g == 0),
                                        stop=(g == G - 1))
                    ins.then_inc(a_full, 1)

                pe.wait_ge(loaded, 16 * n_loads)
                if lora:
                    for unit in range(LORA_UNITS):
                        use_a(unit)
                        n, kt = unit // KT, unit % KT
                        if n < 3:
                            lhs = l_in[:, n * D + kt * P:n * D + (kt + 1) * P]
                            rhs = l_out[:, n * G * P:n * G * P + (G * P if n < 2 else D)]
                        else:
                            g = unit - 3 * KT
                            lhs = l_in[:, 3 * D + g * P:3 * D + (g + 1) * P]
                            rhs = l_out_o
                        pe.matmul(ps_a[unit % 2][:, 0:rhs.shape[-1]], lhs, rhs, start=True,
                                  stop=True).then_inc(a_full, 1)
                ln.take_mean(pe, 0)
                ln.take_var(pe, 0)
                pe.wait_ge(w_split, 3)
                pe.wait_ge(ln.lo, ln.done + 1)
                unit = before
                for n in range(2 * HALF):
                    project(unit, n, unit % 2)
                    unit += 1
                pe.wait_ge(stacked, STACKED)
                for n in range(TT * HG):
                    max_scores(unit, 0, n, unit % 2)
                    unit += 1
                pe.wait_ge(ln.refined, ln.done + 1)
                turn_max(0, unit - 1)
                for n in range(2 * HALF, 4 * HALF):
                    project(unit, n, unit % 2)
                    unit += 1
                for q in range(TT):
                    project_v(unit, q, unit % 2)
                    unit += 1
                assert unit == base and base % 2 == 0 and A_UNITS % 2 == 0

                def chunk(b, last):
                    count = [0]

                    def next_a():
                        count[0] += 1
                        return base + A_UNITS * b + count[0] - 1, (count[0] - 1) % 2

                    for s in range(1, G + 1):
                        m = G * b + s
                        maxima = s < G or not last
                        for u in range(SLOTS):
                            if s == G and u < 2 * HALF and not last:
                                unit, parity = next_a()
                                project(unit, 2 * HALF + u, parity)
                            if maxima and u < 8:
                                if u == 0 and s in (HALF, G):
                                    pe.wait_ge(stacked, 2 * STACKED * b + STACKED * (s // HALF + 1))
                                for n in (2 * u, 2 * u + 1):
                                    unit, parity = next_a()
                                    max_scores(unit, s % G, n, parity)
                            v = u - LAG
                            if v >= 0:
                                if v == 0:
                                    pe.wait_ge(max_stacked, MAX_STACKED * m)
                                scores(m - 1, s - 1, v)
                                if v % 2 == 1 and v >= 3:
                                    attend(m - 1, s - 1, (v - 3) // 2)
                            if s == 1 and not last:
                                if u == 1:
                                    pe.wait_ge(max_hi_made, m)
                                    pe.wait_ge(max_lo_made, m)
                                    pe.wait_ge(den_log, m)
                                    ln.take_mean(pe, b + 1)
                                if u == 5:
                                    ln.take_var(pe, b + 1)
                                if u in (8, 9):
                                    if u == 8:
                                        pe.wait_ge(ln.lo, ln.done + b + 2)
                                    for n in range(2 * (u - 8), 2 * (u - 8) + 2):
                                        unit, parity = next_a()
                                        project(unit, n, parity)
                            if maxima and u == TURN:
                                pe.wait_ge(max_hi_made, m)
                                pe.wait_ge(max_lo_made, m)
                                pe.wait_ge(den_log, m)
                                if not last:
                                    pe.wait_ge(ln.refined, ln.done + b + 2)
                                turn_max(m, base + A_UNITS * b + (s - 1) * TT * HG + TT * HG - 1
                                         + (2 * HALF if s > 1 and not last else 0) + (2 * HALF if s == G else 0))
                        attend(m - 1, s - 1, TT - 1)
                        spread_den(m - 1, not maxima)
                    if not last:
                        for q in range(TT):
                            unit, parity = next_a()
                            project_v(unit, q, parity)
                    for mt in range(KT):
                        unit, parity = next_a()
                        output(unit, mt, parity, b)

                with pe.Fori(0, B - 1) as b:
                    chunk(b, False)
                chunk(B - 1, True)

            @block.scalar
            def _(act):
                act.sem_inc(b_taken, 2)
                act.sem_inc(heads_kept, 1)
                act.sem_inc(den_log, 1)
                act.sem_inc(qk_hi_made, 2)
                act.preload_act_table_set("natural_log_exp_and_others")
                act.wait_ge(loaded, 16 * n_loads)
                if lora:
                    act.wait_ge(a_taken, LORA_UNITS + 2)
                act.activation(wqk_hi[:, 0], wqk[:, 0], ACT.Copy).then_inc(w_hi_made, 1)
                act.activation(wqk_hi[:, 1], wqk[:, 1], ACT.Copy).then_inc(w_hi_made, 1)
                act.activation(wv_hi[:], wv, ACT.Copy).then_inc(w_hi_made, 1)

                def split_hi(b, n, unit):
                    which = n % 2
                    act.wait_ge(a_taken, unit + 3)
                    act.activation(qk_hi[:, which, n // 2 % HALF], qk[which][:], ACT.Copy).then_inc(qk_hi_made, 1)

                def keep_max(m):
                    act.wait_ge(max_turned, m + 1)
                    act.activation(max_hi[:], misc[0:HG], ACT.Copy).then_inc(max_hi_made, 1)

                def exps(m, u):
                    k = u // 2
                    lo = q_start(k)
                    act.wait_ge(b_full, B_UNITS * m + u + 1)
                    act.wait_ge(pv_made, TT * m + (u - PROBS) // 2 + 3)
                    act.activation(probs[:, u % PROBS, :, lo:S], ps_b[u % 2][:, :, lo:S], ACT.Exp,
                                   scale=float(HD) ** -0.5).then_inc(b_taken, 1)

                def denominators(m):
                    act.wait_ge(pv_made, TT * m + TT + 2)
                    act.wait_ge(context_made, m + 1)
                    act.activation(heads[:], ps_o[:], ACT.Copy).then_inc(heads_kept, 1)
                    act.wait_ge(den_made, m + 1)
                    act.activation(rden[:], misc[:], ACT.Ln).then_inc(den_log, 1)
                    act.wait_ge(den_log, m + 2)
                    act.activation(rden[:], rden[:], ACT.Exp, scale=-1.0).then_inc(rden_made, 1)

                ln.square(act, 0)
                ln.take_root(act, 0)
                ln.split_hi(act, x_hi, 0)
                for n in range(2 * HALF):
                    split_hi(0, n, before + n)
                keep_max(0)
                act.wait_ge(stacked, STACKED)
                for n in range(2 * HALF, 4 * HALF):
                    split_hi(0, n, base - TT - 4 * HALF + n)

                def chunk(b, last):
                    for s in range(1, G + 1):
                        m = G * b + s
                        for u in range(SLOTS):
                            if s == G and u < 2 * HALF and not last:
                                if u == 0:
                                    act.wait_ge(stacked, 2 * STACKED * b + 3 * STACKED)
                                split_hi(b + 1, 2 * HALF + u, base + A_UNITS * b + A_QK[1] + 3 * u)
                            v = u - LAG
                            if v >= 0:
                                exps(m - 1, v)
                            if s == 1 and not last:
                                if u == 3:
                                    ln.square(act, b + 1)
                                if u == 6:
                                    ln.take_root(act, b + 1)
                                if u == 7:
                                    ln.split_hi(act, x_hi, b + 1)
                                if u in (9, 10):
                                    if u == 9:
                                        act.wait_ge(stacked, 2 * STACKED * b + 2 * STACKED)
                                    for n in range(2 * (u - 9), 2 * (u - 9) + 2):
                                        split_hi(b + 1, n, base + A_UNITS * b + A_QK[0] + n)
                            if u == TURN and (s < G or not last):
                                act.wait_ge(max_stacked, MAX_STACKED * m)
                                keep_max(m)
                        denominators(m - 1)

                with act.Fori(0, B - 1) as b:
                    chunk(b, False)
                chunk(B - 1, True)

            @block.vector
            def _(dve):
                dve.sem_inc(a_taken, 2)
                dve.sem_inc(context_made, 1)
                ln.sum_tiles(dve, sh.x[:, 0])
                dve.memset(v_one[:, :, :, HD:32], 1.0)
                dve.wait_ge(loaded, 16 * n_loads)
                if causal:
                    dve.tensor_copy(mask[:], mask_in[:]).then_inc(set_up, 1)
                if lora:
                    targets = [wqk[:, n, kt] for n in range(2) for kt in range(KT)]
                    targets += [wv[:, kt] for kt in range(KT)] + [wo[:, g] for g in range(G)]
                    for unit, w in enumerate(targets):
                        dve.wait_ge(a_full, unit + 1)
                        dve.scalar_tensor_tensor(out=w, in0=ps_a[unit % 2][:, 0:w.shape[-1]], scalar=0.5, in1=w,
                                                 op0=ALU.mult, op1=ALU.add).then_inc(a_taken, 1)
                ln.centre(dve, sh.x[:, 0], 0)
                ln.sum_squares(dve, 0)
                ln.scale(dve, 0)

                def keep_qk(b, unit, parity, n):
                    g, which = n // 2, n % 2
                    dve.wait_ge(a_full, unit + 1)
                    dve.wait_ge(qk_hi_made, 2 * G * b + n + 1)
                    dve.wait_ge(qk_lo_made, 2 * G * b + n + 1)
                    bias = b_col[:, G * which + g:G * which + g + 1]
                    if which == 1 and causal:
                        dve.scalar_tensor_tensor(out=qk[1][:], in0=ps_a[parity], scalar=bias, in1=bias_rows[:, g],
                                                 op0=ALU.add, op1=ALU.add).then_inc(a_taken, 1)
                    else:
                        dve.tensor_scalar(qk[which][:], ps_a[parity], bias, None, ALU.add).then_inc(a_taken, 1)

                def take_max(unit, parity, n):
                    q, j = n // HG, n % HG
                    dve.wait_ge(a_full, unit + 1)
                    dve.tensor_reduce(neg_max[:, q, j:j + 1], ps_a[parity][:, 0:k_end(q)], AX.X, ALU.max,
                                      negate=True).then_inc(a_taken, 1)

                def split_max(m):
                    dve.wait_ge(max_hi_made, m + 1)
                    dve.tensor_tensor(max_lo[:], misc[0:HG], max_hi[:].bitcast(F32),
                                      ALU.subtract).then_inc(max_lo_made, 1)

                def keep_v(unit, parity, q):
                    dve.wait_ge(a_full, unit + 1)
                    dve.tensor_tensor(v_one[:, q, :, 0:HD], ps_a[parity][:, 0:D].rearrange("p (h c) -> p h c", h=H),
                                      bv[:].rearrange("p (h c) -> p h c", h=H), ALU.add).then_inc(a_taken, 1)

                def make_context(m, g):
                    dve.wait_ge(rden_made, m + 1)
                    dve.tensor_tensor(context[:, g], heads[:], rden[:], ALU.mult).then_inc(context_made, 1)

                unit = before
                for n in range(2 * HALF):
                    keep_qk(0, unit, unit % 2, n)
                    unit += 1
                for n in range(TT * HG):
                    take_max(unit, unit % 2, n)
                    unit += 1
                split_max(0)
                for n in range(2 * HALF, 4 * HALF):
                    keep_qk(0, unit, unit % 2, n)
                    unit += 1
                for q in range(TT):
                    keep_v(unit, unit % 2, q)
                    unit += 1

                def chunk(b, last):
                    count = [0]

                    def next_a():
                        count[0] += 1
                        return base + A_UNITS * b + count[0] - 1, (count[0] - 1) % 2

                    for s in range(1, G + 1):
                        m = G * b + s
                        maxima = s < G or not last
                        for u in range(SLOTS):
                            if s == G and u < 2 * HALF and not last:
                                unit, parity = next_a()
                                keep_qk(b + 1, unit, parity, 2 * HALF + u)
                            if maxima and u < 8:
                                if u == 0:
                                    dve.wait_ge(max_turned, m)
                                for n in (2 * u, 2 * u + 1):
                                    unit, parity = next_a()
                                    take_max(unit, parity, n)
                            if u == 2 and s > 1:
                                make_context(m - 2, s - 2)
                            if s == 1 and not last:
                                xn = sh.x[:, b + 1]
                                if u == 0:
                                    ln.sum_tiles(dve, xn)
                                if u == 2:
                                    ln.centre(dve, xn, b + 1)
                                if u == 4:
                                    ln.sum_squares(dve, b + 1)
                                if u == 7:
                                    ln.scale(dve, b + 1)
                                if u in (8, 9):
                                    for n in range(2 * (u - 8), 2 * (u - 8) + 2):
                                        unit, parity = next_a()
                                        keep_qk(b + 1, unit, parity, n)
                            if maxima and u == TURN:
                                split_max(m)
                    if not last:
                        dve.wait_ge(pv_made, TT * (G * b + G) + 2)
                        for q in range(TT):
                            unit, parity = next_a()
                            keep_v(unit, parity, q)
                    make_context(G * b + G - 1, G - 1)
                    for mt in range(KT):
                        unit, parity = next_a()
                        xm = sh.x[:, b, mt]
                        dve.wait_ge(a_full, unit + 1)
                        dve.scalar_tensor_tensor(out=xm, in0=ps_a[parity], scalar=bo[:, mt:mt + 1], in1=xm,
                                                 op0=ALU.add, op1=ALU.add).then_inc(a_taken, 1)

                with dve.Fori(0, B - 1) as b:
                    chunk(b, False)
                chunk(B - 1, True)


def program(nc, dram, out, phases):
    with ExitStack() as ctx:
        class Sh:
            pass
        sh = Sh()
        sh.ctx = ctx

        def sb(n, shape, dt):
            return ctx.enter_context(nc.sbuf_tensor(n, shape, dt))

        sh.x = sb("x", [P, B, KT, S], F32)
        sh.mean_w = sb("mean_weights", [P, P], F32)
        sh.ident = sb("identity", [P, P], F32)
        sh.eps = sb("eps", [P, 1], F32)
        sh.ln_sum = sb("ln_sum", [P, S], F32)
        sh.ln_x = sb("ln_x", [P, KT, S], F32)
        sh.ln_sq = sb("ln_sq", [P, KT, S], F32)
        sh.ln_r = sb("ln_r", [P, S], F32)
        sh.pair_a = ctx.enter_context(nc.psum_tensor("pair_a", [P, 2, S], F32))
        sh.pair_b = [ctx.enter_context(nc.psum_tensor(f"pair_b{n}", [P, 2, S], F32)) for n in range(2)]
        sh.bank = ctx.enter_context(nc.psum_tensor("bank", [P, S], F32))
        sh.misc = ctx.enter_context(nc.psum_tensor("misc", [P, S], F32))
        loaded = ctx.enter_context(nc.semaphore("loaded"))
        made = ctx.enter_context(nc.semaphore("made"))
        stored = ctx.enter_context(nc.semaphore("stored"))
        sh.semaphores = []
        sh.norm = Norm(sh, lambda n: ctx.enter_context(nc.semaphore(n)))
        load_constants(nc, sh, dram, loaded, made)
        for n, (kind, layer) in enumerate(phases):
            if kind == "ffn":
                ffn_phase(nc, sh, f"f{n}", layer, dram)
                sh.norm.done += B + 1
            else:
                attention_phase(nc, sh, f"a{n}", layer, dram)
                sh.norm.done += B
            nc.clear_and_free_semaphores(sh.semaphores)
            sh.semaphores = []
            nc.all_engine_barrier()
        store_output(nc, sh, out, stored)


PHASES = (("ffn", 0), ("attn", 0), ("ffn", 0), ("ffn", 1), ("attn", 1), ("ffn", 1))


def feature_major(w):
    return w.reshape(KT, P, -1).transpose(1, 0, 2)


def ffn_tiles(gate, up, down, layer):
    T = TILES[layer]
    f = gate.shape[0]
    out = np.zeros((T, P, WC), np.float32)
    for at, w in ((0, gate), (D, up)):
        padded = np.zeros((T * P, D), np.float32)
        padded[:f] = w
        out[:, :, at:at + D] = padded.reshape(T, P, KT, P).transpose(0, 3, 2, 1).reshape(T, P, D)
    padded = np.zeros((T * P, D), np.float32)
    padded[:f] = down.T
    out[:, :, 2 * D:] = padded.reshape(T, P, D)
    return out


def selectors(layer):
    T = TILES[layer]
    owner = np.minimum(np.arange(T * P) // MOE, E)
    rows = (np.arange(RC)[:, None] == owner[None, :]).astype(np.float32)
    out = np.zeros((LO_ROW + RC, T * P), np.float32)
    out[:RC] = rows
    out[LO_ROW:] = rows
    return out


def head_columns(w):
    out = np.zeros((w.shape[0], G, HG, 32), np.float32)
    out[..., ROW_D:ROW_D + HD] = w.reshape(-1, G, HG, HD)
    return out.reshape(w.shape[0], G * P)


def head_rows(w):
    out = np.zeros((G, HG, 32, w.shape[1]), np.float32)
    out[:, :, :HD] = w.reshape(G, HG, HD, -1)
    return out.reshape(G, P, -1).transpose(1, 0, 2)


def attention_layout(inp):
    a = {}
    for n in range(2):
        w = {c: inp[f"L{n}_attn_W{c}"] if n == 0 else inp[f"L{n}_attn_W{c}"].T for c in "qkvo"}
        b = {c: inp[f"L{n}_attn_b{c}"] for c in "qkvo"}
        a[f"wqk{n}"] = np.stack([feature_major(head_columns(w[c])) for c in "qk"], 1)
        a[f"wv{n}"] = feature_major(w["v"])
        a[f"wo{n}"] = head_rows(w["o"])
        rows = np.stack([head_columns(b[c][None])[0].reshape(G, HG, 32) for c in "qk"])
        rows[1, :, :, ROW_M] = 1.0
        if n == 0:
            rows[0, :, :, ROW_A] = 1.0
        a[f"b_col{n}"] = rows.reshape(2 * G, P).T
        a[f"bv{n}"] = np.broadcast_to(b["v"], (P, D))
        a[f"bo{n}"] = b["o"].reshape(KT, P).T
    slope = 2.0 ** (-8.0 / H * np.arange(1, H + 1))
    bias = np.zeros((G, HG, 32, S), np.float32)
    bias[:, :, ROW_A] = np.sqrt(HD) * slope.astype(np.float32).reshape(G, HG, 1) * np.arange(1 - S, 1)
    a["bias_rows"] = bias.reshape(G, P, S).transpose(1, 0, 2)
    ahead = np.arange(P)[None, :] > np.arange(P)[:, None]
    a["masks"] = np.stack([np.eye(P), NEG * ahead, NEG * ahead.T], 1)
    sel = np.zeros((HG, 32, HG, 32), np.float32)
    for j in range(HG):
        sel[j, HD, j] = 1.0
    a["den_sel"] = sel.reshape(P, P)
    a["l_in"] = np.concatenate([inp[f"L1_attn_B{c}"] for c in "qkv"] +
                               [head_rows(inp["L1_attn_Bo"].T).transpose(2, 1, 0).reshape(RANK, G * P)], 1)
    a["l_out"] = np.concatenate([head_columns(inp[f"L1_attn_A{c}"].T) for c in "qk"] + [inp["L1_attn_Av"].T], 1)
    a["l_out_o"] = inp["L1_attn_Ao"].T
    return a


def layout(inp):
    a = {}
    a["x"] = inp["L0_attn_x"].reshape(B, S, KT, P).transpose(3, 0, 2, 1)
    a["mean_w"] = np.full((P, P), 1.0 / D, np.float32)
    a["ident"] = np.eye(P, dtype=np.float32)
    a["tri"] = np.broadcast_to((np.arange(E)[None, :] < np.arange(E)[:, None]).astype(np.float32).reshape(1, -1),
                               (P, E * E))
    gate = [np.concatenate([inp["L0_ffn_exp_wg"].reshape(E * MOE, D), inp["L0_ffn_shared_wg"]])]
    up = [np.concatenate([inp["L0_ffn_exp_wu"].reshape(E * MOE, D), inp["L0_ffn_shared_wu"]])]
    down = [np.concatenate([inp["L0_ffn_exp_wd"].transpose(1, 0, 2).reshape(D, E * MOE), inp["L0_ffn_shared_wd"]], 1)]
    gu = inp["L1_ffn_gate_up_proj"]
    gate.append(np.concatenate([gu[:, :MOE].reshape(E * MOE, D), inp["L1_ffn_sh_gate_w"]]))
    up.append(np.concatenate([gu[:, MOE:].reshape(E * MOE, D), inp["L1_ffn_sh_up_w"]]))
    down.append(np.concatenate([inp["L1_ffn_down_proj"].transpose(1, 0, 2).reshape(D, E * MOE),
                                inp["L1_ffn_sh_down_w"]], 1))
    routers = [inp["L0_ffn_gate_w"], np.concatenate([inp["L1_ffn_router_weight"], inp["L1_ffn_shared_gate_w"]])]
    for n in range(2):
        a[f"ffn{n}"] = ffn_tiles(gate[n], up[n], down[n], n)
        r = np.zeros((D, RC), np.float32)
        r[:, :routers[n].shape[0]] = routers[n].T
        a[f"router{n}"] = feature_major(r)
        a[f"sel{n}"] = selectors(n)
    a.update(attention_layout(inp))
    return {k: np.ascontiguousarray(v, dtype=np.float32) for k, v in a.items()}


def build(nc, shapes, phases):
    aps = {k: nc.dram_tensor(f"in_{k}", s, F32, kind="ExternalInput").ap() for k, s in shapes.items()}
    out = nc.dram_tensor("out_x", (P, B, KT, S), F32, kind="ExternalOutput").ap()
    dram = dict(aps)
    for group in ("ffn", "router", "sel", "wqk", "wv", "wo", "b_col", "bv", "bo"):
        if f"{group}0" in aps or f"{group}1" in aps:
            dram[group] = [aps.get(f"{group}{n}") for n in range(2)]
    program(nc, dram, out, phases)


def kernel(**inputs):
    import concourse.bacc as bacc
    from concourse.bass_utils import run_bass_kernel_spmd

    nc = bacc.Bacc("TRN2", target_bir_lowering=False, num_devices=1)
    arrays = layout({k: np.asarray(v) for k, v in inputs.items()})
    build(nc, {k: v.shape for k, v in arrays.items()}, PHASES)
    r = run_bass_kernel_spmd(nc, [{f"in_{k}": v for k, v in arrays.items()}], core_ids=[0])
    y = np.asarray(r.results[0]["out_x"])
    return np.ascontiguousarray(y.transpose(1, 3, 2, 0).reshape(B, S, D))
```

```python
from contextlib import ExitStack

import numpy as np

import concourse.bass as bass
from concourse import mybir

F32 = mybir.dt.float32
F32R = mybir.dt.float32r
BF16 = mybir.dt.bfloat16
ALU = mybir.AluOpType
ACT = mybir.ActivationFunctionType
AX = mybir.AxisListType

P = 128
D = 256
KT = D // P
B, S = 4, 512
TT = S // P
E = 8
MOE = 176
SHARED = (352, 704)
TILES = tuple(-(-(E * MOE + s) // P) for s in SHARED)
WC = 3 * D
RC = 16
LO_ROW = 32
EPS = 1e-5
RING = 5
EXP_SET = "natural_log_exp_and_others"

H = 16
HD = D // H
G = 4
HG = H // G
ROW_M, ROW_A, ROW_D = 0, 1, 2
ROWS = ROW_D + HD
STACK = 96
RANK = 16
NEG = -1e30
SLOTS = G * TT * HG // 2
LAG = 4
LATE_V = (29, 30, 31)
PROBS = 4
B_UNITS = 2 * TT
LORA_UNITS = 3 * KT + G
A_PROLOGUE = 2 * G + TT * HG + 2 * LAG + TT
PROLOGUE_QK = (4, 8, 16, 20)
A_UNITS = 2 * G + G * TT * HG + TT + KT
QK_SLOTS = (4, 12, 20, 27)
SYNC_STACKED, POOL_STACKED = 16 * 4 * HG, 16 * 2 * HG
MAX_STACKED = 16 * 3

ROUTER_STEPS = (11, 15)


def split3(pe, out, w_hi, w_lo, x_hi, x_lo, start, stop):
    pe.matmul(out, w_hi, x_hi, start=start, stop=False)
    pe.matmul(out, w_hi, x_lo, start=False, stop=False)
    return pe.matmul(out, w_lo, x_hi, start=False, stop=stop)


class Norm:

    def __init__(self, sh, sem):
        self.sh = sh
        self.done = 0
        self.summed = sem("ln_summed")
        self.mean = sem("ln_mean")
        self.centred = sem("ln_centred")
        self.squared = sem("ln_squared")
        self.sq_summed = sem("ln_sq_summed")
        self.var = sem("ln_var")
        self.log = sem("ln_log")
        self.root = sem("ln_root")
        self.root_squared = sem("ln_root_squared")
        self.refined = sem("ln_refined")
        self.rstd = sem("ln_rstd")
        self.normed = sem("ln_normed")
        self.hi = sem("ln_hi")
        self.lo = sem("ln_lo")

    def sum_tiles(self, dve, x):
        dve.tensor_tensor(self.sh.ln_sum[:], x[:, 0, :], x[:, 1, :], ALU.add).then_inc(self.summed, 1)

    def take_mean(self, pe, n):
        pe.wait_ge(self.summed, self.done + n + 1)
        pe.matmul(self.sh.misc[:], self.sh.mean_w[:], self.sh.ln_sum[:], start=True, stop=True).then_inc(self.mean, 1)

    def centre(self, dve, x, n):
        dve.wait_ge(self.mean, self.done + n + 1)
        dve.tensor_tensor(self.sh.ln_x[:, 0, :], x[:, 0, :], self.sh.misc[:], ALU.subtract)
        dve.tensor_tensor(self.sh.ln_x[:, 1, :], x[:, 1, :], self.sh.misc[:],
                          ALU.subtract).then_inc(self.centred, 1)

    def square(self, act, n):
        act.wait_ge(self.centred, self.done + n + 1)
        act.activation(self.sh.ln_sq[:], self.sh.ln_x[:], ACT.Square).then_inc(self.squared, 1)

    def sum_squares(self, dve, n):
        dve.wait_ge(self.squared, self.done + n + 1)
        dve.tensor_tensor(self.sh.ln_sum[:], self.sh.ln_sq[:, 0, :], self.sh.ln_sq[:, 1, :],
                          ALU.add).then_inc(self.sq_summed, 1)

    def take_var(self, pe, n):
        pe.wait_ge(self.sq_summed, self.done + n + 1)
        pe.matmul(self.sh.misc[:], self.sh.mean_w[:], self.sh.ln_sum[:], start=True, stop=True).then_inc(self.var, 1)

    def take_root(self, act, n):
        act.wait_ge(self.var, self.done + n + 1)
        act.activation(self.sh.ln_r[:], self.sh.misc[:], ACT.Ln, bias=self.sh.eps[:, 0:1]).then_inc(self.log, 1)
        act.wait_ge(self.log, self.done + n + 1)
        act.activation(self.sh.ln_r[:], self.sh.ln_r[:], ACT.Exp, scale=-0.5).then_inc(self.root, 1)
        act.wait_ge(self.root, self.done + n + 1)
        act.activation(self.sh.ln_sq[:, 0], self.sh.ln_r[:], ACT.Square).then_inc(self.root_squared, 1)

    def scale(self, dve, n):
        r, r2 = self.sh.ln_r, self.sh.ln_sq[:, 0]
        dve.wait_ge(self.root_squared, self.done + n + 1)
        dve.scalar_tensor_tensor(out=r2, in0=self.sh.misc[:], scalar=EPS, in1=r2, op0=ALU.add,
                                 op1=ALU.mult).then_inc(self.refined, 1)
        dve.wait_ge(self.refined, self.done + n + 1)
        dve.scalar_tensor_tensor(out=r[:], in0=r2, scalar=-3.0, in1=r[:], op0=ALU.add,
                                 op1=ALU.mult).then_inc(self.rstd, 1)
        dve.wait_ge(self.centred, self.done + n + 1)
        dve.wait_ge(self.rstd, self.done + n + 1)
        for kt in range(KT):
            x = self.sh.ln_x[:, kt, :]
            last = dve.scalar_tensor_tensor(out=x, in0=x, scalar=-0.5, in1=r[:], op0=ALU.mult, op1=ALU.mult)
        last.then_inc(self.normed, 1)

    def split_hi(self, act, hi, n):
        act.wait_ge(self.normed, self.done + n + 1)
        act.activation(hi[:], self.sh.ln_x[:], ACT.Copy).then_inc(self.hi, 1)

    def split_lo(self, pool, hi, lo, n):
        pool.wait_ge(self.hi, self.done + n + 1)
        pool.tensor_tensor(lo[:], self.sh.ln_x[:], hi[:].bitcast(F32), ALU.subtract).then_inc(self.lo, 1)


def load_constants(nc, sh, dram, loaded, made):
    with nc.Block() as block:
        @block.sync
        def _(sp):
            for b in range(B):
                sp.dma_start(sh.x[:, b], dram["x"][:, b]).then_inc(loaded, 16)
            sp.dma_start(sh.mean_w[:], dram["mean_w"]).then_inc(loaded, 16)
            sp.dma_start(sh.ident[:], dram["ident"]).then_inc(loaded, 16)
            sp.wait_ge(loaded, 16 * (B + 2))

        @block.vector
        def _(dve):
            dve.memset(sh.eps[:], EPS).then_inc(made, 1)
            dve.wait_ge(made, 1)


def store_output(nc, sh, out, stored):
    with nc.Block() as block:
        @block.sync
        def _(sp):
            for b in range(B):
                sp.dma_start(out[:, b], sh.x[:, b]).then_inc(stored, 16)
            sp.wait_ge(stored, 16 * B)




def ffn_phase(nc, sh, name, layer, dram):
    T = TILES[layer]
    with ExitStack() as ctx:
        def sb(n, shape, dt):
            return ctx.enter_context(nc.sbuf_tensor(f"{name}_{n}", shape, dt))

        def sem(n):
            handle = nc.alloc_semaphore(name=f"{name}_{n}")
            sh.semaphores.append(handle)
            return handle

        raw = sb("raw", [P, RING, WC], F32)
        w_hi = sb("w_hi", [P, T, WC], F32R)
        w_lo = sb("w_lo", [P, T, WC], F32R)
        rw = sb("rw", [P, KT, RC], F32)
        rw_hi = sb("rw_hi", [P, KT, RC], F32R)
        rw_lo = sb("rw_lo", [P, KT, RC], F32R)
        sel = sb("sel", [LO_ROW + RC, T, P], F32R)
        comb_t = [sb(f"comb_t{p}", [LO_ROW + RC, S], F32R) for p in range(2)]
        hidden = sb("hidden", [P, 5, S], F32)
        hidden_flat = hidden[:].rearrange("p a b -> p (a b)")
        act_g = [hidden[:, p] for p in range(2)]
        hid = [hidden[:, 2 + p] for p in range(2)]
        hid_hi = [sb(f"hid_hi{p}", [P, S], F32R) for p in range(2)]
        hid_lo = [sb(f"hid_lo{p}", [P, S], F32R) for p in range(2)]
        x_hi = [sb(f"x_hi{p}", [P, KT, S], F32R) for p in range(2)]
        x_lo = [sb(f"x_lo{p}", [P, KT, S], F32R) for p in range(2)]
        tri = sb("tri", [P, E * E], F32)
        sig = sb("sig", [P, TT, E + 1], F32)
        score = sb("score", [P, TT, E], F32)
        ahead = sb("ahead", [P, TT, E, E], F32)
        tied = sb("tied", [P, TT, E, E], F32)
        col = sb("col", [P, 4, TT], F32)
        comb = sb("comb", [P, TT, RC], F32)
        logits = sb("logits", [P, S], F32)

        sel_raw = hidden_flat[0:LO_ROW + RC, 0:T * P]

        psg = [sh.pair_b[0][:, 0], sh.pair_b[0][:, 1]]
        psu = [sh.pair_b[1][:, 0], sh.pair_b[1][:, 1]]
        psc = sh.bank
        psy = sh.pair_a

        const_loaded = sem("const_loaded")
        const_split = sem("const_split")
        const_set = sem("const_set")
        raw_loaded = [sem(f"raw_loaded{r}") for r in range(RING)]
        w_hi_made = sem("w_hi_made")
        w_split = sem("w_split")
        ln = sh.norm
        logits_t_made = sem("logits_t_made")
        logits_kept = sem("logits_kept")
        logits_made = sem("logits_made")
        neg_exp_made = sem("neg_exp_made")
        shifted = sem("shifted")
        soft_exp_made = sem("soft_exp_made")
        comb_made = sem("comb_made")
        comb_turned = sem("comb_turned")
        comb_hi_made = sem("comb_hi_made")
        comb_split = sem("comb_split")
        router_step = sem("router_step")
        gate_made = sem("gate_made")
        up_made = sem("up_made")
        scale_made = sem("scale_made")
        act_made = sem("act_made")
        up_used = sem("up_used")
        hid_made = sem("hid_made")
        hid_hi_made = sem("hid_hi_made")
        hid_lo_made = sem("hid_lo_made")
        down_made = sem("down_made")
        added = sem("added")

        def chunk_ahead(i, j):
            return 2 * i + 1 if j == 0 else 2 - 2 * i

        with nc.Block() as block:
            @block.sync
            def _(sp):
                sp.dma_start(rw[:], dram["router"][layer]).then_inc(const_loaded, 16)
                sp.dma_start(tri[:], dram["tri"]).then_inc(const_loaded, 16)
                sp.dma_start(sel_raw, dram["sel"][layer]).then_inc(const_loaded, 16)
                for t in range(T):
                    if t >= RING:
                        sp.wait_ge(w_split, t - RING + 1)
                    sp.dma_start(raw[:, t % RING], dram["ffn"][layer][t]).then_inc(raw_loaded[t % RING], 16)

            @block.gpsimd
            def _(pool):
                for t in range(T):
                    pool.wait_ge(w_hi_made, t + 1)
                    pool.tensor_tensor(w_lo[:, t], raw[:, t % RING], w_hi[:, t].bitcast(F32),
                                       ALU.subtract).then_inc(w_split, 1)
                with pool.Fori(0, B // 2) as i:
                    for j in range(2):
                        ln.split_lo(pool, x_hi[1 - j], x_lo[1 - j], 2 * i + j + 1)

            @block.tensor
            def _(pe):
                pe.sem_inc(down_made, 2)

                def router_logits(p, n):
                    pe.wait_ge(ln.lo, ln.done + n + 1)
                    out = sh.misc[0:RC]
                    for k in range(KT):
                        ins = split3(pe, out, rw_hi[:, k], rw_lo[:, k], x_hi[p][:, k], x_lo[p][:, k],
                                     start=(k == 0), stop=(k == KT - 1))
                    ins.then_inc(logits_t_made, 1)

                def turn_logits(n):
                    pe.wait_ge(logits_kept, n + 1)
                    for q in range(TT):
                        c = slice(q * P, (q + 1) * P)
                        ins = pe.transpose(sh.misc[:, c], logits[:, c], sh.ident[:])
                    ins.then_inc(logits_made, 1)

                def turn_comb(n):
                    pe.wait_ge(comb_made, n + 1)
                    for q in range(TT):
                        ins = pe.transpose(sh.misc[0:RC, q * P:(q + 1) * P], comb[:, q, :], sh.ident[:])
                    ins.then_inc(comb_turned, 1)

                def down(i, k):
                    t = k % T
                    pe.wait_ge(hid_hi_made, 2 * T * i + k + 3)
                    pe.wait_ge(hid_lo_made, 2 * T * i + k + 3)
                    if t == 0:
                        pe.wait_ge(added, 2 * i + k // T + 1)
                    for mt in range(KT):
                        cols = slice(2 * D + mt * P, 2 * D + (mt + 1) * P)
                        ins = split3(pe, psy[:, mt], w_hi[:, t, cols], w_lo[:, t, cols], hid_hi[k % 2][:],
                                     hid_lo[k % 2][:], start=(t == 0), stop=(t == T - 1))
                    ins.then_inc(down_made, 1)

                ln.take_mean(pe, 0)
                ln.take_var(pe, 0)
                pe.wait_ge(const_split, 3)
                router_logits(0, 0)
                turn_logits(0)
                with pe.Fori(0, B // 2) as i:
                    for k in range(2 * T):
                        j, t = k // T, k % T
                        if t == 0:
                            pe.wait_ge(ln.lo, ln.done + 2 * i + j + 1)
                        if j == 0:
                            pe.wait_ge(w_split, t + 1)
                        pe.wait_ge(act_made, 2 * T * i + k + 1)
                        for kt in range(KT):
                            c = slice(kt * P, (kt + 1) * P)
                            ins = split3(pe, psg[k % 2], w_hi[:, t, c], w_lo[:, t, c], x_hi[j][:, kt],
                                         x_lo[j][:, kt], start=(kt == 0), stop=(kt == KT - 1))
                        ins.then_inc(gate_made, 1)
                        if t == 0:
                            turn_comb(2 * i + j)
                        pe.wait_ge(up_used, 2 * T * i + k + 1)
                        for kt in range(KT):
                            c = slice(D + kt * P, D + (kt + 1) * P)
                            ins = split3(pe, psu[k % 2], w_hi[:, t, c], w_lo[:, t, c], x_hi[j][:, kt],
                                         x_lo[j][:, kt], start=(kt == 0), stop=(kt == KT - 1))
                        ins.then_inc(up_made, 1)
                        if t == 0:
                            pe.wait_ge(comb_split, 2 * i + j + 1)
                        pe.wait_ge(hid_made, 2 * T * i + k + 2)
                        pe.matmul(psc[:], sel[:, t], comb_t[j][:], start=True, stop=True).then_inc(scale_made, 1)
                        if k >= 2:
                            down(i, k - 2)
                        n = 2 * i + j + 1
                        if t == 2:
                            ln.take_mean(pe, n)
                        if t == 5:
                            ln.take_var(pe, n)
                        if t == 8:
                            router_logits(1 - j, n)
                        if t == 9:
                            turn_logits(n)
                    down(i, 2 * T - 2)
                    down(i, 2 * T - 1)

            @block.scalar
            def _(act):
                act.sem_inc(act_made, 2)
                act.sem_inc(hid_hi_made, 2)

                def keep_logits(n):
                    act.wait_ge(logits_t_made, n + 1)
                    act.activation(logits[0:RC], sh.misc[0:RC], ACT.Copy).then_inc(logits_kept, 1)

                def router_exps(n):
                    act.wait_ge(logits_made, n + 1)
                    act.activation(sig[:], sh.misc[:].rearrange("p (q c) -> p q c", c=P)[:, :, 0:E + 1],
                                   ACT.Exp, scale=-1.0).then_inc(neg_exp_made, 1)
                    if layer == 1:
                        act.wait_ge(shifted, n + 1)
                        act.activation(score[:], score[:], ACT.Exp).then_inc(soft_exp_made, 1)

                def split_hid(i, k):
                    act.wait_ge(hid_made, 2 * T * i + k + 3)
                    act.wait_ge(down_made, 2 * T * i + k + 1)
                    act.activation(hid_hi[k % 2][:], hid[k % 2], ACT.Copy).then_inc(hid_hi_made, 1)

                def weights_hi(first, last):
                    for t in range(first, last):
                        act.wait_ge(raw_loaded[t % RING], 16 * (t // RING + 1))
                        act.activation(w_hi[:, t], raw[:, t % RING], ACT.Copy).then_inc(w_hi_made, 1)

                act.preload_act_table_set(EXP_SET)
                weights_hi(0, 2)
                ln.square(act, 0)
                weights_hi(2, 4)
                ln.take_root(act, 0)
                weights_hi(4, 6)
                ln.split_hi(act, x_hi[0], 0)
                weights_hi(6, 7)
                keep_logits(0)
                weights_hi(7, 8)
                router_exps(0)
                weights_hi(8, T)
                with act.Fori(0, B // 2) as i:
                    for k in range(2 * T):
                        j, t = k // T, k % T
                        act.wait_ge(gate_made, 2 * T * i + k + 1)
                        act.wait_ge(hid_made, 2 * T * i + k + 1)
                        act.activation(act_g[k % 2], psg[k % 2], ACT.Silu).then_inc(act_made, 1)
                        if k >= 1:
                            split_hid(i, k - 1)
                        n = 2 * i + j + 1
                        if t == 3:
                            ln.square(act, n)
                        if t == 6:
                            act.preload_act_table_set(EXP_SET)
                            ln.take_root(act, n)
                        if t == 7:
                            ln.split_hi(act, x_hi[1 - j], n)
                        if t == 8:
                            keep_logits(n)
                        if t == 10:
                            act.preload_act_table_set(EXP_SET)
                            router_exps(n)
                    split_hid(i, 2 * T - 1)

            @block.vector
            def _(dve):
                dve.sem_inc(up_used, 2)
                dve.sem_inc(hid_made, 2)
                dve.sem_inc(hid_lo_made, 2)
                dve.sem_inc(added, 1)

                def router(n):
                    steps = [0]

                    def link(ins):
                        ins.then_inc(router_step, 1)
                        steps[0] += 1
                        dve.wait_ge(router_step, n * ROUTER_STEPS[layer] + steps[0])

                    lg = sh.misc[:].rearrange("p (q c) -> p q c", c=P)[:, :, 0:E]
                    dve.wait_ge(neg_exp_made, n + 1)
                    link(dve.tensor_scalar(sig[:], sig[:], 1.0, None, ALU.add))
                    link(dve.reciprocal(sig[:], sig[:]))
                    if layer == 1:
                        link(dve.tensor_reduce(col[:, 0], lg, AX.X, ALU.max))
                        dve.tensor_tensor(score[:], lg, col[:, 0].unsqueeze(2).to_broadcast([P, TT, E]),
                                          ALU.subtract).then_inc(shifted, 1)
                        dve.wait_ge(soft_exp_made, n + 1)
                        link(dve.tensor_reduce(col[:, 1], score[:], AX.X, ALU.add))
                        link(dve.reciprocal(col[:, 1], col[:, 1]))
                        link(dve.tensor_tensor(score[:], score[:], col[:, 1].unsqueeze(2).to_broadcast([P, TT, E]),
                                               ALU.mult))
                        sc = score[:]
                    else:
                        sc = sig[:, :, 0:E]
                    mine = sc.unsqueeze(3).to_broadcast([P, TT, E, E])
                    other = sc.unsqueeze(2).to_broadcast([P, TT, E, E])
                    tri4 = tri[:].rearrange("p (a b) -> p a b", a=E)
                    link(dve.tensor_tensor(ahead[:], other, mine, ALU.is_gt))
                    link(dve.tensor_tensor(tied[:], other, mine, ALU.is_equal))
                    for q in range(TT):
                        last = dve.tensor_tensor(tied[:, q], tied[:, q], tri4, ALU.mult)
                    link(last)
                    link(dve.tensor_tensor(ahead[:], ahead[:], tied[:], ALU.add))
                    link(dve.tensor_reduce(tied[:, :, :, 0], ahead[:], AX.X, ALU.add))
                    link(dve.scalar_tensor_tensor(out=comb[:, :, 0:E], in0=tied[:, :, :, 0], scalar=2.0, in1=sc,
                                                  op0=ALU.is_lt, op1=ALU.mult))
                    if layer == 1:
                        link(dve.tensor_reduce(col[:, 2], comb[:, :, 0:E], AX.X, ALU.add))
                        link(dve.reciprocal(col[:, 3], col[:, 2]))
                        link(dve.tensor_copy(comb[:, :, E:E + 1], sig[:, :, E:E + 1]))
                        gain = 1.0
                    else:
                        link(dve.tensor_reduce(col[:, 2], comb[:, :, 0:E], AX.X, ALU.add))
                        link(dve.tensor_scalar(col[:, 2], col[:, 2], 1e-20, None, ALU.add))
                        link(dve.reciprocal(col[:, 3], col[:, 2]))
                        gain = 2.5
                    dve.scalar_tensor_tensor(out=comb[:, :, 0:E], in0=comb[:, :, 0:E], scalar=gain,
                                             in1=col[:, 3].unsqueeze(2).to_broadcast([P, TT, E]), op0=ALU.mult,
                                             op1=ALU.mult).then_inc(comb_made, 1)
                    assert steps[0] == ROUTER_STEPS[layer], steps[0]

                def split_comb(p, n):
                    dve.wait_ge(comb_turned, n + 1)
                    dve.tensor_copy(comb_t[p][0:RC], sh.misc[0:RC]).then_inc(comb_hi_made, 1)
                    dve.wait_ge(comb_hi_made, n + 1)
                    dve.tensor_tensor(comb_t[p][LO_ROW:LO_ROW + RC], sh.misc[0:RC], comb_t[p][0:RC].bitcast(F32),
                                      ALU.subtract).then_inc(comb_split, 1)

                def split_hid(i, k):
                    dve.wait_ge(hid_hi_made, 2 * T * i + k + 3)
                    dve.wait_ge(down_made, 2 * T * i + k + 1)
                    dve.tensor_tensor(hid_lo[k % 2][:], hid[k % 2], hid_hi[k % 2][:].bitcast(F32),
                                      ALU.subtract).then_inc(hid_lo_made, 1)

                def add_output(i, j):
                    dve.wait_ge(down_made, 2 * T * i + (j + 1) * T + 2)
                    xc = sh.x[:, 2 * i + j]
                    dve.scalar_tensor_tensor(out=xc, in0=psy[:], scalar=0.5, in1=xc, op0=ALU.mult,
                                             op1=ALU.add).then_inc(added, 1)

                ln.sum_tiles(dve, sh.x[:, 0])
                dve.wait_ge(const_loaded, 48)
                dve.tensor_copy(rw_hi[:], rw[:]).then_inc(const_split, 1)
                ln.centre(dve, sh.x[:, 0], 0)
                dve.tensor_copy(sel[:].rearrange("p t c -> p (t c)"), sel_raw).then_inc(const_split, 1)
                ln.sum_squares(dve, 0)
                dve.wait_ge(const_split, 2)
                dve.tensor_tensor(rw_lo[:], rw[:], rw_hi[:].bitcast(F32), ALU.subtract).then_inc(const_split, 1)
                ln.scale(dve, 0)
                dve.memset(comb_t[0][:].bitcast(F32), 0.0).then_inc(const_set, 1)
                dve.memset(comb_t[1][:].bitcast(F32), 0.0).then_inc(const_set, 1)
                dve.memset(comb[:], 0.0).then_inc(const_set, 1)
                dve.memset(logits[:], 0.0).then_inc(const_set, 1)
                dve.wait_ge(const_set, 4)
                dve.memset(comb[:, :, E:E + 1], 1.0).then_inc(const_set, 1)
                dve.wait_ge(const_set, 5)
                ln.split_lo(dve, x_hi[0], x_lo[0], 0)
                router(0)
                with dve.Fori(0, B // 2) as i:
                    for k in range(2 * T):
                        j, t = k // T, k % T
                        if k == T + 2:
                            add_output(i, 0)
                        if k == T + 1:
                            dve.wait_ge(added, i + 1)
                        if t == 0:
                            split_comb(j, 2 * i + j)
                        dve.wait_ge(act_made, 2 * T * i + k + 3)
                        dve.wait_ge(up_made, 2 * T * i + k + 1)
                        dve.tensor_tensor(act_g[k % 2], act_g[k % 2], psu[k % 2],
                                          ALU.mult).then_inc(up_used, 1)
                        dve.wait_ge(up_used, 2 * T * i + k + 3)
                        dve.wait_ge(scale_made, 2 * T * i + k + 1)
                        dve.wait_ge(hid_hi_made, 2 * T * i + k + 1)
                        dve.wait_ge(hid_lo_made, 2 * T * i + k + 1)
                        dve.tensor_tensor(hid[k % 2], act_g[k % 2], psc[:], ALU.mult).then_inc(hid_made, 1)
                        if k >= 1:
                            split_hid(i, k - 1)
                        n = 2 * i + j + 1
                        xn = sh.x[:, chunk_ahead(i, j)]
                        if t == 1:
                            ln.sum_tiles(dve, xn)
                        if t == 3:
                            ln.centre(dve, xn, n)
                        if t == 4:
                            ln.sum_squares(dve, n)
                        if t == 6:
                            ln.scale(dve, n)
                        if t == 10:
                            router(n)
                    split_hid(i, 2 * T - 1)
                    add_output(i, 1)




def attention_phase(nc, sh, name, layer, dram):
    causal = layer == 0
    lora = layer == 1
    with ExitStack() as ctx:
        def sb(n, shape, dt):
            return ctx.enter_context(nc.sbuf_tensor(f"{name}_{n}", shape, dt))

        def sem(n):
            handle = nc.alloc_semaphore(name=f"{name}_{n}")
            sh.semaphores.append(handle)
            return handle

        wqk_hi = sb("wqk_hi", [P, 2, KT, G * P], F32R)
        wqk_lo = sb("wqk_lo", [P, 2, KT, G * P], F32R)
        wv_hi = sb("wv_hi", [P, KT, D], F32R)
        wv_lo = sb("wv_lo", [P, KT, D], F32R)
        wo = sb("wo", [P, G, D], F32)
        b_col = sb("b_col", [P, 2 * G], F32)
        bv = sb("bv", [P, D], F32)
        bo = sb("bo", [P, KT], F32)
        den_sel = sb("den_sel", [P, P], F32)
        if causal:
            bias_rows = sb("bias_rows", [P, G, S], F32)
            mask_in = sb("mask_in", [P, 3, P], F32)
            mask = sb("mask", [P, 3, P], BF16)
        x_hi = sb("x_hi", [P, KT, S], F32R)
        x_lo = sb("x_lo", [P, KT, S], F32R)
        qk = [sb(f"{n}_all", [P, S], F32) for n in "qk"]
        qk_hi = sb("qk_hi", [P, 2, 2, S], F32R)
        qk_lo = sb("qk_lo", [P, 2, 2, S], F32R)
        stack = [sb(f"{n}_stack", [STACK, G, HG, S], F32R) for n in "qk"]
        neg_max = sb("neg_max", [P, 2, TT, HG], F32)
        max_hi = sb("max_hi", [HG, S], F32R)
        max_lo = sb("max_lo", [HG, S], F32R)
        probs = sb("probs", [P, PROBS, 2, S], F32)
        v_one = sb("v_one", [P, TT, H, 32], F32)
        heads = sb("heads", [P, S], F32)
        rden = sb("rden", [P, S], F32)
        context = sb("context", [P, G, S], F32)

        flat = probs[:].rearrange("p a b c -> p (a b c)")
        wqk = flat[:, 0:4 * G * P].rearrange("p (w k c) -> p w k c", w=2, k=KT)
        wv = flat[:, 4 * G * P:4 * G * P + KT * D].rearrange("p (k c) -> p k c", k=KT)
        l_in = context[0:RANK].rearrange("p a b -> p (a b)")[:, 0:3 * D + G * P]
        l_out = flat[0:RANK, 4 * G * P + KT * D:4 * G * P + KT * D + 2 * G * P + D]
        l_out_o = rden[0:RANK, 0:D]

        ps_a = [sh.pair_a[:, 0], sh.pair_a[:, 1]]
        ps_b = sh.pair_b
        ps_o = sh.bank
        misc = sh.misc

        loaded = sem("loaded")
        w_hi_made = sem("w_hi_made")
        w_split = sem("w_split")
        set_up = sem("set_up")
        ln = sh.norm
        a_full = sem("a_full")
        a_taken = sem("a_taken")
        qk_hi_made = sem("qk_hi_made")
        qk_lo_made = sem("qk_lo_made")
        parts_ready = sem("parts_ready")
        sync_stacked = [sem(f"sync_stacked{p}") for p in range(2)]
        pool_stacked = [sem(f"pool_stacked{p}") for p in range(2)]
        max_stacked = sem("max_stacked")
        max_turned = sem("max_turned")
        max_hi_made = sem("max_hi_made")
        max_lo_made = sem("max_lo_made")
        b_full = sem("b_full")
        b_taken = sem("b_taken")
        pv_made = sem("pv_made")
        heads_kept = sem("heads_kept")
        den_made = sem("den_made")
        den_log = sem("den_log")
        rden_made = sem("rden_made")
        context_made = sem("context_made")

        def k_end(q):
            return (q + 1) * P if causal else S

        def q_start(k):
            return k * P if causal else 0

        n_loads = 9 if causal else 10
        before = LORA_UNITS if lora else 0
        base = before + A_PROLOGUE

        def qk_ahead(t):
            return sum(min(max(t + 1 - at, 0), 2) for at in QK_SLOTS)

        def qk_part(t):
            for g, at in enumerate(QK_SLOTS):
                if at <= t < at + 2:
                    return 2 * g + t - at
            return None

        def stack_group(eng, which, rows, g, done):
            for row in rows:
                src = {0: qk_hi, 32: (qk_hi, qk_lo)[which], 64: (qk_lo, qk_hi)[which]}[row]
                for j in range(HG):
                    eng.dma_start(stack[which][row:row + ROWS, g, j].bitcast(F32),
                                  src[32 * j:32 * j + ROWS, which, g % 2].bitcast(F32)).then_inc(done, 16)

        with nc.Block() as block:
            @block.sync
            def _(sp):
                for dst, src in ((wqk, "wqk"), (wv, "wv"), (wo[:], "wo"), (b_col[:], "b_col"), (bv[:], "bv"),
                                 (bo[:], "bo")):
                    sp.dma_start(dst, dram[src][layer]).then_inc(loaded, 16)
                sp.dma_start(den_sel[:], dram["den_sel"]).then_inc(loaded, 16)
                if causal:
                    sp.dma_start(bias_rows[:], dram["bias_rows"]).then_inc(loaded, 16)
                    sp.dma_start(mask_in[:], dram["masks"]).then_inc(loaded, 16)
                if lora:
                    for dst, src in ((l_in, "l_in"), (l_out, "l_out"), (l_out_o, "l_out_o")):
                        sp.dma_start(dst, dram[src]).then_inc(loaded, 16)
                sp.wait_ge(set_up, 2)

                def stack_qk(g, groups):
                    sp.wait_ge(parts_ready, groups)
                    stack_group(sp, 1, (0,), g, sync_stacked[g % 2])
                    stack_group(sp, 0, (0, 32, 64), g, sync_stacked[g % 2])

                def stack_max(m, g):
                    sp.wait_ge(max_lo_made, m + 1)
                    for row, src in ((0, max_hi), (32, max_hi), (64, max_lo)):
                        sp.dma_start(stack[0][row:row + 1, g].bitcast(F32), src[:].bitcast(F32)
                                     ).then_inc(max_stacked, 16)

                def chunk(b, last):
                    for g in range(G):
                        if g + 1 < G or not last:
                            stack_max(G * b + g + 1, (g + 1) % G)
                        if not last:
                            stack_qk(g, G * b + G + g + 1)

                stack_qk(0, 1)
                stack_qk(1, 2)
                stack_max(0, 0)
                stack_qk(2, 3)
                stack_qk(3, 4)
                with sp.Fori(0, B - 1) as b:
                    chunk(b, False)
                chunk(B - 1, True)

            @block.gpsimd
            def _(pool):
                pool.sem_inc(qk_lo_made, 2)
                for which in range(2):
                    pool.memset(stack[which][:].bitcast(F32), 0.0).then_inc(set_up, 1)

                def split_lo(b, n):
                    which = n % 2
                    pool.wait_ge(qk_hi_made, 2 * G * b + n + 3)
                    pool.tensor_tensor(qk_lo[:, which, n // 2 % 2], qk[which][:],
                                       qk_hi[:, which, n // 2 % 2].bitcast(F32),
                                       ALU.subtract).then_inc(qk_lo_made, 1)

                def stack_k(g, made):
                    pool.wait_ge(qk_lo_made, made)
                    pool.sem_inc(parts_ready, 1)
                    stack_group(pool, 1, (32, 64), g, pool_stacked[g % 2])

                pool.wait_ge(set_up, 2)
                for g in range(G):
                    split_lo(0, 2 * g)
                    split_lo(0, 2 * g + 1)
                    stack_k(g, 2 * g + 4)
                with pool.Fori(0, B - 1) as b:
                    for g in range(G):
                        split_lo(b + 1, 2 * g)
                        pool.wait_ge(b_full, B_UNITS * G * b + B_UNITS * (g + 1))
                        split_lo(b + 1, 2 * g + 1)
                        stack_k(g, 2 * G * b + 2 * G + 2 * g + 4)

            @block.tensor
            def _(pe):
                pe.sem_inc(pv_made, 2)

                def use_a(unit):
                    pe.wait_ge(a_taken, unit + 1)

                def project(unit, n, parity):
                    g, which = n // 2, n % 2
                    use_a(unit)
                    c = slice(g * P, (g + 1) * P)
                    for kt in range(KT):
                        ins = split3(pe, ps_a[parity], wqk_hi[:, which, kt, c], wqk_lo[:, which, kt, c],
                                     x_hi[:, kt], x_lo[:, kt], start=(kt == 0), stop=(kt == KT - 1))
                    ins.then_inc(a_full, 1)

                def project_v(unit, q, parity):
                    use_a(unit)
                    t = slice(q * P, (q + 1) * P)
                    for kt in range(KT):
                        ins = split3(pe, ps_a[parity][:, 0:D], x_hi[:, kt, t], x_lo[:, kt, t], wv_hi[:, kt],
                                     wv_lo[:, kt], start=(kt == 0), stop=(kt == KT - 1))
                    ins.then_inc(a_full, 1)

                def max_scores(unit, g, n, parity):
                    q, j = n // HG, n % HG
                    use_a(unit)
                    out = ps_a[parity]
                    end = k_end(q)
                    ins = pe.matmul(out[:, 0:end], stack[0][:, g, j, q * P:(q + 1) * P], stack[1][:, g, j, 0:end],
                                    start=True, stop=not causal)
                    if causal:
                        ins = pe.matmul(out[:, q * P:end], mask[:, 0], mask[:, 1], start=False, stop=True)
                    ins.then_inc(a_full, 1)

                def scores(m, g, u):
                    k, pair = u // 2, u % 2
                    pe.wait_ge(b_taken, B_UNITS * m + u + 1)
                    lo = q_start(k)
                    for half in range(2):
                        j = 2 * pair + half
                        out = ps_b[u % 2][:, half]
                        ins = pe.matmul(out[:, lo:S], stack[1][:, g, j, k * P:(k + 1) * P],
                                        stack[0][:, g, j, lo:S], start=True, stop=not causal)
                        if causal:
                            ins = pe.matmul(out[:, lo:lo + P], mask[:, 0], mask[:, 2], start=False, stop=True)
                    ins.then_inc(b_full, 1)

                def attend(m, g, k):
                    pe.wait_ge(b_taken, B_UNITS * m + 2 * k + 4)
                    if k == 0:
                        pe.wait_ge(heads_kept, m + 1)
                    lo = q_start(k)
                    for j in range(HG):
                        ins = pe.matmul(ps_o[32 * j:32 * (j + 1), lo:S], v_one[:, k, HG * g + j],
                                        probs[:, (2 * k + j // 2) % PROBS, j % 2, lo:S], start=(k == 0),
                                        stop=(k == TT - 1), tile_position=(0, 32 * j), skip_group_check=True)
                    ins.then_inc(pv_made, 1)

                def turn_max(m, side, last_unit):
                    pe.wait_ge(a_taken, last_unit + 3)
                    for q in range(TT):
                        ins = pe.transpose(misc[0:HG, q * P:(q + 1) * P], neg_max[:, side, q], sh.ident[:])
                    ins.then_inc(max_turned, 1)

                def spread_den(m, alone):
                    pe.wait_ge(heads_kept, m + 2)
                    if alone:
                        pe.wait_ge(den_log, m + 1)
                    else:
                        pe.wait_ge(max_hi_made, m + 2)
                        pe.wait_ge(max_lo_made, m + 2)
                    pe.matmul(misc[:], den_sel[:], heads[:], start=True, stop=True).then_inc(den_made, 1)

                def output(parity, mt, b, groups):
                    for g in groups:
                        pe.wait_ge(context_made, G * b + g + 2)
                        ins = pe.matmul(ps_a[parity], wo[:, g, mt * P:(mt + 1) * P], context[:, g], start=(g == 0),
                                        stop=(g == G - 1))
                    return ins

                ln.take_mean(pe, 0)
                ln.take_var(pe, 0)
                pe.wait_ge(loaded, 16 * n_loads)
                if lora:
                    for unit in range(LORA_UNITS):
                        use_a(unit)
                        n, kt = unit // KT, unit % KT
                        if n < 3:
                            lhs = l_in[:, n * D + kt * P:n * D + (kt + 1) * P]
                            rhs = l_out[:, n * G * P:n * G * P + (G * P if n < 2 else D)]
                        else:
                            g = unit - 3 * KT
                            lhs = l_in[:, 3 * D + g * P:3 * D + (g + 1) * P]
                            rhs = l_out_o
                        pe.matmul(ps_a[unit % 2][:, 0:rhs.shape[-1]], lhs, rhs, start=True,
                                  stop=True).then_inc(a_full, 1)
                pe.wait_ge(w_split, 3)
                pe.wait_ge(ln.lo, ln.done + 1)
                unit = before
                for n in range(4):
                    project(unit, n, unit % 2)
                    unit += 1
                for q in range(TT):
                    project_v(unit, q, unit % 2)
                    unit += 1
                pe.wait_ge(ln.refined, ln.done + 1)
                ln.take_mean(pe, 1)
                ln.take_var(pe, 1)
                pe.wait_ge(sync_stacked[0], SYNC_STACKED)
                pe.wait_ge(pool_stacked[0], POOL_STACKED)
                for n in range(TT * HG + 2 * LAG):
                    if n == TT * HG:
                        pe.wait_ge(sync_stacked[1], SYNC_STACKED)
                        pe.wait_ge(pool_stacked[1], POOL_STACKED)
                    max_scores(unit, n // 16, n % 16, unit % 2)
                    unit += 1
                    if n + 1 in PROLOGUE_QK:
                        project(unit, 4 + PROLOGUE_QK.index(n + 1), unit % 2)
                        unit += 1
                    if n == TT * HG + 1:
                        pe.wait_ge(ln.refined, ln.done + 2)
                        turn_max(0, 0, before + 4 + TT + TT * HG - 1 + 2)
                assert unit == base and base % 2 == 0 and A_UNITS % 2 == 0

                def chunk(b, ahead, last):
                    count = [0]

                    def next_a():
                        count[0] += 1
                        return base + A_UNITS * b + count[0] - 1, (count[0] - 1) % 2

                    m = G * b
                    end = SLOTS - 8 - LAG if last else SLOTS
                    for t in range(SLOTS):
                        if not last and qk_part(t) is not None:
                            if qk_part(t) == 0:
                                pe.wait_ge(ln.lo, ln.done + b + 2)
                            unit, parity = next_a()
                            project(unit, qk_part(t), parity)
                        g, u = (t + LAG) // 8 + 1, (t + LAG) % 8
                        if t < end:
                            if u == 0:
                                p, here, each = g % 2, g // 2 + 1, G // 2
                                pe.wait_ge(sync_stacked[p], each * SYNC_STACKED * b + here * SYNC_STACKED)
                                pe.wait_ge(pool_stacked[p], each * POOL_STACKED * b + here * POOL_STACKED)
                            unit, parity = next_a()
                            max_scores(unit, g % G, 2 * u, parity)
                        if t % 8 == 0:
                            pe.wait_ge(max_stacked, MAX_STACKED * (m + t // 8 + 1))
                        scores(m + t // 8, t // 8, t % 8)
                        if t < end:
                            unit, parity = next_a()
                            max_scores(unit, g % G, 2 * u + 1, parity)
                        k = (t - 3) // 2
                        if t % 2 == 1 and k >= 0:
                            attend(m + k // TT, k // TT, k % TT)
                        if t in (6, 14) and ahead:
                            pe.wait_ge(max_hi_made, m + t // 8 + 2)
                            pe.wait_ge(max_lo_made, m + t // 8 + 2)
                            if t == 6:
                                ln.take_mean(pe, b + 2)
                            else:
                                ln.take_var(pe, b + 2)
                        if t % 8 == 3 and t >= 11:
                            if t == 11 and ahead:
                                pe.wait_ge(ln.centred, ln.done + b + 3)
                            if t == 19 and ahead:
                                pe.wait_ge(ln.refined, ln.done + b + 3)
                            spread_den(m + t // 8 - 1, False)
                        if t % 8 == LAG and t <= end:
                            g = t // 8 + 1
                            pe.wait_ge(max_hi_made, m + g)
                            pe.wait_ge(max_lo_made, m + g)
                            pe.wait_ge(den_log, m + g)
                            turn_max(m + g, g % 2, base + A_UNITS * b + 2 * t - 1
                                     + (0 if last else qk_ahead(t - 1)))
                        if t in LATE_V and not last:
                            unit, parity = next_a()
                            project_v(unit, LATE_V.index(t), parity)
                    attend(m + G - 1, G - 1, TT - 1)
                    if not last:
                        unit, parity = next_a()
                        project_v(unit, TT - 1, parity)
                    spread_den(m + G - 1, last)
                    (unit0, parity0), (unit1, parity1) = next_a(), next_a()
                    use_a(unit0)
                    use_a(unit1)
                    output(parity0, 0, b, range(G - 1))
                    output(parity1, 1, b, range(G - 1))
                    output(parity0, 0, b, (G - 1,)).then_inc(a_full, 1)
                    output(parity1, 1, b, (G - 1,)).then_inc(a_full, 1)

                with pe.Fori(0, B - 2) as b:
                    chunk(b, True, False)
                chunk(B - 2, False, False)
                chunk(B - 1, False, True)

            @block.scalar
            def _(act):
                act.sem_inc(b_taken, 2)
                act.sem_inc(heads_kept, 1)
                act.sem_inc(den_log, 1)
                act.sem_inc(qk_hi_made, 2)
                act.preload_act_table_set(EXP_SET)
                ln.square(act, 0)
                ln.take_root(act, 0)
                ln.split_hi(act, x_hi, 0)
                act.wait_ge(loaded, 16 * n_loads)
                if lora:
                    act.wait_ge(a_taken, LORA_UNITS + 2)
                act.activation(wqk_hi[:, 0], wqk[:, 0], ACT.Copy).then_inc(w_hi_made, 1)
                act.activation(wqk_hi[:, 1], wqk[:, 1], ACT.Copy).then_inc(w_hi_made, 1)
                act.activation(wv_hi[:], wv, ACT.Copy).then_inc(w_hi_made, 1)

                def split_hi(b, n, unit):
                    which = n % 2
                    act.wait_ge(a_taken, unit + 3)
                    act.activation(qk_hi[:, which, n // 2 % 2], qk[which][:], ACT.Copy).then_inc(qk_hi_made, 1)

                def keep_max(m):
                    act.wait_ge(max_turned, m + 1)
                    act.activation(max_hi[:], misc[0:HG], ACT.Copy).then_inc(max_hi_made, 1)

                def exps(m, u):
                    k = u // 2
                    lo = q_start(k)
                    act.wait_ge(b_full, B_UNITS * m + u + 1)
                    act.wait_ge(pv_made, TT * m + (u - PROBS) // 2 + 3)
                    act.activation(probs[:, u % PROBS, :, lo:S], ps_b[u % 2][:, :, lo:S], ACT.Exp,
                                   scale=float(HD) ** -0.5).then_inc(b_taken, 1)

                def keep_heads(m):
                    act.wait_ge(pv_made, TT * m + TT + 2)
                    act.wait_ge(context_made, m + 1)
                    act.activation(heads[:], ps_o[:], ACT.Copy).then_inc(heads_kept, 1)

                def invert_den(m):
                    act.wait_ge(den_made, m + 1)
                    act.activation(rden[:], misc[:], ACT.Ln).then_inc(den_log, 1)
                    act.wait_ge(den_log, m + 2)
                    act.activation(rden[:], rden[:], ACT.Exp, scale=-1.0).then_inc(rden_made, 1)

                for n in range(4):
                    split_hi(0, n, before + n)
                ln.square(act, 1)
                ln.take_root(act, 1)
                for n in range(4, 2 * G):
                    if n % 2 == 0:
                        act.wait_ge(sync_stacked[n // 2 % 2], SYNC_STACKED * (n // 4))
                        act.wait_ge(pool_stacked[n // 2 % 2], POOL_STACKED * (n // 4))
                    split_hi(0, n, before + TT + n + PROLOGUE_QK[n - 4])
                    if n == 6:
                        keep_max(0)

                def chunk(b, ahead, last):
                    m = G * b
                    for t in range(SLOTS):
                        n = None if last else qk_part(t)
                        if n is not None:
                            if n % 2 == 0:
                                p, here, each = n // 2 % 2, n // 4 + G // 2, G // 2
                                act.wait_ge(sync_stacked[p], each * SYNC_STACKED * b + here * SYNC_STACKED)
                                act.wait_ge(pool_stacked[p], each * POOL_STACKED * b + here * POOL_STACKED)
                            split_hi(b + 1, n, base + A_UNITS * b + 2 * t + qk_ahead(t) - 1)
                        exps(m + t // 8, t % 8)
                        if t == 0 and not last:
                            act.wait_ge(a_full, base + A_UNITS * b - KT)
                            ln.split_hi(act, x_hi, b + 1)
                        if ahead:
                            if t == 8:
                                ln.square(act, b + 2)
                            if t == 15:
                                ln.take_root(act, b + 2)
                        if t % 8 == LAG and t <= (SLOTS - 8 - LAG if last else SLOTS):
                            act.wait_ge(max_stacked, MAX_STACKED * (m + t // 8 + 1))
                            keep_max(m + t // 8 + 1)
                        if t % 8 == 2 and t >= 10:
                            keep_heads(m + t // 8 - 1)
                        if t % 8 == 3 and t >= 11:
                            invert_den(m + t // 8 - 1)
                    keep_heads(m + G - 1)
                    invert_den(m + G - 1)

                with act.Fori(0, B - 2) as b:
                    chunk(b, True, False)
                chunk(B - 2, False, False)
                chunk(B - 1, False, True)

            @block.vector
            def _(dve):
                dve.sem_inc(a_taken, 2)
                dve.sem_inc(context_made, 1)
                ln.sum_tiles(dve, sh.x[:, 0])
                dve.memset(v_one[:, :, :, HD:32], 1.0)
                ln.centre(dve, sh.x[:, 0], 0)
                ln.sum_squares(dve, 0)
                ln.scale(dve, 0)
                ln.split_lo(dve, x_hi, x_lo, 0)
                dve.wait_ge(loaded, 16 * n_loads)
                if causal:
                    dve.tensor_copy(mask[:], mask_in[:]).then_inc(set_up, 1)
                if lora:
                    targets = [wqk[:, n, kt] for n in range(2) for kt in range(KT)]
                    targets += [wv[:, kt] for kt in range(KT)] + [wo[:, g] for g in range(G)]
                    for unit, w in enumerate(targets):
                        dve.wait_ge(a_full, unit + 1)
                        dve.scalar_tensor_tensor(out=w, in0=ps_a[unit % 2][:, 0:w.shape[-1]], scalar=0.5, in1=w,
                                                 op0=ALU.mult, op1=ALU.add).then_inc(a_taken, 1)
                for n, (lo, hi, w) in enumerate(((wqk_lo[:, 0], wqk_hi[:, 0], wqk[:, 0]),
                                                 (wqk_lo[:, 1], wqk_hi[:, 1], wqk[:, 1]), (wv_lo[:], wv_hi[:], wv))):
                    dve.wait_ge(w_hi_made, n + 1)
                    dve.tensor_tensor(lo, w, hi.bitcast(F32), ALU.subtract).then_inc(w_split, 1)

                def keep_qk(b, unit, parity, n):
                    g, which = n // 2, n % 2
                    dve.wait_ge(a_full, unit + 1)
                    dve.wait_ge(qk_hi_made, 2 * G * b + n + 1)
                    dve.wait_ge(qk_lo_made, 2 * G * b + n + 1)
                    bias = b_col[:, G * which + g:G * which + g + 1]
                    if which == 1 and causal:
                        dve.scalar_tensor_tensor(out=qk[1][:], in0=ps_a[parity], scalar=bias, in1=bias_rows[:, g],
                                                 op0=ALU.add, op1=ALU.add).then_inc(a_taken, 1)
                    else:
                        dve.tensor_scalar(qk[which][:], ps_a[parity], bias, None, ALU.add).then_inc(a_taken, 1)

                def take_max(unit, parity, side, n):
                    q, j = n // HG, n % HG
                    dve.wait_ge(a_full, unit + 1)
                    dve.tensor_reduce(neg_max[:, side, q, j:j + 1], ps_a[parity][:, 0:k_end(q)], AX.X, ALU.max,
                                      negate=True).then_inc(a_taken, 1)

                def split_max(m):
                    dve.wait_ge(max_hi_made, m + 1)
                    dve.tensor_tensor(max_lo[:], misc[0:HG], max_hi[:].bitcast(F32),
                                      ALU.subtract).then_inc(max_lo_made, 1)

                def keep_v(unit, parity, q):
                    dve.wait_ge(a_full, unit + 1)
                    dve.tensor_tensor(v_one[:, q, :, 0:HD], ps_a[parity][:, 0:D].rearrange("p (h c) -> p h c", h=H),
                                      bv[:].rearrange("p (h c) -> p h c", h=H), ALU.add).then_inc(a_taken, 1)

                def make_context(m, g):
                    dve.wait_ge(rden_made, m + 1)
                    dve.tensor_tensor(context[:, g], heads[:], rden[:], ALU.mult).then_inc(context_made, 1)

                unit = before
                for n in range(4):
                    keep_qk(0, unit, unit % 2, n)
                    unit += 1
                for q in range(TT):
                    keep_v(unit, unit % 2, q)
                    unit += 1
                ln.sum_tiles(dve, sh.x[:, 1])
                ln.centre(dve, sh.x[:, 1], 1)
                ln.sum_squares(dve, 1)
                ln.scale(dve, 1)
                for n in range(TT * HG + 2 * LAG):
                    take_max(unit, unit % 2, n // 16, n % 16)
                    unit += 1
                    if n + 1 in PROLOGUE_QK:
                        keep_qk(0, unit, unit % 2, 4 + PROLOGUE_QK.index(n + 1))
                        unit += 1
                    if n == TT * HG + 3:
                        split_max(0)

                def chunk(b, ahead, last):
                    count = [0]

                    def next_a():
                        count[0] += 1
                        return base + A_UNITS * b + count[0] - 1, (count[0] - 1) % 2

                    m = G * b
                    end = SLOTS - 8 - LAG if last else SLOTS
                    for t in range(SLOTS):
                        if t % 8 == LAG + 1 and t <= end + 1:
                            split_max(m + t // 8 + 1)
                        if not last and qk_part(t) is not None:
                            unit, parity = next_a()
                            keep_qk(b + 1, unit, parity, qk_part(t))
                        if t < end:
                            g, u = (t + LAG) // 8 + 1, (t + LAG) % 8
                            for n in (2 * u, 2 * u + 1):
                                unit, parity = next_a()
                                take_max(unit, parity, g % 2, n)
                        if t % 8 == LAG + 1 and t >= 13:
                            make_context(m + t // 8 - 1, t // 8 - 1)
                        if ahead:
                            xn = sh.x[:, b + 2]
                            if t == 5:
                                ln.sum_tiles(dve, xn)
                            if t == 7:
                                ln.centre(dve, xn, b + 2)
                            if t == 10:
                                ln.sum_squares(dve, b + 2)
                            if t == 16:
                                ln.scale(dve, b + 2)
                        if not last:
                            if t == 1:
                                ln.split_lo(dve, x_hi, x_lo, b + 1)
                            if t in LATE_V:
                                unit, parity = next_a()
                                keep_v(unit, parity, LATE_V.index(t))
                    if not last:
                        unit, parity = next_a()
                        keep_v(unit, parity, TT - 1)
                    make_context(G * b + G - 1, G - 1)
                    for mt in range(KT):
                        unit, parity = next_a()
                        xm = sh.x[:, b, mt]
                        dve.wait_ge(a_full, unit + 1)
                        dve.scalar_tensor_tensor(out=xm, in0=ps_a[parity], scalar=bo[:, mt:mt + 1], in1=xm,
                                                 op0=ALU.add, op1=ALU.add).then_inc(a_taken, 1)

                with dve.Fori(0, B - 2) as b:
                    chunk(b, True, False)
                chunk(B - 2, False, False)
                chunk(B - 1, False, True)


def program(nc, dram, out, phases):
    with ExitStack() as ctx:
        class Sh:
            pass
        sh = Sh()
        sh.ctx = ctx

        def sb(n, shape, dt):
            return ctx.enter_context(nc.sbuf_tensor(n, shape, dt))

        sh.x = sb("x", [P, B, KT, S], F32)
        sh.mean_w = sb("mean_weights", [P, P], F32)
        sh.ident = sb("identity", [P, P], F32)
        sh.eps = sb("eps", [P, 1], F32)
        sh.ln_sum = sb("ln_sum", [P, S], F32)
        sh.ln_x = sb("ln_x", [P, KT, S], F32)
        sh.ln_sq = sb("ln_sq", [P, KT, S], F32)
        sh.ln_r = sb("ln_r", [P, S], F32)
        sh.pair_a = ctx.enter_context(nc.psum_tensor("pair_a", [P, 2, S], F32))
        sh.pair_b = [ctx.enter_context(nc.psum_tensor(f"pair_b{n}", [P, 2, S], F32)) for n in range(2)]
        sh.bank = ctx.enter_context(nc.psum_tensor("bank", [P, S], F32))
        sh.misc = ctx.enter_context(nc.psum_tensor("misc", [P, S], F32))
        loaded = ctx.enter_context(nc.semaphore("loaded"))
        made = ctx.enter_context(nc.semaphore("made"))
        stored = ctx.enter_context(nc.semaphore("stored"))
        sh.semaphores = []
        sh.norm = Norm(sh, lambda n: ctx.enter_context(nc.semaphore(n)))
        load_constants(nc, sh, dram, loaded, made)
        for n, (kind, layer) in enumerate(phases):
            if kind == "ffn":
                ffn_phase(nc, sh, f"f{n}", layer, dram)
                sh.norm.done += B + 1
            else:
                attention_phase(nc, sh, f"a{n}", layer, dram)
                sh.norm.done += B
            nc.clear_and_free_semaphores(sh.semaphores)
            sh.semaphores = []
            nc.all_engine_barrier()
        store_output(nc, sh, out, stored)


PHASES = (("ffn", 0), ("attn", 0), ("ffn", 0), ("ffn", 1), ("attn", 1), ("ffn", 1))


def feature_major(w):
    return w.reshape(KT, P, -1).transpose(1, 0, 2)


def ffn_tiles(gate, up, down, layer):
    T = TILES[layer]
    f = gate.shape[0]
    out = np.zeros((T, P, WC), np.float32)
    for at, w in ((0, gate), (D, up)):
        padded = np.zeros((T * P, D), np.float32)
        padded[:f] = w
        out[:, :, at:at + D] = padded.reshape(T, P, KT, P).transpose(0, 3, 2, 1).reshape(T, P, D)
    padded = np.zeros((T * P, D), np.float32)
    padded[:f] = down.T
    out[:, :, 2 * D:] = padded.reshape(T, P, D)
    return out


def selectors(layer):
    T = TILES[layer]
    owner = np.minimum(np.arange(T * P) // MOE, E)
    rows = (np.arange(RC)[:, None] == owner[None, :]).astype(np.float32)
    out = np.zeros((LO_ROW + RC, T * P), np.float32)
    out[:RC] = rows
    out[LO_ROW:] = rows
    return out


def head_columns(w):
    out = np.zeros((w.shape[0], G, HG, 32), np.float32)
    out[..., ROW_D:ROW_D + HD] = w.reshape(-1, G, HG, HD)
    return out.reshape(w.shape[0], G * P)


def head_rows(w):
    out = np.zeros((G, HG, 32, w.shape[1]), np.float32)
    out[:, :, :HD] = w.reshape(G, HG, HD, -1)
    return out.reshape(G, P, -1).transpose(1, 0, 2)


def attention_layout(inp):
    a = {}
    for n in range(2):
        w = {c: inp[f"L{n}_attn_W{c}"] if n == 0 else inp[f"L{n}_attn_W{c}"].T for c in "qkvo"}
        b = {c: inp[f"L{n}_attn_b{c}"] for c in "qkvo"}
        a[f"wqk{n}"] = np.stack([feature_major(head_columns(w[c])) for c in "qk"], 1)
        a[f"wv{n}"] = feature_major(w["v"])
        a[f"wo{n}"] = head_rows(w["o"])
        rows = np.stack([head_columns(b[c][None])[0].reshape(G, HG, 32) for c in "qk"])
        rows[1, :, :, ROW_M] = 1.0
        if n == 0:
            rows[0, :, :, ROW_A] = 1.0
        a[f"b_col{n}"] = rows.reshape(2 * G, P).T
        a[f"bv{n}"] = np.broadcast_to(b["v"], (P, D))
        a[f"bo{n}"] = b["o"].reshape(KT, P).T
    slope = 2.0 ** (-8.0 / H * np.arange(1, H + 1))
    bias = np.zeros((G, HG, 32, S), np.float32)
    bias[:, :, ROW_A] = np.sqrt(HD) * slope.astype(np.float32).reshape(G, HG, 1) * np.arange(1 - S, 1)
    a["bias_rows"] = bias.reshape(G, P, S).transpose(1, 0, 2)
    ahead = np.arange(P)[None, :] > np.arange(P)[:, None]
    a["masks"] = np.stack([np.eye(P), NEG * ahead, NEG * ahead.T], 1)
    sel = np.zeros((HG, 32, HG, 32), np.float32)
    for j in range(HG):
        sel[j, HD, j] = 1.0
    a["den_sel"] = sel.reshape(P, P)
    a["l_in"] = np.concatenate([inp[f"L1_attn_B{c}"] for c in "qkv"] +
                               [head_rows(inp["L1_attn_Bo"].T).transpose(2, 1, 0).reshape(RANK, G * P)], 1)
    a["l_out"] = np.concatenate([head_columns(inp[f"L1_attn_A{c}"].T) for c in "qk"] + [inp["L1_attn_Av"].T], 1)
    a["l_out_o"] = inp["L1_attn_Ao"].T
    return a


def layout(inp):
    a = {}
    a["x"] = inp["L0_attn_x"].reshape(B, S, KT, P).transpose(3, 0, 2, 1)
    a["mean_w"] = np.full((P, P), 1.0 / D, np.float32)
    a["ident"] = np.eye(P, dtype=np.float32)
    a["tri"] = np.broadcast_to((np.arange(E)[None, :] < np.arange(E)[:, None]).astype(np.float32).reshape(1, -1),
                               (P, E * E))
    gate = [np.concatenate([inp["L0_ffn_exp_wg"].reshape(E * MOE, D), inp["L0_ffn_shared_wg"]])]
    up = [np.concatenate([inp["L0_ffn_exp_wu"].reshape(E * MOE, D), inp["L0_ffn_shared_wu"]])]
    down = [np.concatenate([inp["L0_ffn_exp_wd"].transpose(1, 0, 2).reshape(D, E * MOE), inp["L0_ffn_shared_wd"]], 1)]
    gu = inp["L1_ffn_gate_up_proj"]
    gate.append(np.concatenate([gu[:, :MOE].reshape(E * MOE, D), inp["L1_ffn_sh_gate_w"]]))
    up.append(np.concatenate([gu[:, MOE:].reshape(E * MOE, D), inp["L1_ffn_sh_up_w"]]))
    down.append(np.concatenate([inp["L1_ffn_down_proj"].transpose(1, 0, 2).reshape(D, E * MOE),
                                inp["L1_ffn_sh_down_w"]], 1))
    routers = [inp["L0_ffn_gate_w"], np.concatenate([inp["L1_ffn_router_weight"], inp["L1_ffn_shared_gate_w"]])]
    for n in range(2):
        a[f"ffn{n}"] = ffn_tiles(gate[n], up[n], down[n], n)
        r = np.zeros((D, RC), np.float32)
        r[:, :routers[n].shape[0]] = routers[n].T
        a[f"router{n}"] = feature_major(r)
        a[f"sel{n}"] = selectors(n)
    a.update(attention_layout(inp))
    return {k: np.ascontiguousarray(v, dtype=np.float32) for k, v in a.items()}


def build(nc, shapes, phases):
    aps = {k: nc.dram_tensor(f"in_{k}", s, F32, kind="ExternalInput").ap() for k, s in shapes.items()}
    out = nc.dram_tensor("out_x", (P, B, KT, S), F32, kind="ExternalOutput").ap()
    dram = dict(aps)
    for group in ("ffn", "router", "sel", "wqk", "wv", "wo", "b_col", "bv", "bo"):
        if f"{group}0" in aps or f"{group}1" in aps:
            dram[group] = [aps.get(f"{group}{n}") for n in range(2)]
    program(nc, dram, out, phases)


def kernel(**inputs):
    import concourse.bacc as bacc
    from concourse.bass_utils import run_bass_kernel_spmd

    nc = bacc.Bacc("TRN2", target_bir_lowering=False, num_devices=1)
    arrays = layout({k: np.asarray(v) for k, v in inputs.items()})
    build(nc, {k: v.shape for k, v in arrays.items()}, PHASES)
    r = run_bass_kernel_spmd(nc, [{f"in_{k}": v for k, v in arrays.items()}], core_ids=[0])
    y = np.asarray(r.results[0]["out_x"])
    return np.ascontiguousarray(y.transpose(1, 3, 2, 0).reshape(B, S, D))
```

```python
from contextlib import ExitStack

import numpy as np

import concourse.bass as bass
from concourse import mybir

F32 = mybir.dt.float32
F32R = mybir.dt.float32r
BF16 = mybir.dt.bfloat16
ALU = mybir.AluOpType
ACT = mybir.ActivationFunctionType
AX = mybir.AxisListType

P = 128
D = 256
KT = D // P
B, S = 4, 512
TT = S // P
E = 8
MOE = 176
SHARED = (352, 704)
ROUTED = E * MOE // P
assert E * MOE % P == 0
TILES = tuple(-(-(E * MOE + s) // P) for s in SHARED)
WC = 3 * D
RC = 16
LO_ROW = 32
EPS = 1e-5
RING = 6
ACT_TILES = 11
EXP_SET = "natural_log_exp_and_others"

H = 16
HD = D // H
G = 4
HG = H // G
ROW_M, ROW_A, ROW_D = 0, 1, 2
ROWS = ROW_D + HD
STACK = 96
RANK = 16
NEG = -1e30
SLOTS = G * TT * HG // 2
LAG = 4
LATE_V = (29, 30, 31)
PROBS = 4
B_UNITS = 2 * TT
LORA_UNITS = 3 * KT + G
A_PROLOGUE = 2 * G + TT * HG + 2 * LAG + TT
A_UNITS = 2 * G + G * TT * HG + TT + KT
QK_SLOTS = (4, 12, 20, 27)
SYNC_STACKED, POOL_STACKED = 16 * 4 * HG, 16 * 2 * HG
MAX_STACKED = 16 * 3

ROUTER_STEPS = ((0, 2, 4, 11), (0, 3, 8, 15))


def split3(pe, out, w_hi, w_lo, x_hi, x_lo, start, stop):
    pe.matmul(out, w_hi, x_hi, start=start, stop=False)
    pe.matmul(out, w_hi, x_lo, start=False, stop=False)
    return pe.matmul(out, w_lo, x_hi, start=False, stop=stop)


class Norm:

    def __init__(self, sh, sem):
        self.sh = sh
        self.done = 0
        self.summed = sem("ln_summed")
        self.mean = sem("ln_mean")
        self.centred = sem("ln_centred")
        self.squared = sem("ln_squared")
        self.sq_summed = sem("ln_sq_summed")
        self.var = sem("ln_var")
        self.log = sem("ln_log")
        self.root = sem("ln_root")
        self.root_squared = sem("ln_root_squared")
        self.refined = sem("ln_refined")
        self.rstd = sem("ln_rstd")
        self.normed = sem("ln_normed")
        self.hi = sem("ln_hi")
        self.lo = sem("ln_lo")

    def sum_tiles(self, dve, x):
        dve.tensor_tensor(self.sh.ln_sum[:], x[:, 0, :], x[:, 1, :], ALU.add).then_inc(self.summed, 1)

    def take_mean(self, pe, n):
        pe.wait_ge(self.summed, self.done + n + 1)
        pe.matmul(self.sh.misc[:], self.sh.mean_w[:], self.sh.ln_sum[:], start=True, stop=True).then_inc(self.mean, 1)

    def centre(self, dve, x, n):
        dve.wait_ge(self.mean, self.done + n + 1)
        dve.tensor_tensor(self.sh.ln_x[:, 0, :], x[:, 0, :], self.sh.misc[:], ALU.subtract)
        dve.tensor_tensor(self.sh.ln_x[:, 1, :], x[:, 1, :], self.sh.misc[:],
                          ALU.subtract).then_inc(self.centred, 1)

    def square(self, act, n):
        act.wait_ge(self.centred, self.done + n + 1)
        act.activation(self.sh.ln_sq[:], self.sh.ln_x[:], ACT.Square).then_inc(self.squared, 1)

    def sum_squares(self, dve, n):
        dve.wait_ge(self.squared, self.done + n + 1)
        dve.tensor_tensor(self.sh.ln_sum[:], self.sh.ln_sq[:, 0, :], self.sh.ln_sq[:, 1, :],
                          ALU.add).then_inc(self.sq_summed, 1)

    def take_var(self, pe, n):
        pe.wait_ge(self.sq_summed, self.done + n + 1)
        pe.matmul(self.sh.misc[:], self.sh.mean_w[:], self.sh.ln_sum[:], start=True, stop=True).then_inc(self.var, 1)

    def take_root(self, act, n):
        act.wait_ge(self.var, self.done + n + 1)
        act.activation(self.sh.ln_r[:], self.sh.misc[:], ACT.Ln, bias=self.sh.eps[:, 0:1]).then_inc(self.log, 1)
        act.wait_ge(self.log, self.done + n + 1)
        act.activation(self.sh.ln_r[:], self.sh.ln_r[:], ACT.Exp, scale=-0.5).then_inc(self.root, 1)
        act.wait_ge(self.root, self.done + n + 1)
        act.activation(self.sh.ln_sq[:, 0], self.sh.ln_r[:], ACT.Square).then_inc(self.root_squared, 1)

    def refine(self, dve, n):
        r, r2 = self.sh.ln_r, self.sh.ln_sq[:, 0]
        dve.wait_ge(self.root_squared, self.done + n + 1)
        dve.scalar_tensor_tensor(out=r2, in0=self.sh.misc[:], scalar=EPS, in1=r2, op0=ALU.add,
                                 op1=ALU.mult).then_inc(self.refined, 1)
        dve.wait_ge(self.refined, self.done + n + 1)
        dve.scalar_tensor_tensor(out=r[:], in0=r2, scalar=-3.0, in1=r[:], op0=ALU.add,
                                 op1=ALU.mult).then_inc(self.rstd, 1)

    def scale(self, dve, n):
        r = self.sh.ln_r
        dve.wait_ge(self.centred, self.done + n + 1)
        dve.wait_ge(self.rstd, self.done + n + 1)
        for kt in range(KT):
            x = self.sh.ln_x[:, kt, :]
            last = dve.scalar_tensor_tensor(out=x, in0=x, scalar=-0.5, in1=r[:], op0=ALU.mult, op1=ALU.mult)
        last.then_inc(self.normed, 1)

    def split_hi(self, act, hi, n):
        act.wait_ge(self.normed, self.done + n + 1)
        act.activation(hi[:], self.sh.ln_x[:], ACT.Copy).then_inc(self.hi, 1)

    def split_lo(self, pool, hi, lo, n):
        pool.wait_ge(self.hi, self.done + n + 1)
        pool.tensor_tensor(lo[:], self.sh.ln_x[:], hi[:].bitcast(F32), ALU.subtract).then_inc(self.lo, 1)


def load_constants(nc, sh, dram, loaded, made):
    with nc.Block() as block:
        @block.sync
        def _(sp):
            sp.dma_start(sh.x[:, 0], dram["x"][:, 0]).then_inc(loaded, 16)
            sp.dma_start(sh.mean_w[:], dram["mean_w"]).then_inc(loaded, 16)
            sp.dma_start(sh.ident[:], dram["ident"]).then_inc(loaded, 16)
            sp.wait_ge(loaded, 48)

        @block.vector
        def _(dve):
            dve.memset(sh.eps[:], EPS).then_inc(made, 1)
            dve.wait_ge(made, 1)




def ffn_phase(nc, sh, name, layer, dram, out, first, last):
    T = TILES[layer]
    SCALES = (ROUTED, ROUTED + 1)[layer]
    with ExitStack() as ctx:
        def sb(n, shape, dt):
            return ctx.enter_context(nc.sbuf_tensor(f"{name}_{n}", shape, dt))

        def sem(n):
            handle = nc.alloc_semaphore(name=f"{name}_{n}")
            sh.semaphores.append(handle)
            return handle

        raw = sb("raw", [P, RING, WC], F32)
        w_hi = sb("w_hi", [P, T, WC], F32R)
        w_lo = sb("w_lo", [P, T, WC], F32R)
        rw = sb("rw", [P, KT, RC], F32)
        rw_hi = sb("rw_hi", [P, KT, RC], F32R)
        rw_lo = sb("rw_lo", [P, KT, RC], F32R)
        sel = sb("sel", [LO_ROW + RC, T, P], F32R)
        comb_t = [sb(f"comb_t{p}", [LO_ROW + RC, S], F32R) for p in range(2)]
        hidden = sb("hidden", [P, 5, S], F32)
        hidden_flat = hidden[:].rearrange("p a b -> p (a b)")
        act_g = [hidden[:, p] for p in range(2)]
        hid = [hidden[:, 2 + p] for p in range(2)]
        hid_hi = [sb(f"hid_hi{p}", [P, S], F32R) for p in range(2)]
        hid_lo = [sb(f"hid_lo{p}", [P, S], F32R) for p in range(2)]
        x_hi, x_lo = sh.x_hi, sh.x_lo
        tri = sb("tri", [P, E * E], F32)
        sig = sb("sig", [P, TT, E + 1], F32)
        score = sb("score", [P, TT, E], F32)
        ahead = sb("ahead", [P, TT, E, E], F32)
        tied = sb("tied", [P, TT, E, E], F32)
        col = sb("col", [P, 4, TT], F32)
        comb = sb("comb", [P, TT, RC], F32)
        logits = sb("logits", [P, S], F32)

        sel_raw = hidden_flat[0:LO_ROW + RC, 0:T * P]

        psg = [sh.pair_b[0][:, 0], sh.pair_b[0][:, 1]]
        psu = [sh.pair_b[1][:, 0], sh.pair_b[1][:, 1]]
        psc = sh.bank
        psy = sh.pair_a

        router_loaded = sem("router_loaded")
        const_loaded = sem("const_loaded")
        const_split = sem("const_split")
        x_loaded = sem("x_loaded")
        stored = sem("stored")
        const_set = sem("const_set")
        sel_made = sem("sel_made")
        raw_loaded = [sem(f"raw_loaded{r}") for r in range(RING)]
        w_hi_made = sem("w_hi_made")
        late_hi_made = sem("late_hi_made")
        w_split = sem("w_split")
        ln = sh.norm
        logits_t_made = sem("logits_t_made")
        logits_kept = sem("logits_kept")
        logits_made = sem("logits_made")
        neg_exp_made = sem("neg_exp_made")
        shifted = sem("shifted")
        soft_exp_made = sem("soft_exp_made")
        comb_made = sem("comb_made")
        comb_turned = sem("comb_turned")
        comb_hi_made = sem("comb_hi_made")
        comb_split = sem("comb_split")
        router_step = sem("router_step")
        gate_made = sem("gate_made")
        up_made = sem("up_made")
        scale_made = sem("scale_made")
        act_made = sem("act_made")
        up_used = sem("up_used")
        hid_made = sem("hid_made")
        hid_hi_made = sem("hid_hi_made")
        hid_lo_made = sem("hid_lo_made")
        down_made = sem("down_made")
        added = sem("added")

        def chunk_ahead(i, j):
            return 2 * i + 1 if j == 0 else 2 - 2 * i

        with nc.Block() as block:
            @block.sync
            def _(sp):
                sp.dma_start(rw[:], dram["router"][layer]).then_inc(router_loaded, 16)
                sp.dma_start(tri[:], dram["tri"]).then_inc(const_loaded, 16)
                sp.dma_start(sel_raw, dram["sel"][layer]).then_inc(const_loaded, 16)
                for t in range(T):
                    if t >= RING:
                        sp.wait_ge(w_split, t - RING + 1)
                    sp.dma_start(raw[:, t % RING], dram["ffn"][layer][t]).then_inc(raw_loaded[t % RING], 16)
                    if first and t < B - 1:
                        sp.dma_start(sh.x[:, t + 1], dram["x"][:, t + 1]).then_inc(x_loaded, 16)
                if last:
                    for b in range(B):
                        sp.wait_ge(added, b + 2)
                        sp.dma_start(out[:, b], sh.x[:, b]).then_inc(stored, 16)
                    sp.wait_ge(stored, 16 * B)

            @block.gpsimd
            def _(pool):
                for t in range(T):
                    if t < ACT_TILES:
                        pool.wait_ge(w_hi_made, t + 1)
                    else:
                        pool.wait_ge(raw_loaded[t % RING], 16 * (t // RING + 1))
                        pool.tensor_copy(w_hi[:, t], raw[:, t % RING]).then_inc(late_hi_made, 1)
                        pool.wait_ge(late_hi_made, t - ACT_TILES + 1)
                    pool.tensor_tensor(w_lo[:, t], raw[:, t % RING], w_hi[:, t].bitcast(F32),
                                       ALU.subtract).then_inc(w_split, 1)
                with pool.Fori(0, B // 2) as i:
                    for j in range(2):
                        ln.split_lo(pool, x_hi[1 - j], x_lo[1 - j], 2 * i + j + 1)

            @block.tensor
            def _(pe):
                pe.sem_inc(down_made, 2)

                def router_logits(p):
                    out = sh.misc[0:RC]
                    for k in range(KT):
                        ins = split3(pe, out, rw_hi[:, k], rw_lo[:, k], x_hi[p][:, k], x_lo[p][:, k],
                                     start=(k == 0), stop=(k == KT - 1))
                    ins.then_inc(logits_t_made, 1)

                def turn_logits(n):
                    pe.wait_ge(logits_kept, n + 1)
                    for q in range(TT):
                        c = slice(q * P, (q + 1) * P)
                        ins = pe.transpose(sh.misc[:, c], logits[:, c], sh.ident[:])
                    ins.then_inc(logits_made, 1)

                def turn_comb(n):
                    pe.wait_ge(comb_made, n + 1)
                    for q in range(TT):
                        ins = pe.transpose(sh.misc[0:RC, q * P:(q + 1) * P], comb[:, q, :], sh.ident[:])
                    ins.then_inc(comb_turned, 1)

                def scale(i, k):
                    j, t = k // T, k % T
                    if k == 0:
                        pe.wait_ge(sel_made, 1)
                    if t < SCALES:
                        pe.wait_ge(hid_made, 2 * T * i + k + 2)
                        pe.matmul(psc[:], sel[:, t], comb_t[j][:], start=True, stop=True).then_inc(scale_made, 1)

                def down(i, k):
                    t = k % T
                    pe.wait_ge(hid_hi_made, 2 * T * i + k + 3)
                    pe.wait_ge(hid_lo_made, 2 * T * i + k + 3)
                    if t == 0:
                        pe.wait_ge(added, 2 * i + k // T + 1)
                    for mt in range(KT):
                        cols = slice(2 * D + mt * P, 2 * D + (mt + 1) * P)
                        ins = split3(pe, psy[:, mt], w_hi[:, t, cols], w_lo[:, t, cols], hid_hi[k % 2][:],
                                     hid_lo[k % 2][:], start=(t == 0), stop=(t == T - 1))
                    ins.then_inc(down_made, 1)

                if first:
                    ln.take_mean(pe, 0)
                    ln.take_var(pe, 0)
                    pe.wait_ge(ln.lo, ln.done + 1)
                pe.wait_ge(const_split, 3)
                router_logits(0)
                turn_logits(0)
                with pe.Fori(0, B // 2) as i:
                    for k in range(2 * T):
                        j, t = k // T, k % T
                        if t == 0:
                            pe.wait_ge(ln.lo, ln.done + 2 * i + j + 1)
                        if j == 0:
                            pe.wait_ge(w_split, t + 1)
                        pe.wait_ge(act_made, 2 * T * i + k + 1)
                        for kt in range(KT):
                            c = slice(kt * P, (kt + 1) * P)
                            ins = split3(pe, psg[k % 2], w_hi[:, t, c], w_lo[:, t, c], x_hi[j][:, kt],
                                         x_lo[j][:, kt], start=(kt == 0), stop=(kt == KT - 1))
                        ins.then_inc(gate_made, 1)
                        if t == 1:
                            pe.wait_ge(comb_split, 2 * i + j + 1)
                            scale(i, k - 1)
                        pe.wait_ge(up_used, 2 * T * i + k + 1)
                        for kt in range(KT):
                            c = slice(D + kt * P, D + (kt + 1) * P)
                            ins = split3(pe, psu[k % 2], w_hi[:, t, c], w_lo[:, t, c], x_hi[j][:, kt],
                                         x_lo[j][:, kt], start=(kt == 0), stop=(kt == KT - 1))
                        ins.then_inc(up_made, 1)
                        if t == 0:
                            turn_comb(2 * i + j)
                        else:
                            scale(i, k)
                        if k >= 2:
                            down(i, k - 2)
                        n = 2 * i + j + 1
                        if t == 2:
                            ln.take_mean(pe, n)
                        if t == 5:
                            ln.take_var(pe, n)
                        if t == 8:
                            pe.wait_ge(ln.lo, ln.done + n + 1)
                            router_logits(1 - j)
                        if t == 9:
                            turn_logits(n)
                    down(i, 2 * T - 2)
                    down(i, 2 * T - 1)

            @block.scalar
            def _(act):
                act.sem_inc(act_made, 2)
                act.sem_inc(hid_hi_made, 2)

                def keep_logits(n):
                    act.wait_ge(logits_t_made, n + 1)
                    act.activation(logits[0:RC], sh.misc[0:RC], ACT.Copy).then_inc(logits_kept, 1)

                def router_exps(n):
                    act.wait_ge(logits_made, n + 1)
                    act.activation(sig[:], sh.misc[:].rearrange("p (q c) -> p q c", c=P)[:, :, 0:E + 1],
                                   ACT.Exp, scale=-1.0).then_inc(neg_exp_made, 1)
                    if layer == 1:
                        act.wait_ge(shifted, n + 1)
                        act.activation(score[:], score[:], ACT.Exp).then_inc(soft_exp_made, 1)

                def split_hid(i, k):
                    act.wait_ge(hid_made, 2 * T * i + k + 3)
                    act.wait_ge(down_made, 2 * T * i + k + 1)
                    act.activation(hid_hi[k % 2][:], hid[k % 2], ACT.Copy).then_inc(hid_hi_made, 1)

                def weights_hi(first, last):
                    for t in range(first, last):
                        act.wait_ge(raw_loaded[t % RING], 16 * (t // RING + 1))
                        act.activation(w_hi[:, t], raw[:, t % RING], ACT.Copy).then_inc(w_hi_made, 1)

                act.preload_act_table_set(EXP_SET)
                if first:
                    ln.square(act, 0)
                    weights_hi(0, 2)
                    ln.take_root(act, 0)
                    weights_hi(2, 4)
                    ln.split_hi(act, x_hi[0], 0)
                else:
                    weights_hi(0, 4)
                keep_logits(0)
                weights_hi(4, 5)
                router_exps(0)
                weights_hi(5, ACT_TILES)
                act.wait_ge(sel_made, 1)
                with act.Fori(0, B // 2) as i:
                    for k in range(2 * T):
                        j, t = k // T, k % T
                        act.wait_ge(gate_made, 2 * T * i + k + 1)
                        act.wait_ge(hid_made, 2 * T * i + k + 1)
                        act.activation(act_g[k % 2], psg[k % 2], ACT.Silu).then_inc(act_made, 1)
                        if k >= 1:
                            split_hid(i, k - 1)
                        n = 2 * i + j + 1
                        if t == 3:
                            ln.square(act, n)
                        if t == 6:
                            act.preload_act_table_set(EXP_SET)
                            ln.take_root(act, n)
                        if t == 7:
                            ln.split_hi(act, x_hi[1 - j], n)
                        if t == 8:
                            keep_logits(n)
                        if t == 10:
                            act.preload_act_table_set(EXP_SET)
                            router_exps(n)
                    split_hid(i, 2 * T - 1)

            @block.vector
            def _(dve):
                dve.sem_inc(up_used, 2)
                dve.sem_inc(hid_made, 2)
                dve.sem_inc(hid_lo_made, 2)
                dve.sem_inc(added, 1)

                sc = (sig[:, :, 0:E], score[:])[layer]

                class Chain:

                    def __init__(self, n, part):
                        self.start = n * ROUTER_STEPS[layer][-1]
                        self.steps = ROUTER_STEPS[layer][part]

                    def link(self, ins):
                        ins.then_inc(router_step, 1)
                        self.steps += 1
                        dve.wait_ge(router_step, self.start + self.steps)

                def router_sigmoid(n):
                    chain = Chain(n, 0)
                    dve.wait_ge(neg_exp_made, n + 1)
                    chain.link(dve.tensor_scalar(sig[:], sig[:], 1.0, None, ALU.add))
                    chain.link(dve.reciprocal(sig[:], sig[:]))
                    if layer == 1:
                        lg = sh.misc[:].rearrange("p (q c) -> p q c", c=P)[:, :, 0:E]
                        chain.link(dve.tensor_reduce(col[:, 0], lg, AX.X, ALU.max))
                        dve.tensor_tensor(score[:], lg, col[:, 0].unsqueeze(2).to_broadcast([P, TT, E]),
                                          ALU.subtract).then_inc(shifted, 1)
                    assert chain.steps == ROUTER_STEPS[layer][1]

                def router_compare(n):
                    chain = Chain(n, 1)
                    if layer == 1:
                        dve.wait_ge(soft_exp_made, n + 1)
                        chain.link(dve.tensor_reduce(col[:, 1], score[:], AX.X, ALU.add))
                        chain.link(dve.reciprocal(col[:, 1], col[:, 1]))
                        chain.link(dve.tensor_tensor(score[:], score[:],
                                                     col[:, 1].unsqueeze(2).to_broadcast([P, TT, E]), ALU.mult))
                    mine = sc.unsqueeze(3).to_broadcast([P, TT, E, E])
                    other = sc.unsqueeze(2).to_broadcast([P, TT, E, E])
                    chain.link(dve.tensor_tensor(ahead[:], other, mine, ALU.is_gt))
                    chain.link(dve.tensor_tensor(tied[:], other, mine, ALU.is_equal))
                    assert chain.steps == ROUTER_STEPS[layer][2]

                def router_combine(n):
                    chain = Chain(n, 2)
                    tri4 = tri[:].rearrange("p (a b) -> p a b", a=E)
                    for q in range(TT):
                        last = dve.tensor_tensor(tied[:, q], tied[:, q], tri4, ALU.mult)
                    chain.link(last)
                    chain.link(dve.tensor_tensor(ahead[:], ahead[:], tied[:], ALU.add))
                    chain.link(dve.tensor_reduce(tied[:, :, :, 0], ahead[:], AX.X, ALU.add))
                    chain.link(dve.scalar_tensor_tensor(out=comb[:, :, 0:E], in0=tied[:, :, :, 0], scalar=2.0, in1=sc,
                                                        op0=ALU.is_lt, op1=ALU.mult))
                    chain.link(dve.tensor_reduce(col[:, 2], comb[:, :, 0:E], AX.X, ALU.add))
                    if layer == 1:
                        chain.link(dve.reciprocal(col[:, 3], col[:, 2]))
                        chain.link(dve.tensor_copy(comb[:, :, E:E + 1], sig[:, :, E:E + 1]))
                        gain = 1.0
                    else:
                        chain.link(dve.tensor_scalar(col[:, 2], col[:, 2], 1e-20, None, ALU.add))
                        chain.link(dve.reciprocal(col[:, 3], col[:, 2]))
                        gain = 2.5
                    dve.scalar_tensor_tensor(out=comb[:, :, 0:E], in0=comb[:, :, 0:E], scalar=gain,
                                             in1=col[:, 3].unsqueeze(2).to_broadcast([P, TT, E]), op0=ALU.mult,
                                             op1=ALU.mult).then_inc(comb_made, 1)
                    assert chain.steps == ROUTER_STEPS[layer][3]

                def split_comb(p, n):
                    dve.wait_ge(comb_turned, n + 1)
                    dve.tensor_copy(comb_t[p][0:RC], sh.misc[0:RC]).then_inc(comb_hi_made, 1)
                    dve.wait_ge(comb_hi_made, n + 1)
                    dve.tensor_tensor(comb_t[p][LO_ROW:LO_ROW + RC], sh.misc[0:RC], comb_t[p][0:RC].bitcast(F32),
                                      ALU.subtract).then_inc(comb_split, 1)

                def split_hid(i, k):
                    dve.wait_ge(hid_hi_made, 2 * T * i + k + 3)
                    dve.wait_ge(down_made, 2 * T * i + k + 1)
                    dve.tensor_tensor(hid_lo[k % 2][:], hid[k % 2], hid_hi[k % 2][:].bitcast(F32),
                                      ALU.subtract).then_inc(hid_lo_made, 1)

                def add_output(i, j):
                    dve.wait_ge(down_made, 2 * T * i + (j + 1) * T + 2)
                    xc = sh.x[:, 2 * i + j]
                    dve.scalar_tensor_tensor(out=xc, in0=psy[:], scalar=0.5, in1=xc, op0=ALU.mult,
                                             op1=ALU.add).then_inc(added, 1)

                dve.memset(logits[:], 0.0).then_inc(const_split, 1)
                if first:
                    ln.sum_tiles(dve, sh.x[:, 0])
                    ln.centre(dve, sh.x[:, 0], 0)
                dve.wait_ge(router_loaded, 16)
                dve.tensor_copy(rw_hi[:], rw[:]).then_inc(const_split, 1)
                if first:
                    ln.sum_squares(dve, 0)
                dve.wait_ge(const_split, 2)
                dve.tensor_tensor(rw_lo[:], rw[:], rw_hi[:].bitcast(F32), ALU.subtract).then_inc(const_split, 1)
                if first:
                    ln.refine(dve, 0)
                    ln.scale(dve, 0)
                    ln.split_lo(dve, x_hi[0], x_lo[0], 0)
                dve.memset(comb_t[0][:].bitcast(F32), 0.0).then_inc(const_set, 1)
                dve.memset(comb_t[1][:].bitcast(F32), 0.0).then_inc(const_set, 1)
                dve.memset(comb[:], 0.0).then_inc(const_set, 1)
                dve.wait_ge(const_set, 3)
                dve.memset(comb[:, :, E:E + 1], 1.0).then_inc(const_set, 1)
                dve.wait_ge(const_set, 4)
                dve.wait_ge(const_loaded, 32)
                dve.tensor_copy(sel[:].rearrange("p t c -> p (t c)"), sel_raw).then_inc(sel_made, 1)
                dve.wait_ge(sel_made, 1)
                router_sigmoid(0)
                router_compare(0)
                router_combine(0)
                if first:
                    dve.wait_ge(x_loaded, 16 * (B - 1))
                with dve.Fori(0, B // 2) as i:
                    for k in range(2 * T):
                        j, t = k // T, k % T
                        if k == T + 2:
                            add_output(i, 0)
                        if k == T + 1:
                            dve.wait_ge(added, i + 1)
                        if t == 0:
                            split_comb(j, 2 * i + j)
                        dve.wait_ge(act_made, 2 * T * i + k + 3)
                        dve.wait_ge(up_made, 2 * T * i + k + 1)
                        dve.tensor_tensor(act_g[k % 2], act_g[k % 2], psu[k % 2], ALU.mult).then_inc(up_used, 1)
                        dve.wait_ge(up_used, 2 * T * i + k + 3)
                        dve.wait_ge(scale_made, 2 * SCALES * i + SCALES * j + min(t, SCALES - 1) + 1)
                        dve.wait_ge(hid_hi_made, 2 * T * i + k + 1)
                        dve.wait_ge(hid_lo_made, 2 * T * i + k + 1)
                        if layer == 0 and t >= ROUTED:
                            dve.tensor_copy(hid[k % 2], act_g[k % 2]).then_inc(hid_made, 1)
                        else:
                            dve.tensor_tensor(hid[k % 2], act_g[k % 2], psc[:], ALU.mult).then_inc(hid_made, 1)
                        if k >= 1:
                            split_hid(i, k - 1)
                        n = 2 * i + j + 1
                        xn = sh.x[:, chunk_ahead(i, j)]
                        if t == 1:
                            ln.sum_tiles(dve, xn)
                        if t == 3:
                            ln.centre(dve, xn, n)
                        if t == 4:
                            ln.sum_squares(dve, n)
                        if t == 6:
                            ln.refine(dve, n)
                            ln.scale(dve, n)
                        if t == 10:
                            router_sigmoid(n)
                        if t == 11:
                            router_compare(n)
                        if t == 12:
                            router_combine(n)
                    split_hid(i, 2 * T - 1)
                    add_output(i, 1)




def attention_phase(nc, sh, name, layer, dram):
    causal = layer == 0
    lora = layer == 1
    with ExitStack() as ctx:
        def sb(n, shape, dt):
            return ctx.enter_context(nc.sbuf_tensor(f"{name}_{n}", shape, dt))

        def sem(n):
            handle = nc.alloc_semaphore(name=f"{name}_{n}")
            sh.semaphores.append(handle)
            return handle

        wqk_hi = sb("wqk_hi", [P, 2, KT, G * P], F32R)
        wqk_lo = sb("wqk_lo", [P, 2, KT, G * P], F32R)
        wv_hi = sb("wv_hi", [P, KT, D], F32R)
        wv_lo = sb("wv_lo", [P, KT, D], F32R)
        wo = sb("wo", [P, G, D], F32)
        b_col = sb("b_col", [P, 2 * G], F32)
        bv = sb("bv", [P, D], F32)
        bo = sb("bo", [P, KT], F32)
        den_sel = sb("den_sel", [P, P], F32)
        if causal:
            bias_rows = sb("bias_rows", [P, G, S], F32)
            slope = sb("slope", [P, G], F32)
            ramp = sb("ramp", [P, S], F32)
            mask_in = sb("mask_in", [P, 3, P], F32)
            mask = sb("mask", [P, 3, P], BF16)
        x_hi, x_lo = sh.x_hi[0], sh.x_lo[0]
        qk = [sb(f"{n}_all", [P, S], F32) for n in "qk"]
        qk_hi = sb("qk_hi", [P, 2, 2, S], F32R)
        qk_lo = sb("qk_lo", [P, 2, 2, S], F32R)
        stack = [sb(f"{n}_stack", [STACK, G, HG, S], F32R) for n in "qk"]
        neg_max = sb("neg_max", [P, 2, TT, HG], F32)
        max_hi = sb("max_hi", [HG, S], F32R)
        max_lo = sb("max_lo", [HG, S], F32R)
        probs = sb("probs", [P, PROBS, 2, S], F32)
        v_one = sb("v_one", [P, TT, H, 32], F32)
        heads = sb("heads", [P, S], F32)
        rden = sb("rden", [P, S], F32)
        context = sb("context", [P, G, S], F32)

        flat = probs[:].rearrange("p a b c -> p (a b c)")
        wqk = flat[:, 0:4 * G * P].rearrange("p (w k c) -> p w k c", w=2, k=KT)
        wv = flat[:, 4 * G * P:4 * G * P + KT * D].rearrange("p (k c) -> p k c", k=KT)
        l_in = context[0:RANK].rearrange("p a b -> p (a b)")[:, 0:3 * D + G * P]
        l_out = flat[0:RANK, 4 * G * P + KT * D:4 * G * P + KT * D + 2 * G * P + D]
        l_out_o = rden[0:RANK, 0:D]

        ps_a = [sh.pair_a[:, 0], sh.pair_a[:, 1]]
        ps_b = sh.pair_b
        ps_o = sh.bank
        misc = sh.misc

        qk_loaded = sem("qk_loaded")
        loaded = sem("loaded")
        w_hi_made = sem("w_hi_made")
        w_split = sem("w_split")
        set_up = sem("set_up")
        bias_made = sem("bias_made")
        ln = sh.norm
        a_full = sem("a_full")
        a_taken = sem("a_taken")
        qk_hi_made = sem("qk_hi_made")
        qk_lo_made = sem("qk_lo_made")
        parts_ready = sem("parts_ready")
        sync_stacked = [sem(f"sync_stacked{p}") for p in range(2)]
        pool_stacked = [sem(f"pool_stacked{p}") for p in range(2)]
        max_stacked = sem("max_stacked")
        max_turned = sem("max_turned")
        max_hi_made = sem("max_hi_made")
        max_lo_made = sem("max_lo_made")
        b_full = sem("b_full")
        b_taken = sem("b_taken")
        pv_made = sem("pv_made")
        heads_kept = sem("heads_kept")
        den_made = sem("den_made")
        den_log = sem("den_log")
        rden_made = sem("rden_made")
        context_made = sem("context_made")

        def k_end(q):
            return (q + 1) * P if causal else S

        def q_start(k):
            return k * P if causal else 0

        n_loads = 9 if causal else 6
        n_qk_loads = 2 if causal else 5
        before = LORA_UNITS if lora else 0
        base = before + A_PROLOGUE

        def qk_ahead(t):
            return sum(min(max(t + 1 - at, 0), 2) for at in QK_SLOTS)

        def qk_part(t):
            for g, at in enumerate(QK_SLOTS):
                if at <= t < at + 2:
                    return 2 * g + t - at
            return None

        def stack_group(eng, which, rows, g, done):
            for row in rows:
                src = {0: qk_hi, 32: (qk_hi, qk_lo)[which], 64: (qk_lo, qk_hi)[which]}[row]
                for j in range(HG):
                    eng.dma_start(stack[which][row:row + ROWS, g, j].bitcast(F32),
                                  src[32 * j:32 * j + ROWS, which, g % 2].bitcast(F32)).then_inc(done, 16)

        with nc.Block() as block:
            @block.sync
            def _(sp):
                for n in range(2):
                    sp.dma_start(wqk[:, n], dram["wqk"][layer][:, n]).then_inc(qk_loaded, 16)
                if lora:
                    for dst, src in ((l_in, "l_in"), (l_out, "l_out"), (l_out_o, "l_out_o")):
                        sp.dma_start(dst, dram[src]).then_inc(qk_loaded, 16)
                for dst, src in ((b_col[:], "b_col"), (bv[:], "bv"), (bo[:], "bo"), (wv, "wv"), (wo[:], "wo")):
                    sp.dma_start(dst, dram[src][layer]).then_inc(loaded, 16)
                sp.dma_start(den_sel[:], dram["den_sel"]).then_inc(loaded, 16)
                if causal:
                    for dst, src in ((slope, "slope"), (ramp, "ramp"), (mask_in, "masks")):
                        sp.dma_start(dst[:], dram[src]).then_inc(loaded, 16)
                sp.wait_ge(set_up, 2)

                def stack_qk(g, groups):
                    sp.wait_ge(parts_ready, groups)
                    stack_group(sp, 1, (0,), g, sync_stacked[g % 2])
                    stack_group(sp, 0, (0, 32, 64), g, sync_stacked[g % 2])

                def stack_max(m, g):
                    sp.wait_ge(max_lo_made, m + 1)
                    for row, src in ((0, max_hi), (32, max_hi), (64, max_lo)):
                        sp.dma_start(stack[0][row:row + 1, g].bitcast(F32), src[:].bitcast(F32)
                                     ).then_inc(max_stacked, 16)

                def chunk(b, last):
                    for g in range(G):
                        if g + 1 < G or not last:
                            stack_max(G * b + g + 1, (g + 1) % G)
                        if not last:
                            stack_qk(g, G * b + G + g + 1)

                stack_qk(0, 1)
                stack_qk(1, 2)
                stack_qk(2, 3)
                stack_max(0, 0)
                stack_qk(3, 4)
                with sp.Fori(0, B - 1) as b:
                    chunk(b, False)
                chunk(B - 1, True)

            @block.gpsimd
            def _(pool):
                for which in range(2):
                    pool.memset(stack[which][:].bitcast(F32), 0.0).then_inc(set_up, 1)

                def split_lo(b, n):
                    which = n % 2
                    pool.wait_ge(qk_hi_made, 2 * G * b + n + 3)
                    pool.tensor_tensor(qk_lo[:, which, n // 2 % 2], qk[which][:],
                                       qk_hi[:, which, n // 2 % 2].bitcast(F32),
                                       ALU.subtract).then_inc(qk_lo_made, 1)

                def stack_k(g, made):
                    pool.wait_ge(qk_lo_made, made)
                    pool.sem_inc(parts_ready, 1)
                    stack_group(pool, 1, (32, 64), g, pool_stacked[g % 2])

                pool.wait_ge(set_up, 2)
                for g in range(G):
                    stack_k(g, 2 * g + 4)
                with pool.Fori(0, B - 1) as b:
                    for g in range(G):
                        split_lo(b + 1, 2 * g)
                        pool.wait_ge(b_full, B_UNITS * G * b + B_UNITS * (g + 1))
                        split_lo(b + 1, 2 * g + 1)
                        stack_k(g, 2 * G * b + 2 * G + 2 * g + 4)

            @block.tensor
            def _(pe):
                pe.sem_inc(pv_made, 2)

                def use_a(unit):
                    pe.wait_ge(a_taken, unit + 1)

                def project(unit, n, parity):
                    g, which = n // 2, n % 2
                    use_a(unit)
                    c = slice(g * P, (g + 1) * P)
                    for kt in range(KT):
                        ins = split3(pe, ps_a[parity], wqk_hi[:, which, kt, c], wqk_lo[:, which, kt, c],
                                     x_hi[:, kt], x_lo[:, kt], start=(kt == 0), stop=(kt == KT - 1))
                    ins.then_inc(a_full, 1)

                def project_v(unit, q, parity):
                    use_a(unit)
                    t = slice(q * P, (q + 1) * P)
                    for kt in range(KT):
                        ins = split3(pe, ps_a[parity][:, 0:D], x_hi[:, kt, t], x_lo[:, kt, t], wv_hi[:, kt],
                                     wv_lo[:, kt], start=(kt == 0), stop=(kt == KT - 1))
                    ins.then_inc(a_full, 1)

                def max_scores(unit, g, n, parity):
                    q, j = n // HG, n % HG
                    use_a(unit)
                    out = ps_a[parity]
                    end = k_end(q)
                    ins = pe.matmul(out[:, 0:end], stack[0][:, g, j, q * P:(q + 1) * P], stack[1][:, g, j, 0:end],
                                    start=True, stop=not causal)
                    if causal:
                        ins = pe.matmul(out[:, q * P:end], mask[:, 0], mask[:, 1], start=False, stop=True)
                    ins.then_inc(a_full, 1)

                def scores(m, g, u):
                    k, pair = u // 2, u % 2
                    pe.wait_ge(b_taken, B_UNITS * m + u + 1)
                    lo = q_start(k)
                    for half in range(2):
                        j = 2 * pair + half
                        out = ps_b[u % 2][:, half]
                        ins = pe.matmul(out[:, lo:S], stack[1][:, g, j, k * P:(k + 1) * P],
                                        stack[0][:, g, j, lo:S], start=True, stop=not causal)
                        if causal:
                            ins = pe.matmul(out[:, lo:lo + P], mask[:, 0], mask[:, 2], start=False, stop=True)
                    ins.then_inc(b_full, 1)

                def attend(m, g, k):
                    pe.wait_ge(b_taken, B_UNITS * m + 2 * k + 4)
                    if k == 0:
                        pe.wait_ge(heads_kept, m + 1)
                    lo = q_start(k)
                    for j in range(HG):
                        ins = pe.matmul(ps_o[32 * j:32 * (j + 1), lo:S], v_one[:, k, HG * g + j],
                                        probs[:, (2 * k + j // 2) % PROBS, j % 2, lo:S], start=(k == 0),
                                        stop=(k == TT - 1), tile_position=(0, 32 * j), skip_group_check=True)
                    ins.then_inc(pv_made, 1)

                def turn_max(m, side, last_unit):
                    pe.wait_ge(a_taken, last_unit + 3)
                    for q in range(TT):
                        ins = pe.transpose(misc[0:HG, q * P:(q + 1) * P], neg_max[:, side, q], sh.ident[:])
                    ins.then_inc(max_turned, 1)

                def spread_den(m, alone):
                    pe.wait_ge(heads_kept, m + 2)
                    if alone:
                        pe.wait_ge(den_log, m + 1)
                    else:
                        pe.wait_ge(max_hi_made, m + 2)
                        pe.wait_ge(max_lo_made, m + 2)
                    pe.matmul(misc[:], den_sel[:], heads[:], start=True, stop=True).then_inc(den_made, 1)

                def output(parity, mt, b, groups):
                    for g in groups:
                        pe.wait_ge(context_made, G * b + g + 2)
                        ins = pe.matmul(ps_a[parity], wo[:, g, mt * P:(mt + 1) * P], context[:, g], start=(g == 0),
                                        stop=(g == G - 1))
                    return ins

                if lora:
                    pe.wait_ge(qk_loaded, 16 * n_qk_loads)
                    for unit in range(LORA_UNITS):
                        use_a(unit)
                        n, kt = unit // KT, unit % KT
                        if n < 3:
                            lhs = l_in[:, n * D + kt * P:n * D + (kt + 1) * P]
                            rhs = l_out[:, n * G * P:n * G * P + (G * P if n < 2 else D)]
                        else:
                            g = unit - 3 * KT
                            lhs = l_in[:, 3 * D + g * P:3 * D + (g + 1) * P]
                            rhs = l_out_o
                        pe.matmul(ps_a[unit % 2][:, 0:rhs.shape[-1]], lhs, rhs, start=True,
                                  stop=True).then_inc(a_full, 1)
                pe.wait_ge(w_split, 2)
                unit = before
                for n in range(4):
                    project(unit, n, unit % 2)
                    unit += 1
                ln.take_mean(pe, 1)
                pe.wait_ge(loaded, 16 * n_loads)
                pe.wait_ge(w_split, 3)
                for q in range(TT):
                    project_v(unit, q, unit % 2)
                    unit += 1
                ln.take_var(pe, 1)
                for n in range(4, 2 * G):
                    project(unit, n, unit % 2)
                    unit += 1
                pe.wait_ge(sync_stacked[0], SYNC_STACKED)
                pe.wait_ge(pool_stacked[0], POOL_STACKED)
                for n in range(TT * HG + 2 * LAG):
                    if n == TT * HG:
                        pe.wait_ge(sync_stacked[1], SYNC_STACKED)
                        pe.wait_ge(pool_stacked[1], POOL_STACKED)
                    max_scores(unit, n // 16, n % 16, unit % 2)
                    unit += 1
                    if n == TT * HG + 1:
                        pe.wait_ge(ln.refined, ln.done + 2)
                        turn_max(0, 0, before + 2 * G + TT + TT * HG - 1)
                assert unit == base and base % 2 == 0 and A_UNITS % 2 == 0

                def chunk(b, last):
                    count = [0]

                    def next_a():
                        count[0] += 1
                        return base + A_UNITS * b + count[0] - 1, (count[0] - 1) % 2

                    m = G * b
                    end = SLOTS - 8 - LAG if last else SLOTS
                    for t in range(SLOTS):
                        if not last and qk_part(t) is not None:
                            if qk_part(t) == 0:
                                pe.wait_ge(ln.lo, ln.done + b + 2)
                            unit, parity = next_a()
                            project(unit, qk_part(t), parity)
                        g, u = (t + LAG) // 8 + 1, (t + LAG) % 8
                        if t < end:
                            if u == 0:
                                p, here, each = g % 2, g // 2 + 1, G // 2
                                pe.wait_ge(sync_stacked[p], each * SYNC_STACKED * b + here * SYNC_STACKED)
                                pe.wait_ge(pool_stacked[p], each * POOL_STACKED * b + here * POOL_STACKED)
                            unit, parity = next_a()
                            max_scores(unit, g % G, 2 * u, parity)
                        if t % 8 == 0:
                            pe.wait_ge(max_stacked, MAX_STACKED * (m + t // 8 + 1))
                        scores(m + t // 8, t // 8, t % 8)
                        if t < end:
                            unit, parity = next_a()
                            max_scores(unit, g % G, 2 * u + 1, parity)
                        k = (t - 3) // 2
                        if t % 2 == 1 and k >= 0:
                            attend(m + k // TT, k // TT, k % TT)
                        if t in (6, 14) and not last:
                            pe.wait_ge(max_hi_made, m + t // 8 + 2)
                            pe.wait_ge(max_lo_made, m + t // 8 + 2)
                            if t == 6:
                                ln.take_mean(pe, b + 2)
                            else:
                                ln.take_var(pe, b + 2)
                        if t % 8 == 3 and t >= 11:
                            if t == 11 and not last:
                                pe.wait_ge(ln.centred, ln.done + b + 3)
                            if t == 19 and not last:
                                pe.wait_ge(ln.refined, ln.done + b + 3)
                            spread_den(m + t // 8 - 1, False)
                        if t % 8 == LAG and t <= end:
                            g = t // 8 + 1
                            pe.wait_ge(max_hi_made, m + g)
                            pe.wait_ge(max_lo_made, m + g)
                            pe.wait_ge(den_log, m + g)
                            turn_max(m + g, g % 2, base + A_UNITS * b + 2 * t - 1
                                     + (0 if last else qk_ahead(t - 1)))
                        if t in LATE_V and not last:
                            unit, parity = next_a()
                            project_v(unit, LATE_V.index(t), parity)
                    attend(m + G - 1, G - 1, TT - 1)
                    if not last:
                        unit, parity = next_a()
                        project_v(unit, TT - 1, parity)
                    spread_den(m + G - 1, last)
                    (unit0, parity0), (unit1, parity1) = next_a(), next_a()
                    use_a(unit0)
                    use_a(unit1)
                    output(parity0, 0, b, range(G - 1))
                    output(parity1, 1, b, range(G - 1))
                    output(parity0, 0, b, (G - 1,)).then_inc(a_full, 1)
                    output(parity1, 1, b, (G - 1,)).then_inc(a_full, 1)

                with pe.Fori(0, B - 1) as b:
                    chunk(b, False)
                chunk(B - 1, True)

            @block.scalar
            def _(act):
                act.sem_inc(b_taken, 2)
                act.sem_inc(heads_kept, 1)
                act.sem_inc(den_log, 1)
                act.sem_inc(qk_hi_made, 2)
                act.preload_act_table_set(EXP_SET)
                act.wait_ge(qk_loaded, 16 * n_qk_loads)
                if lora:
                    act.wait_ge(a_taken, 2 * KT + 2)
                act.activation(wqk_hi[:, 0], wqk[:, 0], ACT.Copy).then_inc(w_hi_made, 1)
                act.activation(wqk_hi[:, 1], wqk[:, 1], ACT.Copy).then_inc(w_hi_made, 1)
                act.wait_ge(loaded, 16 * n_loads)
                if lora:
                    act.wait_ge(a_taken, LORA_UNITS + 2)
                act.activation(wv_hi[:], wv, ACT.Copy).then_inc(w_hi_made, 1)

                def split_hi(b, n, unit):
                    which = n % 2
                    act.wait_ge(a_taken, unit + 3)
                    act.activation(qk_hi[:, which, n // 2 % 2], qk[which][:], ACT.Copy).then_inc(qk_hi_made, 1)

                def keep_max(m):
                    act.wait_ge(max_turned, m + 1)
                    act.activation(max_hi[:], misc[0:HG], ACT.Copy).then_inc(max_hi_made, 1)

                def exps(m, u):
                    k = u // 2
                    lo = q_start(k)
                    act.wait_ge(b_full, B_UNITS * m + u + 1)
                    act.wait_ge(pv_made, TT * m + (u - PROBS) // 2 + 3)
                    act.activation(probs[:, u % PROBS, :, lo:S], ps_b[u % 2][:, :, lo:S], ACT.Exp,
                                   scale=float(HD) ** -0.5).then_inc(b_taken, 1)

                def keep_heads(m):
                    act.wait_ge(pv_made, TT * m + TT + 2)
                    act.wait_ge(context_made, m + 1)
                    act.activation(heads[:], ps_o[:], ACT.Copy).then_inc(heads_kept, 1)

                def invert_den(m):
                    act.wait_ge(den_made, m + 1)
                    act.activation(rden[:], misc[:], ACT.Ln).then_inc(den_log, 1)
                    act.wait_ge(den_log, m + 2)
                    act.activation(rden[:], rden[:], ACT.Exp, scale=-1.0).then_inc(rden_made, 1)

                for n in range(4):
                    split_hi(0, n, before + n)
                ln.square(act, 1)
                ln.take_root(act, 1)
                for n in range(4, 2 * G):
                    if n % 2 == 0:
                        act.wait_ge(sync_stacked[n // 2 % 2], SYNC_STACKED * (n // 4))
                        act.wait_ge(pool_stacked[n // 2 % 2], POOL_STACKED * (n // 4))
                    split_hi(0, n, before + TT + n)
                keep_max(0)

                def chunk(b, last):
                    m = G * b
                    for t in range(SLOTS):
                        n = None if last else qk_part(t)
                        if n is not None:
                            if n % 2 == 0:
                                p, here, each = n // 2 % 2, n // 4 + G // 2, G // 2
                                act.wait_ge(sync_stacked[p], each * SYNC_STACKED * b + here * SYNC_STACKED)
                                act.wait_ge(pool_stacked[p], each * POOL_STACKED * b + here * POOL_STACKED)
                            split_hi(b + 1, n, base + A_UNITS * b + 2 * t + qk_ahead(t) - 1)
                        exps(m + t // 8, t % 8)
                        if t == 0:
                            act.wait_ge(a_full, base + A_UNITS * b - KT)
                            ln.split_hi(act, x_hi, b + 1)
                        if not last:
                            if t == 8:
                                ln.square(act, b + 2)
                            if t == 15:
                                ln.take_root(act, b + 2)
                        if t % 8 == LAG and t <= (SLOTS - 8 - LAG if last else SLOTS):
                            act.wait_ge(max_stacked, MAX_STACKED * (m + t // 8 + 1))
                            keep_max(m + t // 8 + 1)
                        if t % 8 == 2 and t >= 10:
                            keep_heads(m + t // 8 - 1)
                        if t % 8 == 3 and t >= 11:
                            invert_den(m + t // 8 - 1)
                    keep_heads(m + G - 1)
                    invert_den(m + G - 1)

                with act.Fori(0, B - 1) as b:
                    chunk(b, False)
                chunk(B - 1, True)

            @block.vector
            def _(dve):
                dve.sem_inc(a_taken, 2)
                dve.sem_inc(context_made, 1)
                dve.sem_inc(qk_lo_made, 2)
                ln.sum_tiles(dve, sh.x[:, 1])
                dve.memset(v_one[:, :, :, HD:32], 1.0)
                def merge(units):
                    for unit in units:
                        w = targets[unit]
                        dve.wait_ge(a_full, unit + 1)
                        dve.scalar_tensor_tensor(out=w, in0=ps_a[unit % 2][:, 0:w.shape[-1]], scalar=0.5, in1=w,
                                                 op0=ALU.mult, op1=ALU.add).then_inc(a_taken, 1)

                targets = [wqk[:, n, kt] for n in range(2) for kt in range(KT)]
                targets += [wv[:, kt] for kt in range(KT)] + [wo[:, g] for g in range(G)]
                if lora:
                    dve.wait_ge(qk_loaded, 16 * n_qk_loads)
                    merge(range(2 * KT))
                for n in range(2):
                    dve.wait_ge(w_hi_made, n + 1)
                    dve.tensor_tensor(wqk_lo[:, n], wqk[:, n], wqk_hi[:, n].bitcast(F32),
                                      ALU.subtract).then_inc(w_split, 1)
                dve.wait_ge(loaded, 16 * n_loads)
                if causal:
                    dve.tensor_copy(mask[:], mask_in[:])
                    for g in range(G):
                        dve.tensor_scalar(bias_rows[:, g], ramp[:], slope[:, g:g + 1], b_col[:, G + g:G + g + 1],
                                          ALU.mult, ALU.add).then_inc(bias_made, 1)
                    dve.wait_ge(bias_made, G)
                if lora:
                    merge(range(2 * KT, LORA_UNITS))
                dve.wait_ge(w_hi_made, 3)
                dve.tensor_tensor(wv_lo[:], wv, wv_hi[:].bitcast(F32), ALU.subtract).then_inc(w_split, 1)

                def keep_qk(b, unit, parity, n):
                    g, which = n // 2, n % 2
                    dve.wait_ge(a_full, unit + 1)
                    dve.wait_ge(qk_hi_made, 2 * G * b + n + 1)
                    dve.wait_ge(qk_lo_made, 2 * G * b + n + 1)
                    bias = b_col[:, G * which + g:G * which + g + 1]
                    if which == 1 and causal:
                        dve.tensor_tensor(qk[1][:], ps_a[parity], bias_rows[:, g], ALU.add).then_inc(a_taken, 1)
                    else:
                        dve.tensor_scalar(qk[which][:], ps_a[parity], bias, None, ALU.add).then_inc(a_taken, 1)

                def split_lo(n):
                    which = n % 2
                    dve.wait_ge(qk_hi_made, n + 3)
                    dve.tensor_tensor(qk_lo[:, which, n // 2 % 2], qk[which][:],
                                      qk_hi[:, which, n // 2 % 2].bitcast(F32),
                                      ALU.subtract).then_inc(qk_lo_made, 1)

                def take_max(unit, parity, side, n):
                    q, j = n // HG, n % HG
                    dve.wait_ge(a_full, unit + 1)
                    dve.tensor_reduce(neg_max[:, side, q, j:j + 1], ps_a[parity][:, 0:k_end(q)], AX.X, ALU.max,
                                      negate=True).then_inc(a_taken, 1)

                def split_max(m):
                    dve.wait_ge(max_hi_made, m + 1)
                    dve.tensor_tensor(max_lo[:], misc[0:HG], max_hi[:].bitcast(F32),
                                      ALU.subtract).then_inc(max_lo_made, 1)

                def keep_v(unit, parity, q):
                    dve.wait_ge(a_full, unit + 1)
                    dve.tensor_tensor(v_one[:, q, :, 0:HD], ps_a[parity][:, 0:D].rearrange("p (h c) -> p h c", h=H),
                                      bv[:].rearrange("p (h c) -> p h c", h=H), ALU.add).then_inc(a_taken, 1)

                def make_context(m, g):
                    dve.wait_ge(rden_made, m + 1)
                    dve.tensor_tensor(context[:, g], heads[:], rden[:], ALU.mult).then_inc(context_made, 1)

                unit = before
                for n in range(4):
                    keep_qk(0, unit, unit % 2, n)
                    unit += 1
                    if n % 2 == 1:
                        split_lo(n - 1)
                        split_lo(n)
                ln.centre(dve, sh.x[:, 1], 1)
                for q in range(TT):
                    keep_v(unit, unit % 2, q)
                    unit += 1
                ln.sum_squares(dve, 1)
                ln.refine(dve, 1)
                ln.scale(dve, 1)
                for n in range(4, 2 * G):
                    if n >= 6:
                        split_lo(n - 2)
                    keep_qk(0, unit, unit % 2, n)
                    unit += 1
                for n in range(TT * HG + 2 * LAG):
                    take_max(unit, unit % 2, n // 16, n % 16)
                    unit += 1
                    if n == TT * HG - 1:
                        split_lo(6)
                        split_lo(7)
                    if n == TT * HG + 3:
                        split_max(0)

                def chunk(b, xn, last):
                    count = [0]

                    def next_a():
                        count[0] += 1
                        return base + A_UNITS * b + count[0] - 1, (count[0] - 1) % 2

                    m = G * b
                    end = SLOTS - 8 - LAG if last else SLOTS
                    for t in range(SLOTS):
                        if t % 8 == LAG + 1 and t <= end + 1:
                            split_max(m + t // 8 + 1)
                        if not last and qk_part(t) is not None:
                            unit, parity = next_a()
                            keep_qk(b + 1, unit, parity, qk_part(t))
                        if t < end:
                            g, u = (t + LAG) // 8 + 1, (t + LAG) % 8
                            for n in (2 * u, 2 * u + 1):
                                unit, parity = next_a()
                                take_max(unit, parity, g % 2, n)
                        if t % 8 == LAG + 1 and t >= 13:
                            make_context(m + t // 8 - 1, t // 8 - 1)
                        if not last:
                            if t == 5:
                                ln.sum_tiles(dve, xn)
                            if t == 7:
                                ln.centre(dve, xn, b + 2)
                            if t == 10:
                                ln.sum_squares(dve, b + 2)
                            if t == 16:
                                ln.refine(dve, b + 2)
                            if t == 18:
                                ln.scale(dve, b + 2)
                        if t == 1:
                            ln.split_lo(dve, x_hi, x_lo, b + 1)
                        if t in LATE_V and not last:
                            unit, parity = next_a()
                            keep_v(unit, parity, LATE_V.index(t))
                    if not last:
                        unit, parity = next_a()
                        keep_v(unit, parity, TT - 1)
                    make_context(G * b + G - 1, G - 1)
                    for mt in range(KT):
                        unit, parity = next_a()
                        xm = sh.x[:, b, mt]
                        dve.wait_ge(a_full, unit + 1)
                        dve.scalar_tensor_tensor(out=xm, in0=ps_a[parity], scalar=bo[:, mt:mt + 1], in1=xm,
                                                 op0=ALU.add, op1=ALU.add).then_inc(a_taken, 1)

                with dve.Fori(0, B - 2) as b:
                    chunk(b, sh.x[:, b + 2], False)
                chunk(B - 2, sh.x[:, 0], False)
                chunk(B - 1, None, True)


def program(nc, dram, out, phases):
    with ExitStack() as ctx:
        class Sh:
            pass
        sh = Sh()
        sh.ctx = ctx

        def sb(n, shape, dt):
            return ctx.enter_context(nc.sbuf_tensor(n, shape, dt))

        sh.x = sb("x", [P, B, KT, S], F32)
        sh.mean_w = sb("mean_weights", [P, P], F32)
        sh.ident = sb("identity", [P, P], F32)
        sh.eps = sb("eps", [P, 1], F32)
        sh.ln_sum = sb("ln_sum", [P, S], F32)
        sh.ln_x = sb("ln_x", [P, KT, S], F32)
        sh.ln_sq = sb("ln_sq", [P, KT, S], F32)
        sh.ln_r = sb("ln_r", [P, S], F32)
        sh.x_hi = [sb(f"x_hi{p}", [P, KT, S], F32R) for p in range(2)]
        sh.x_lo = [sb(f"x_lo{p}", [P, KT, S], F32R) for p in range(2)]
        sh.pair_a = ctx.enter_context(nc.psum_tensor("pair_a", [P, 2, S], F32))
        sh.pair_b = [ctx.enter_context(nc.psum_tensor(f"pair_b{n}", [P, 2, S], F32)) for n in range(2)]
        sh.bank = ctx.enter_context(nc.psum_tensor("bank", [P, S], F32))
        sh.misc = ctx.enter_context(nc.psum_tensor("misc", [P, S], F32))
        loaded = ctx.enter_context(nc.semaphore("loaded"))
        made = ctx.enter_context(nc.semaphore("made"))
        sh.semaphores = []
        sh.norm = Norm(sh, lambda n: ctx.enter_context(nc.semaphore(n)))
        load_constants(nc, sh, dram, loaded, made)
        for n, (kind, layer) in enumerate(phases):
            if kind == "ffn":
                ffn_phase(nc, sh, f"f{n}", layer, dram, out, n == 0, n == len(phases) - 1)
            else:
                attention_phase(nc, sh, f"a{n}", layer, dram)
            sh.norm.done += B
            nc.clear_and_free_semaphores(sh.semaphores)
            sh.semaphores = []
            nc.all_engine_barrier()


PHASES = (("ffn", 0), ("attn", 0), ("ffn", 0), ("ffn", 1), ("attn", 1), ("ffn", 1))


def feature_major(w):
    return w.reshape(KT, P, -1).transpose(1, 0, 2)


def ffn_tiles(gate, up, down, layer):
    T = TILES[layer]
    f = gate.shape[0]
    out = np.zeros((T, P, WC), np.float32)
    for at, w in ((0, gate), (D, up)):
        padded = np.zeros((T * P, D), np.float32)
        padded[:f] = w
        out[:, :, at:at + D] = padded.reshape(T, P, KT, P).transpose(0, 3, 2, 1).reshape(T, P, D)
    padded = np.zeros((T * P, D), np.float32)
    padded[:f] = down.T
    out[:, :, 2 * D:] = padded.reshape(T, P, D)
    return out


def selectors(layer):
    T = TILES[layer]
    owner = np.minimum(np.arange(T * P) // MOE, E)
    rows = (np.arange(RC)[:, None] == owner[None, :]).astype(np.float32)
    out = np.zeros((LO_ROW + RC, T * P), np.float32)
    out[:RC] = rows
    out[LO_ROW:] = rows
    return out


def head_columns(w):
    out = np.zeros((w.shape[0], G, HG, 32), np.float32)
    out[..., ROW_D:ROW_D + HD] = w.reshape(-1, G, HG, HD)
    return out.reshape(w.shape[0], G * P)


def head_rows(w):
    out = np.zeros((G, HG, 32, w.shape[1]), np.float32)
    out[:, :, :HD] = w.reshape(G, HG, HD, -1)
    return out.reshape(G, P, -1).transpose(1, 0, 2)


def attention_layout(inp):
    a = {}
    for n in range(2):
        w = {c: inp[f"L{n}_attn_W{c}"] if n == 0 else inp[f"L{n}_attn_W{c}"].T for c in "qkvo"}
        b = {c: inp[f"L{n}_attn_b{c}"] for c in "qkvo"}
        a[f"wqk{n}"] = np.stack([feature_major(head_columns(w[c])) for c in "qk"], 1)
        a[f"wv{n}"] = feature_major(w["v"])
        a[f"wo{n}"] = head_rows(w["o"])
        rows = np.stack([head_columns(b[c][None])[0].reshape(G, HG, 32) for c in "qk"])
        rows[1, :, :, ROW_M] = 1.0
        if n == 0:
            rows[0, :, :, ROW_A] = 1.0
        a[f"b_col{n}"] = rows.reshape(2 * G, P).T
        a[f"bv{n}"] = np.broadcast_to(b["v"], (P, D))
        a[f"bo{n}"] = b["o"].reshape(KT, P).T
    slope = 2.0 ** (-8.0 / H * np.arange(1, H + 1))
    rows = np.zeros((G, HG, 32), np.float32)
    rows[:, :, ROW_A] = np.sqrt(HD) * slope.astype(np.float32).reshape(G, HG)
    a["slope"] = rows.reshape(G, P).T
    a["ramp"] = np.broadcast_to(np.arange(1 - S, 1), (P, S))
    ahead = np.arange(P)[None, :] > np.arange(P)[:, None]
    a["masks"] = np.stack([np.eye(P), NEG * ahead, NEG * ahead.T], 1)
    sel = np.zeros((HG, 32, HG, 32), np.float32)
    for j in range(HG):
        sel[j, HD, j] = 1.0
    a["den_sel"] = sel.reshape(P, P)
    a["l_in"] = np.concatenate([inp[f"L1_attn_B{c}"] for c in "qkv"] +
                               [head_rows(inp["L1_attn_Bo"].T).transpose(2, 1, 0).reshape(RANK, G * P)], 1)
    a["l_out"] = np.concatenate([head_columns(inp[f"L1_attn_A{c}"].T) for c in "qk"] + [inp["L1_attn_Av"].T], 1)
    a["l_out_o"] = inp["L1_attn_Ao"].T
    return a


def layout(inp):
    a = {}
    a["x"] = inp["L0_attn_x"].reshape(B, S, KT, P).transpose(3, 0, 2, 1)
    a["mean_w"] = np.full((P, P), 1.0 / D, np.float32)
    a["ident"] = np.eye(P, dtype=np.float32)
    a["tri"] = np.broadcast_to((np.arange(E)[None, :] < np.arange(E)[:, None]).astype(np.float32).reshape(1, -1),
                               (P, E * E))
    gate = [np.concatenate([inp["L0_ffn_exp_wg"].reshape(E * MOE, D), inp["L0_ffn_shared_wg"]])]
    up = [np.concatenate([inp["L0_ffn_exp_wu"].reshape(E * MOE, D), inp["L0_ffn_shared_wu"]])]
    down = [np.concatenate([inp["L0_ffn_exp_wd"].transpose(1, 0, 2).reshape(D, E * MOE), inp["L0_ffn_shared_wd"]], 1)]
    gu = inp["L1_ffn_gate_up_proj"]
    gate.append(np.concatenate([gu[:, :MOE].reshape(E * MOE, D), inp["L1_ffn_sh_gate_w"]]))
    up.append(np.concatenate([gu[:, MOE:].reshape(E * MOE, D), inp["L1_ffn_sh_up_w"]]))
    down.append(np.concatenate([inp["L1_ffn_down_proj"].transpose(1, 0, 2).reshape(D, E * MOE),
                                inp["L1_ffn_sh_down_w"]], 1))
    routers = [inp["L0_ffn_gate_w"], np.concatenate([inp["L1_ffn_router_weight"], inp["L1_ffn_shared_gate_w"]])]
    for n in range(2):
        a[f"ffn{n}"] = ffn_tiles(gate[n], up[n], down[n], n)
        r = np.zeros((D, RC), np.float32)
        r[:, :routers[n].shape[0]] = routers[n].T
        a[f"router{n}"] = feature_major(r)
        a[f"sel{n}"] = selectors(n)
    a.update(attention_layout(inp))
    return {k: np.ascontiguousarray(v, dtype=np.float32) for k, v in a.items()}


def build(nc, shapes, phases):
    aps = {k: nc.dram_tensor(f"in_{k}", s, F32, kind="ExternalInput").ap() for k, s in shapes.items()}
    out = nc.dram_tensor("out_x", (P, B, KT, S), F32, kind="ExternalOutput").ap()
    dram = dict(aps)
    for group in ("ffn", "router", "sel", "wqk", "wv", "wo", "b_col", "bv", "bo"):
        if f"{group}0" in aps or f"{group}1" in aps:
            dram[group] = [aps.get(f"{group}{n}") for n in range(2)]
    program(nc, dram, out, phases)


def kernel(**inputs):
    import concourse.bacc as bacc
    from concourse.bass_utils import run_bass_kernel_spmd

    nc = bacc.Bacc("TRN2", target_bir_lowering=False, num_devices=1)
    arrays = layout({k: np.asarray(v) for k, v in inputs.items()})
    build(nc, {k: v.shape for k, v in arrays.items()}, PHASES)
    r = run_bass_kernel_spmd(nc, [{f"in_{k}": v for k, v in arrays.items()}], core_ids=[0])
    y = np.asarray(r.results[0]["out_x"])
    return np.ascontiguousarray(y.transpose(1, 3, 2, 0).reshape(B, S, D))
```
